# Optimizing a Trainium2 kernel written in Bass

```python
import numpy as np
import jax
import jax.numpy as jnp

def _softmax(x, axis=-1):
    return jax.nn.softmax(x, axis=axis)

def _gelu(x):
    return jax.nn.gelu(x, approximate=True)

def _silu(x):
    return jax.nn.silu(x)

def _sigmoid(x):
    return jax.nn.sigmoid(x)

def _layernorm(x, axis=-1, eps=1e-05):
    m = jnp.mean(x, axis=axis, keepdims=True)
    v = jnp.var(x, axis=axis, keepdims=True)
    return (x - m) / jnp.sqrt(v + eps)

def _scatter_add(tgt, idx, src, axis=0):
    return tgt.at[idx].add(src)

def _segment_sum(src, seg, n):
    return jax.ops.segment_sum(src, seg, n)
kernel_name = 'mk_adaln_d2_jaxref_r8_25f4c0'

def setup_inputs(seed: int=0):
    np.random.seed(seed)
    _w = jnp.asarray

    def _L0_attn_setup():
        import jax, jax.numpy as jnp
        import numpy as np
        EMBED_DIM = 256
        NUM_HEADS = 16
        HEAD_DIM = EMBED_DIM // NUM_HEADS

        def _apply_rope(q, k, seq_len):
            hd = q.shape[-1]
            theta = 10000.0 ** (-jnp.arange(0, hd, 2, dtype=jnp.float32) / hd)
            pos = jnp.arange(seq_len, dtype=jnp.float32)
            freqs = pos[:, None] * theta[None, :]
            sin = jnp.sin(freqs)[None, None]
            cos = jnp.cos(freqs)[None, None]
            q_rot = q[..., ::2] * cos - q[..., 1::2] * sin
            k_rot = k[..., ::2] * cos - k[..., 1::2] * sin
            q = jnp.concatenate([q_rot, q[..., 1::2]], axis=-1)
            k = jnp.concatenate([k_rot, k[..., 1::2]], axis=-1)
            return (q, k)
        key = jax.random.key(seed)
        ks = jax.random.split(key, 9)
        D = EMBED_DIM
        s = 1.0 / np.sqrt(D)
        inp = {'x': jax.random.normal(ks[0], (2, 256, D), dtype=jnp.float32), 'wq': jax.random.uniform(ks[1], (D, D), jnp.float32, -s, s), 'bq': jax.random.uniform(ks[2], (D,), jnp.float32, -s, s), 'wk': jax.random.uniform(ks[3], (D, D), jnp.float32, -s, s), 'bk': jax.random.uniform(ks[4], (D,), jnp.float32, -s, s), 'wv': jax.random.uniform(ks[5], (D, D), jnp.float32, -s, s), 'bv': jax.random.uniform(ks[6], (D,), jnp.float32, -s, s), 'wo': jax.random.uniform(ks[7], (D, D), jnp.float32, -s, s), 'bo': jax.random.uniform(ks[8], (D,), jnp.float32, -s, s)}
        return inp
    _L0_attn_in = _L0_attn_setup()

    def _L0_ffn_setup():
        import jax, jax.numpy as jnp
        import numpy as np
        B, S, D = (4, 64, 256)
        E, K, H = (8, 2, 176)
        HS = 2 * 176
        ALPHA = 0.001
        W_SCALE = 0.02

        def _moe_forward(hidden_states, gate_w, w_gate, w_up, w_down, sw_gate, sw_up, sw_down):
            b, s, d = hidden_states.shape
            x = hidden_states.reshape(-1, d)
            T = x.shape[0]
            logits = x @ gate_w
            scores = jax.nn.softmax(logits, axis=-1)
            topk_w, topk_idx = jax.lax.top_k(scores, K)
            mask = jax.nn.one_hot(topk_idx, E, dtype=scores.dtype).sum(axis=1)
            ce = mask.mean(axis=0)
            Pi = scores.mean(axis=0)
            aux_loss = (Pi * ce * E).sum() * ALPHA
            comb = jnp.zeros((T, E), dtype=x.dtype)
            comb = comb.at[jnp.arange(T)[:, None], topk_idx].add(topk_w)
            g = jax.nn.silu(jnp.einsum('td,edh->teh', x, w_gate)) * jnp.einsum('td,edh->teh', x, w_up)
            routed = jnp.einsum('teh,ehd,te->td', g, w_down, comb)
            shared = jax.nn.silu(x @ sw_gate) * (x @ sw_up) @ sw_down
            out = (routed + shared).reshape(b, s, d)
            return (out, aux_loss)
        key = jax.random.key(seed)
        ks = jax.random.split(key, 8)
        rn = lambda k, sh: jax.random.normal(k, sh, dtype=jnp.float32)
        return {'hidden_states': rn(ks[0], (B, S, D)), 'gate_w': rn(ks[1], (D, E)) * W_SCALE, 'w_gate': rn(ks[2], (E, D, H)) * W_SCALE, 'w_up': rn(ks[3], (E, D, H)) * W_SCALE, 'w_down': rn(ks[4], (E, H, D)) * W_SCALE, 'sw_gate': rn(ks[5], (D, HS)) * W_SCALE, 'sw_up': rn(ks[6], (D, HS)) * W_SCALE, 'sw_down': rn(ks[7], (HS, D)) * W_SCALE}
    _L0_ffn_in = _L0_ffn_setup()
    _L0_c = _w((lambda *s: np.random.randn(*s).astype(np.float32) * 0.05)(4, 256))
    _L0_wmod = _w((lambda *s: np.random.randn(*s).astype(np.float32) * 0.05)(256, 6 * 256) * 256 ** (-0.5))

    def _L1_attn_setup():
        import jax, jax.numpy as jnp
        import numpy as np
        B, SQ, HIDDEN = (2, 256, 256)
        HEADS, GROUPS, KVC = (16, 4, 128)
        HPG = HEADS // GROUPS
        LAYER_INDEX = 1
        SCALE = KVC ** (-0.5)
        key = jax.random.key(seed)
        k1, k2, k3, k4 = jax.random.split(key, 4)
        return {'x': jax.random.normal(k1, (B, SQ, HIDDEN), jnp.float32), 'w_q': jax.random.normal(k2, (HIDDEN, HEADS * KVC), jnp.float32) * 0.02, 'w_kv': jax.random.normal(k3, (HIDDEN, 2 * GROUPS * KVC), jnp.float32) * 0.02, 'w_dense': jax.random.normal(k4, (HEADS * KVC, HIDDEN), jnp.float32) * 0.02}
    _L1_attn_in = _L1_attn_setup()

    def _L1_ffn_setup():
        import jax, jax.numpy as jnp
        import numpy as np
        DIM = 256
        N_EXPERTS = 32
        TOPK = 4
        INTER = 128
        ROUTE_SCALE = 1.0
        key = jax.random.key(seed)
        ks = jax.random.split(key, 8)
        s = 0.02
        return {'x': jax.random.normal(ks[0], (2, 256, DIM), dtype=jnp.float32), 'gate_w': jax.random.normal(ks[1], (N_EXPERTS, DIM), dtype=jnp.float32) * s, 'w1': jax.random.normal(ks[2], (N_EXPERTS, INTER, DIM), dtype=jnp.float32) * s, 'w2': jax.random.normal(ks[3], (N_EXPERTS, DIM, INTER), dtype=jnp.float32) * s, 'w3': jax.random.normal(ks[4], (N_EXPERTS, INTER, DIM), dtype=jnp.float32) * s, 'sw1': jax.random.normal(ks[5], (2 * INTER, DIM), dtype=jnp.float32) * s, 'sw2': jax.random.normal(ks[6], (DIM, 2 * INTER), dtype=jnp.float32) * s, 'sw3': jax.random.normal(ks[7], (2 * INTER, DIM), dtype=jnp.float32) * s}
    _L1_ffn_in = _L1_ffn_setup()
    _L1_c = _w((lambda *s: np.random.randn(*s).astype(np.float32) * 0.05)(4, 256))
    _L1_wmod = _w((lambda *s: np.random.randn(*s).astype(np.float32) * 0.05)(256, 6 * 256) * 256 ** (-0.5))
    _d = {'L0_attn_x': _L0_attn_in['x'], 'L0_attn_wq': _L0_attn_in['wq'], 'L0_attn_bq': _L0_attn_in['bq'], 'L0_attn_wk': _L0_attn_in['wk'], 'L0_attn_bk': _L0_attn_in['bk'], 'L0_attn_wv': _L0_attn_in['wv'], 'L0_attn_bv': _L0_attn_in['bv'], 'L0_attn_wo': _L0_attn_in['wo'], 'L0_attn_bo': _L0_attn_in['bo'], 'L0_ffn_gate_w': _L0_ffn_in['gate_w'], 'L0_ffn_w_gate': _L0_ffn_in['w_gate'], 'L0_ffn_w_up': _L0_ffn_in['w_up'], 'L0_ffn_w_down': _L0_ffn_in['w_down'], 'L0_ffn_sw_gate': _L0_ffn_in['sw_gate'], 'L0_ffn_sw_up': _L0_ffn_in['sw_up'], 'L0_ffn_sw_down': _L0_ffn_in['sw_down'], 'L0_c': _L0_c, 'L0_wmod': _L0_wmod, 'L1_attn_w_q': _L1_attn_in['w_q'], 'L1_attn_w_kv': _L1_attn_in['w_kv'], 'L1_attn_w_dense': _L1_attn_in['w_dense'], 'L1_ffn_gate_w': _L1_ffn_in['gate_w'], 'L1_ffn_w1': _L1_ffn_in['w1'], 'L1_ffn_w2': _L1_ffn_in['w2'], 'L1_ffn_w3': _L1_ffn_in['w3'], 'L1_ffn_sw1': _L1_ffn_in['sw1'], 'L1_ffn_sw2': _L1_ffn_in['sw2'], 'L1_ffn_sw3': _L1_ffn_in['sw3'], 'L1_c': _L1_c, 'L1_wmod': _L1_wmod}
    _x0 = _d['L0_attn_x']
    _d['L0_attn_x'] = jax.random.normal(jax.random.fold_in(jax.random.key(seed), 1), (4, 512, 256), dtype=_x0.dtype)
    del _x0
    return _d

def reference(L0_attn_x, L0_attn_wq, L0_attn_bq, L0_attn_wk, L0_attn_bk, L0_attn_wv, L0_attn_bv, L0_attn_wo, L0_attn_bo, L0_ffn_gate_w, L0_ffn_w_gate, L0_ffn_w_up, L0_ffn_w_down, L0_ffn_sw_gate, L0_ffn_sw_up, L0_ffn_sw_down, L0_c, L0_wmod, L1_attn_w_q, L1_attn_w_kv, L1_attn_w_dense, L1_ffn_gate_w, L1_ffn_w1, L1_ffn_w2, L1_ffn_w3, L1_ffn_sw1, L1_ffn_sw2, L1_ffn_sw3, L1_c, L1_wmod):

    def _L0_attn_ref(x, wq, bq, wk, bk, wv, bv, wo, bo):
        import jax, jax.numpy as jnp
        import numpy as np
        EMBED_DIM = 256
        NUM_HEADS = 16
        HEAD_DIM = EMBED_DIM // NUM_HEADS

        def _apply_rope(q, k, seq_len):
            hd = q.shape[-1]
            theta = 10000.0 ** (-jnp.arange(0, hd, 2, dtype=jnp.float32) / hd)
            pos = jnp.arange(seq_len, dtype=jnp.float32)
            freqs = pos[:, None] * theta[None, :]
            sin = jnp.sin(freqs)[None, None]
            cos = jnp.cos(freqs)[None, None]
            q_rot = q[..., ::2] * cos - q[..., 1::2] * sin
            k_rot = k[..., ::2] * cos - k[..., 1::2] * sin
            q = jnp.concatenate([q_rot, q[..., 1::2]], axis=-1)
            k = jnp.concatenate([k_rot, k[..., 1::2]], axis=-1)
            return (q, k)
        B, S, D = x.shape
        H, hd = (NUM_HEADS, HEAD_DIM)

        def proj(w, b):
            return (x @ w.T + b).reshape(B, S, H, hd).transpose(0, 2, 1, 3)
        q = proj(wq, bq)
        k = proj(wk, bk)
        v = proj(wv, bv)
        q, k = _apply_rope(q, k, S)
        scores = jnp.einsum('bhqd,bhkd->bhqk', q, k) / jnp.sqrt(jnp.float32(hd))
        attn = jax.nn.softmax(scores, axis=-1)
        ctx = jnp.einsum('bhqk,bhkd->bhqd', attn, v)
        ctx = ctx.transpose(0, 2, 1, 3).reshape(B, S, D)
        return ctx @ wo.T + bo

    def _L0_ffn_ref(hidden_states, gate_w, w_gate, w_up, w_down, sw_gate, sw_up, sw_down):
        import jax, jax.numpy as jnp
        import numpy as np
        B, S, D = (4, 64, 256)
        E, K, H = (8, 2, 176)
        HS = 2 * 176
        ALPHA = 0.001
        W_SCALE = 0.02

        def _moe_forward(hidden_states, gate_w, w_gate, w_up, w_down, sw_gate, sw_up, sw_down):
            b, s, d = hidden_states.shape
            x = hidden_states.reshape(-1, d)
            T = x.shape[0]
            logits = x @ gate_w
            scores = jax.nn.softmax(logits, axis=-1)
            topk_w, topk_idx = jax.lax.top_k(scores, K)
            mask = jax.nn.one_hot(topk_idx, E, dtype=scores.dtype).sum(axis=1)
            ce = mask.mean(axis=0)
            Pi = scores.mean(axis=0)
            aux_loss = (Pi * ce * E).sum() * ALPHA
            comb = jnp.zeros((T, E), dtype=x.dtype)
            comb = comb.at[jnp.arange(T)[:, None], topk_idx].add(topk_w)
            g = jax.nn.silu(jnp.einsum('td,edh->teh', x, w_gate)) * jnp.einsum('td,edh->teh', x, w_up)
            routed = jnp.einsum('teh,ehd,te->td', g, w_down, comb)
            shared = jax.nn.silu(x @ sw_gate) * (x @ sw_up) @ sw_down
            out = (routed + shared).reshape(b, s, d)
            return (out, aux_loss)
        out, _aux = _moe_forward(hidden_states, gate_w, w_gate, w_up, w_down, sw_gate, sw_up, sw_down)
        return out

    def _L1_attn_ref(x, w_q, w_kv, w_dense):
        import jax, jax.numpy as jnp
        import numpy as np
        B, SQ, HIDDEN = (2, 256, 256)
        HEADS, GROUPS, KVC = (16, 4, 128)
        HPG = HEADS // GROUPS
        LAYER_INDEX = 1
        SCALE = KVC ** (-0.5)
        b, sq, _ = x.shape
        sk = sq
        q = jnp.einsum('bsh,he->bse', x, w_q).reshape(b, sq, GROUPS, HPG, KVC)
        kv = jnp.einsum('bsh,he->bse', x, w_kv)
        k, v = jnp.split(kv, 2, axis=-1)
        k = k.reshape(b, sk, GROUPS, KVC)
        v = v.reshape(b, sk, GROUPS, KVC)
        scores = jnp.einsum('bqgpd,bkgd->bgqpk', q, k) * (SCALE / LAYER_INDEX)
        scores = scores.astype(jnp.float32) * LAYER_INDEX
        causal = jnp.arange(sq)[:, None] >= jnp.arange(sk)[None, :]
        scores = jnp.where(causal[None, None, :, None, :], scores, -jnp.inf)
        probs = jax.nn.softmax(scores, axis=-1).astype(x.dtype)
        ctx = jnp.einsum('bgqpk,bkgd->bqgpd', probs, v).reshape(b, sq, HEADS * KVC)
        return jnp.einsum('bse,eh->bsh', ctx, w_dense)

    def _L1_ffn_ref(x, gate_w, w1, w2, w3, sw1, sw2, sw3):
        import jax, jax.numpy as jnp
        import numpy as np
        DIM = 256
        N_EXPERTS = 32
        TOPK = 4
        INTER = 128
        ROUTE_SCALE = 1.0
        shape = x.shape
        xf = x.reshape(-1, DIM)
        T = xf.shape[0]
        scores = jax.nn.softmax(xf @ gate_w.T, axis=-1)
        weights, indices = jax.lax.top_k(scores, TOPK)
        weights = weights * ROUTE_SCALE
        w_full = jnp.zeros((T, N_EXPERTS), dtype=xf.dtype)
        w_full = w_full.at[jnp.arange(T)[:, None], indices].add(weights)

        def body(y, inp):
            w1e, w2e, w3e, we = inp
            h = jax.nn.silu(xf @ w1e.T) * (xf @ w3e.T)
            return (y + h @ w2e.T * we[:, None], None)
        y0 = jnp.zeros_like(xf)
        y, _ = jax.lax.scan(body, y0, (w1, w2, w3, w_full.T))
        z = jax.nn.silu(xf @ sw1.T) * (xf @ sw3.T) @ sw2.T
        return (y + z).reshape(shape)
    x = L0_attn_x
    mod = (_silu(L0_c) @ L0_wmod).reshape(L0_c.shape[0], 6, 1, -1)
    sa, ca, ga, sb, cb, gb = (mod[:, 0], mod[:, 1], mod[:, 2], mod[:, 3], mod[:, 4], mod[:, 5])
    ga = (2 * (ga >= 0) - 1) * jnp.maximum(jnp.abs(ga), 0.25)
    gb = (2 * (gb >= 0) - 1) * jnp.maximum(jnp.abs(gb), 0.25)
    h = _layernorm(x, axis=-1) * (1 + ca) + sa
    x = x + ga * _L0_attn_ref(h, L0_attn_wq, L0_attn_bq, L0_attn_wk, L0_attn_bk, L0_attn_wv, L0_attn_bv, L0_attn_wo, L0_attn_bo)
    h = _layernorm(x, axis=-1) * (1 + cb) + sb
    x = x + gb * _L0_ffn_ref(h, L0_ffn_gate_w, L0_ffn_w_gate, L0_ffn_w_up, L0_ffn_w_down, L0_ffn_sw_gate, L0_ffn_sw_up, L0_ffn_sw_down)
    mod = (_silu(L1_c) @ L1_wmod).reshape(L1_c.shape[0], 6, 1, -1)
    sa, ca, ga, sb, cb, gb = (mod[:, 0], mod[:, 1], mod[:, 2], mod[:, 3], mod[:, 4], mod[:, 5])
    ga = (2 * (ga >= 0) - 1) * jnp.maximum(jnp.abs(ga), 0.25)
    gb = (2 * (gb >= 0) - 1) * jnp.maximum(jnp.abs(gb), 0.25)
    h = _layernorm(x, axis=-1) * (1 + ca) + sa
    x = x + ga * _L1_attn_ref(h, L1_attn_w_q, L1_attn_w_kv, L1_attn_w_dense)
    h = _layernorm(x, axis=-1) * (1 + cb) + sb
    x = x + gb * _L1_ffn_ref(h, L1_ffn_gate_w, L1_ffn_w1, L1_ffn_w2, L1_ffn_w3, L1_ffn_sw1, L1_ffn_sw2, L1_ffn_sw3)
    return x

_drawn_inputs = setup_inputs


def setup_inputs(seed=0):
    import zlib

    import numpy as np

    out = dict(_drawn_inputs(seed))
    spreads = {}
    factors = {'L0_attn_wq': 8.0,
     'L0_attn_bq': 8.0,
     'L0_attn_wk': 8.0,
     'L0_attn_bk': 8.0,
     'L0_attn_wv': 8.0,
     'L0_attn_bv': 8.0,
     'L0_attn_wo': 8.0,
     'L0_attn_bo': 6.416,
     'L0_ffn_gate_w': 8.0,
     'L0_ffn_w_gate': 8.0,
     'L0_ffn_w_up': 8.0,
     'L0_ffn_w_down': 8.0,
     'L0_ffn_sw_gate': 8.0,
     'L0_ffn_sw_up': 8.0,
     'L0_ffn_sw_down': 8.0,
     'L0_c': 4.623,
     'L0_wmod': 4.621,
     'L1_attn_w_q': 8.0,
     'L1_attn_w_kv': 6.686,
     'L1_attn_w_dense': 6.715,
     'L1_ffn_gate_w': 8.0,
     'L1_ffn_w1': 8.0,
     'L1_ffn_w2': 8.0,
     'L1_ffn_w3': 8.0,
     'L1_ffn_sw1': 8.0,
     'L1_ffn_sw2': 8.0,
     'L1_ffn_sw3': 8.0,
     'L1_c': 6.195,
     'L1_wmod': 5.843}
    for name, (base, spread) in spreads.items():
        noise = np.random.default_rng([zlib.crc32(name.encode()), seed]).standard_normal(out[name].shape)
        drawn = base * np.exp(spread * noise) if base else spread * noise
        out[name] = jnp.asarray(drawn.astype(out[name].dtype))
    for name, factor in factors.items():
        out[name] = (out[name] * factor).astype(out[name].dtype)
    return out
```

```python
from contextlib import ExitStack

import numpy as np

import concourse.bass as bass
from concourse import mybir

ALU = mybir.AluOpType
ACT = mybir.ActivationFunctionType
AX = mybir.AxisListType
F32 = mybir.dt.float32
F32R = mybir.dt.float32r

P = 128
B, S, D = 4, 512, 256
KT = D // P
TT = S // P
NT = B * TT
LN_EPS = 1e-5
BIG = 3.0e38

H0, HD0 = 16, 16
GROUP0 = 4
STACK = 64
H1, G1, HD1 = 16, 4, 128
HPG1 = H1 // G1
SCALE1 = HD1 ** -0.5
E0, K0, HID0, SH0 = 8, 2, 176, 352
E1, K1, HID1, SH1 = 32, 4, 128, 256
TILES0_R = E0 * HID0 // P
TILES0 = -(-(E0 * HID0 + SH0) // P)
TILES1_R = E1
TILES1 = E1 + SH1 // P
LO_ROW = 32


class Signals:

    def __init__(self, nc, stack):
        self.nc, self.stack = nc, stack
        self.sems, self.count, self.passed = {}, {}, {}

    def done(self, instruction, name, by=1):
        if name not in self.sems:
            self.sems[name] = self.stack.enter_context(self.nc.semaphore(name))
            self.count[name] = 0
        instruction.then_inc(self.sems[name], by)
        self.count[name] += by
        return name, self.count[name]

    def wait(self, engine, *values):
        for value in values:
            if value is None:
                continue
            name, count = value
            key = (str(engine.engine), name)
            if self.passed.get(key, 0) < count:
                engine.wait_ge(self.sems[name], count)
                self.passed[key] = count

    def everything(self, engine):
        self.wait(engine, *self.count.items())


class Ring:

    def __init__(self, signals, n, first=0):
        self.signals, self.n, self.first, self.turn = signals, n, first, 0
        self.freed = [()] * n

    def take(self, engine):
        i = self.turn % self.n
        self.turn += 1
        self.signals.wait(engine, *self.freed[i])
        return i + self.first

    def give(self, i, *values):
        self.freed[i - self.first] = values


class Program:
    def __init__(self, nc, ins, out, stack):
        self.nc, self.ins, self.out = nc, ins, out
        self.pe, self.dve, self.act, self.pool, self.sp = nc.tensor, nc.vector, nc.scalar, nc.gpsimd, nc.sync
        self.sig = Signals(nc, stack)
        self.stack = stack
        self.psum = stack.enter_context(nc.psum_tensor("psum", [P, 8, 512], F32))
        self.n_loads = 0

    def sb(self, stack, name, shape, dtype=F32):
        return stack.enter_context(self.nc.sbuf_tensor(name, shape, dtype))

    def load(self, dst, src, *waits, name=None, queue=None):
        queue = queue or self.sp
        self.sig.wait(queue, *waits)
        self.n_loads += 1
        return self.sig.done(queue.dma_start(dst, src), name or f"load{self.n_loads}", 16)

    def mm3(self, out, lhs, rhs, start, stop):
        (lh, ll), (rh, rl) = lhs, rhs
        self.pe.matmul(out, lh, rh, start=start, stop=False, skip_group_check=True)
        self.pe.matmul(out, lh, rl, start=False, stop=False, skip_group_check=True)
        return self.pe.matmul(out, ll, rh, start=False, stop=stop, skip_group_check=True)

    def split(self, hi, lo, src, ready, name, free=()):
        sig = self.sig
        sig.wait(self.act, *ready, *free)
        t_hi = sig.done(self.act.activation(hi, src, ACT.Copy), f"act_{name}_hi")
        sig.wait(self.pool, *ready, *free, t_hi)
        t_lo = sig.done(self.pool.tensor_tensor(lo, src, hi, ALU.subtract), f"pool_{name}_lo")
        return t_hi, t_lo

    def phase_barrier(self):
        for engine in (self.pe, self.dve, self.act, self.pool, self.sp):
            self.sig.everything(engine)

    def setup(self, stack):
        sig, ins = self.sig, self.ins
        self.x = self.sb(stack, "x_nat", [P, NT, D])
        self.ident = self.sb(stack, "ident", [P, P])
        self.mod = [self.sb(stack, f"mod{l}", [P, 12, B]) for l in range(2)]
        self.gate = [self.sb(stack, f"gate{l}", [P, 2, KT, B]) for l in range(2)]
        self.stats = self.sb(stack, "ln_stats", [P, TT, 6])
        self.mv = self.sb(stack, "ln_mean_var", [P, TT, 2])
        self.lnw = self.sb(stack, "ln_work", [P, 5, TT])
        self.eps = self.sb(stack, "eps", [P, 1])
        self.t_ident = self.load(self.ident[:, :], ins["ident"])
        x_dram = ins["x"].rearrange("b (t p) d -> p (b t) d", p=P)
        self.x_ready = []
        for b in range(B):
            t = self.load(self.x[:, b * TT:(b + 1) * TT, :], x_dram[:, b * TT:(b + 1) * TT, :])
            self.x_ready += [t] * TT
        self.t_eps = sig.done(self.pool.memset(self.eps[:, :], LN_EPS), "pool_eps")
        self.ln_done = None

    def modulation(self, l):
        sig, ins = self.sig, self.ins
        with ExitStack() as st:
            c = self.sb(st, f"c{l}", [P, KT, B])
            sc = self.sb(st, f"silu_c{l}", [P, KT, B])
            w = self.sb(st, f"wmod{l}", [P, KT, 6 * D])
            work = self.sb(st, f"gate_work{l}", [P, 3, 2, KT, B])
            t_c = self.load(c[:, :, :], ins[f"c{l}"])
            t_w = self.load(w[:, :, :], ins[f"wmod{l}"].rearrange("(k p) n -> p k n", p=P))
            sig.wait(self.act, t_c)
            t_sc = sig.done(self.act.activation(sc[:, :, :], c[:, :, :], ACT.Silu), "act_silu_c")
            sig.wait(self.pe, t_sc, t_w)
            ps = self.psum[:, l, 0:12 * B].rearrange("p (m b) -> p m b", b=B)
            for m in range(12):
                for k in range(KT):
                    mm = self.pe.matmul(ps[:, m, :], w[:, k, m * P:(m + 1) * P], sc[:, k, :],
                                        start=(k == 0), stop=(k == KT - 1))
            t_mm = sig.done(mm, "pe_mod")
            mod = self.mod[l]
            sig.wait(self.dve, t_mm)
            t = sig.done(self.dve.tensor_copy(mod[:, :, :], ps), "dve_mod")
            sig.wait(self.dve, t)
            for j in (1, 4):
                v = mod[:, 2 * j:2 * j + 2, :]
                t = sig.done(self.dve.tensor_scalar(v, v, 1.0, None, ALU.add), "dve_mod")
            for n, j in enumerate((2, 5)):
                g = mod[:, 2 * j:2 * j + 2, :]
                neg, sign, mag = (work[:, i, n] for i in range(3))
                t1 = sig.done(self.dve.tensor_scalar(neg, g, -1.0, None, ALU.mult), "dve_mod")
                t2 = sig.done(self.dve.tensor_scalar(sign, g, 0.0, 2.0, ALU.is_ge, ALU.mult), "dve_mod")
                sig.wait(self.dve, t1)
                t3 = sig.done(self.dve.tensor_tensor(mag, g, neg, ALU.max), "dve_mod")
                sig.wait(self.dve, t3)
                t4 = sig.done(self.dve.tensor_scalar(neg, mag, 0.25, None, ALU.max), "dve_mod")
                sig.wait(self.dve, t4)
                t = sig.done(self.dve.scalar_tensor_tensor(self.gate[l][:, n], sign, -1.0, neg, ALU.add, ALU.mult),
                             "dve_mod")
            self.t_mod = t

    def norm_buffers(self, stack, tag, n_h):
        self.xn = self.sb(stack, f"xn_{tag}", [P, 2, D])
        self.xn_ring = Ring(self.sig, 2)
        self.h32 = self.sb(stack, f"h32_{tag}", [P, KT, S])
        self.h32_free = ()
        self.hh = self.sb(stack, f"h_hi_{tag}", [P, n_h, KT, S], F32R)
        self.hl = self.sb(stack, f"h_lo_{tag}", [P, n_h, KT, S], F32R)
        self.h_ring = Ring(self.sig, n_h)

    def norm(self, b, l, which, banks):
        sig, dve, act, pe = self.sig, self.dve, self.act, self.pe
        stats, mv, w = self.stats, self.mv, self.lnw
        sig.wait(dve, self.ln_done, self.t_mod)
        for t in range(TT):
            tile = b * TT + t
            sig.wait(dve, self.x_ready[tile])
            d = sig.done(dve.bn_stats(stats[:, t, :], self.x[:, tile, :]), "dve_stats")
        sig.wait(dve, d)
        for t in range(TT):
            d = sig.done(dve.bn_aggr(mv[:, t, :], stats[:, t, :]), "dve_stats")
        var, mean = mv[:, :, 1], mv[:, :, 0]
        sd, r, a, c, rstd = (w[:, i, :] for i in range(5))
        sig.wait(act, d, self.t_eps)
        d = sig.done(act.activation(sd, var, ACT.Sqrt, bias=self.eps[:, 0:1]), "act_sd")
        sig.wait(dve, d)
        d = sig.done(dve.reciprocal(r, sd), "dve_rstd")
        sig.wait(dve, d)
        d = sig.done(dve.scalar_tensor_tensor(a, var, LN_EPS, r, ALU.add, ALU.mult), "dve_rstd")
        sig.wait(dve, d)
        d = sig.done(dve.tensor_tensor(c, a, r, ALU.mult), "dve_rstd")
        sig.wait(dve, d)
        d = sig.done(dve.tensor_scalar(a, c, -0.5, 1.5, ALU.mult, ALU.add), "dve_rstd")
        sig.wait(dve, d)
        d = sig.done(dve.tensor_tensor(rstd, a, r, ALU.mult), "dve_rstd")
        sig.wait(dve, d)
        bank = [banks.take(pe) for _ in range(KT)]
        sig.wait(pe, self.t_ident)
        for t in range(TT):
            n = self.xn_ring.take(dve)
            d = sig.done(dve.tensor_scalar(self.xn[:, n, :], self.x[:, b * TT + t, :], mean[:, t:t + 1],
                                           rstd[:, t:t + 1], ALU.subtract, ALU.mult), "dve_xn")
            sig.wait(pe, d)
            for k in range(KT):
                mm = pe.transpose(self.psum[:, bank[k], t * P:(t + 1) * P], self.xn[:, n, k * P:(k + 1) * P],
                                  self.ident[:, :])
            t_xT = sig.done(mm, "pe_xT")
            self.xn_ring.give(n, t_xT)
        self.ln_done = d
        slot = self.h_ring.take(dve)
        sig.wait(dve, t_xT, *self.h32_free)
        j = 3 * which
        mod = self.mod[l]
        ready = []
        for k in range(KT):
            t_h = sig.done(dve.tensor_scalar(self.h32[:, k, :], self.psum[:, bank[k], :],
                                             mod[:, 2 * (j + 1) + k, b:b + 1], mod[:, 2 * j + k, b:b + 1],
                                             ALU.mult, ALU.add), "dve_h")
            banks.give(bank[k], t_h)
            ready += self.split(self.hh[:, slot, k, :], self.hl[:, slot, k, :], self.h32[:, k, :], [t_h], "h",
                                self.h_ring.freed[slot])
        self.h32_free = tuple(ready)
        return slot, ready, t_h

    def h(self, slot, k, cols=slice(0, S)):
        return self.hh[:, slot, k, cols], self.hl[:, slot, k, cols]

    def residual(self, b, yT, y_ready, banks, store=False):
        sig, pe, dve = self.sig, self.pe, self.dve
        for half in range(2):
            n = banks.take(pe)
            sig.wait(pe, *y_ready)
            for t in range(TT // 2):
                tile = half * (TT // 2) + t
                for k in range(KT):
                    mm = pe.transpose(self.psum[:, n, t * D + k * P:t * D + (k + 1) * P],
                                      yT[:, k, tile * P:(tile + 1) * P], self.ident[:, :])
            t_T = sig.done(mm, "pe_yT")
            lo = b * TT + half * (TT // 2)
            xs = self.x[:, lo:lo + TT // 2, :].rearrange("p t d -> p (t d)")
            sig.wait(dve, t_T, self.x_ready[lo])
            t_x = sig.done(dve.tensor_tensor(xs, xs, self.psum[:, n, :], ALU.add), "dve_x")
            banks.give(n, t_x)
            for t in range(TT // 2):
                self.x_ready[lo + t] = t_x
            if store:
                o = self.out.rearrange("b (t p) d -> p (b t) d", p=P)
                self.load(o[:, lo:lo + TT // 2, :], self.x[:, lo:lo + TT // 2, :], t_x)
        return t_T

    def split_weights(self, stage, ring, name, src, hi, lo, width):
        ready = []
        n = src.shape[1]
        for a in range(0, n, width):
            e = min(n, a + width)
            s = ring.take(self.sp)
            t = self.load(stage[:, s, 0:e - a], src[:, a:e], name=f"stage_{name}{s}")
            two = self.split(hi[:, a:e], lo[:, a:e], stage[:, s, 0:e - a], [t], "w")
            ring.give(s, *two)
            ready += two
        return ready

    def attention0(self):
        sig, ins, pe, dve, act, pool = self.sig, self.ins, self.pe, self.dve, self.act, self.pool
        psum = self.psum
        with ExitStack() as st:
            sb = lambda name, shape, dt=F32: self.sb(st, "a0_" + name, shape, dt)
            self.norm_buffers(st, "a0", 2)
            NW = 5 * D
            w_hi, w_lo = sb("w_hi", [P, KT * NW], F32R), sb("w_lo", [P, KT * NW], F32R)
            wo_hi, wo_lo = sb("wo_hi", [P, GROUP0 * D], F32R), sb("wo_lo", [P, GROUP0 * D], F32R)
            sel = sb("stack_sel", [P, 4, 4, P], F32R)
            rope = sb("rope", [P, 2, S])
            bias, bv, bo = sb("bias", [P, 8]), sb("bv", [P, D]), sb("bo", [P, KT])
            stage, stage_ring = sb("stage", [P, 2, 512]), Ring(sig, 2)
            rp = sb("rope_tmp", [P, 3, S])
            rp_free = ()
            qk = sb("qk", [P, 2, 2, 2, S], F32R)
            qk_ready, qk_free = {}, {}
            stk = sb("stk", [P, 2, 3, S], F32R)
            stk_ring = Ring(sig, 3)
            v = sb("v", [P, 2, TT, H0, 32])
            v_ready, v_free = {}, {}
            e, e_ring = sb("e", [P, 3, S]), Ring(sig, 3)
            NET = 5
            et, et_ring = sb("et", [P, NET, TT, S]), Ring(sig, NET)
            nmax, rsum = sb("nmax", [P, H0, TT]), sb("rsum", [P, H0, TT])
            rinv, rexp = sb("rinv", [P, GROUP0, TT]), sb("rexp", [P, TT, GROUP0, 32])
            rb, ctx32 = sb("rb", [P, S]), sb("ctx32", [P, S])
            ctx = sb("ctx", [P, 2, GROUP0, S], F32R)
            oT = sb("oT", [P, KT, S])
            oT_free = None

            s_banks, t_banks = Ring(sig, 3), Ring(sig, 2, 3)
            pv_banks, banks = Ring(sig, 1, 5), Ring(sig, 2, 6)

            h_of = {0: self.norm(0, 0, 0, banks)}
            t_w = self.split_weights(stage, stage_ring, "a0", ins["w0_qkv"], w_hi, w_lo, 512)
            self.load(rope[:, :, :], ins["rope"], name="a0_small")
            self.load(bias[:, :], ins["b0_qk"], name="a0_small")
            self.load(bo[:, :], ins["b0_o"], name="a0_small")
            t_small = self.load(bv[:, :], ins["b0_v"].partition_broadcast(P), name="a0_small")
            sel_f = sel[:, :, :, :].rearrange("p a b c -> p (a b c)")
            t_sel = []
            for a in range(0, 2048, 512):
                s = stage_ring.take(self.sp)
                t = self.load(stage[:, s, :], ins["stack_sel"][:, a:a + 512], name=f"stage_a0{s}")
                sig.wait(act, t)
                t = sig.done(act.activation(sel_f[:, a:a + 512], stage[:, s, :], ACT.Copy), "act_sel")
                stage_ring.give(s, t)
                t_sel.append(t)
            t_wo = self.split_weights(stage, stage_ring, "a0", ins["w0_o"], wo_hi, wo_lo, 512)
            t_vz = sig.done(pool.memset(v[:, :, :, :, :].rearrange("p a b c d -> p (a b c d)"), 0.0), "pool_vzero")

            def w(k, a, e_):
                return w_hi[:, k * NW + a:k * NW + e_], w_lo[:, k * NW + a:k * NW + e_]

            def project_qk(b, i, m):
                nonlocal rp_free
                slot, h_ready, _ = h_of[b]
                two = []
                for part in range(2):
                    n = banks.take(pe)
                    sig.wait(pe, *t_w, *h_ready)
                    col = (2 * i + part) * D + m * P
                    for k in range(KT):
                        mm = self.mm3(psum[:, n, :], w(k, col, col + P), self.h(slot, k), k == 0, k == KT - 1)
                    two.append((n, sig.done(mm, "pe_qk")))
                sig.wait(dve, t_small, *rp_free)
                t_part = []
                for part, (n, t) in enumerate(two):
                    sig.wait(dve, t)
                    c = 4 * i + 2 * part + m
                    t = sig.done(dve.scalar_tensor_tensor(rp[:, part, :], psum[:, n, :], bias[:, c:c + 1],
                                                          rope[:, part, :], ALU.add, ALU.mult), "dve_rope")
                    banks.give(n, t)
                    t_part.append(t)
                sig.wait(dve, *t_part)
                t = sig.done(dve.tensor_tensor(rp[:, 2, :], rp[:, 0, :], rp[:, 1, :], ALU.add), "dve_rope")
                two = self.split(qk[:, i, m, 0, :], qk[:, i, m, 1, :], rp[:, 2, :], [t], "qk",
                                 qk_free.get((i, m), ()))
                rp_free = two
                qk_ready[b, i, m] = two
                return mm

            def project_v(b):
                slot, h_ready, _ = h_of[b]
                for t_ in range(TT):
                    n = banks.take(pe)
                    sig.wait(pe, *t_w, *h_ready)
                    for k in range(KT):
                        mm = self.mm3(psum[:, n, 0:D], self.h(slot, k, slice(t_ * P, (t_ + 1) * P)),
                                      w(k, 4 * D, 5 * D), k == 0, k == KT - 1)
                    t = sig.done(mm, "pe_v")
                    sig.wait(dve, t, t_small, t_vz, v_free.get(b % 2))
                    t = sig.done(dve.tensor_tensor(v[:, b % 2, t_, :, 0:HD0],
                                                   psum[:, n, 0:D].rearrange("p (h c) -> p h c", c=HD0),
                                                   bv[:, :].rearrange("p (h c) -> p h c", c=HD0), ALU.add), "dve_v")
                    banks.give(n, t)
                v_ready[b] = t
                return mm

            stk_of = {}

            def stack_pair(b, pair):
                m, p = divmod(pair, 4)
                s = stk_ring.take(act)
                ready = []
                for i in range(2):
                    n = banks.take(pe)
                    sig.wait(pe, *t_sel, *qk_ready[b, i, m])
                    for x in range(2):
                        mm = pe.matmul(psum[:, n, :], sel[:, 2 * i + x, p, :], qk[:, i, m, x, :],
                                       start=(x == 0), stop=(x == 1))
                    t = sig.done(mm, "pe_stack")
                    qk_free[i, m] = (t,)
                    sig.wait(act, t)
                    t = sig.done(act.activation(stk[:, i, s, :], psum[:, n, :], ACT.Copy), "act_stack")
                    banks.give(n, t)
                    ready.append(t)
                stk_of[b, pair] = s, ready

            s_of, e_of, et_of = {}, {}, {}
            last_pe = {}

            def scores(u):
                b, h, qt = u // (H0 * TT), u // TT % H0, u % TT
                s, ready = stk_of[b, h // 2]
                r0 = STACK * (h % 2)
                n = s_banks.take(pe)
                sig.wait(pe, *ready)
                mm = pe.matmul(psum[:, n, :], stk[r0:r0 + STACK, 0, s, qt * P:(qt + 1) * P],
                               stk[r0:r0 + STACK, 1, s, :], start=True, stop=True)
                t = sig.done(mm, "pe_s")
                if h % 2 and qt == TT - 1:
                    stk_ring.give(s, t)
                s_of[u] = n
                sig.wait(dve, t, rsum_free.get((b - 1, h // GROUP0)))
                t = sig.done(dve.tensor_reduce(nmax[:, h, qt:qt + 1], psum[:, n, :], AX.X, ALU.max, negate=True),
                             "dve_max")
                x = e_ring.take(act)
                sig.wait(act, t, rsum_free.get((b - 1, h // GROUP0)))
                t = sig.done(act.activation(e[:, x, :], psum[:, n, :], ACT.Exp, bias=nmax[:, h, qt:qt + 1],
                                            accum_out=rsum[:, h, qt:qt + 1]), "act_e")
                s_banks.give(n, t)
                e_of[u] = x, t

            rsum_free = {}

            def turn(u):
                b, h, qt = u // (H0 * TT), u // TT % H0, u % TT
                x, t_e = e_of[u]
                n = t_banks.take(pe)
                sig.wait(pe, t_e, self.t_ident)
                for k in range(TT):
                    mm = pe.transpose(psum[:, n, k * P:(k + 1) * P], e[:, x, k * P:(k + 1) * P], self.ident[:, :])
                t = sig.done(mm, "pe_turn")
                e_ring.give(x, t)
                on_act = u % 5 in (1, 3)
                eng = act if on_act else dve
                if qt == 0:
                    i = et_ring.turn % NET
                    sig.wait(act, *et_ring.freed[i])
                    et_of[b, h] = [et_ring.take(dve), []]
                i, ready = et_of[b, h]
                sig.wait(eng, t)
                dst = et[:, i, :, qt * P:(qt + 1) * P]
                src = psum[:, n, :].rearrange("p (k q) -> p k q", k=TT)
                if on_act:
                    t = sig.done(act.activation(dst, src, ACT.Copy), "act_et")
                else:
                    t = sig.done(dve.tensor_copy(dst, src), "dve_et")
                t_banks.give(n, t)
                ready.append(t)

            def context(b, g):
                sig.wait(dve, *[et_of[b, GROUP0 * g + j][1][-1] for j in range(GROUP0)])
                sig.wait(dve, e_of[(b * H0 + GROUP0 * g + GROUP0 - 1) * TT + TT - 1][1])
                hs = slice(GROUP0 * g, GROUP0 * (g + 1))
                t_r = sig.done(dve.reciprocal(rinv[:, :, :], rsum[:, hs, :]), "dve_rinv")
                rsum_free[b, g] = t_r
                n = pv_banks.take(pe)
                sig.wait(pe, v_ready[b])
                for j in range(GROUP0):
                    sig.wait(pe, *et_of[b, GROUP0 * g + j][1])
                for k in range(TT):
                    for j in range(GROUP0):
                        mm = pe.matmul(psum[32 * j:32 * j + 32, n, :], v[:, b % 2, k, GROUP0 * g + j, :],
                                       et[:, et_of[b, GROUP0 * g + j][0], k, :], start=(k == 0), stop=(k == TT - 1),
                                       tile_position=(0, 32 * j), skip_group_check=True)
                t_pv = sig.done(mm, "pe_pv")
                v_free[b % 2] = t_pv
                for j in range(GROUP0):
                    et_ring.give(et_of[b, GROUP0 * g + j][0], t_pv)
                sig.wait(pool, t_r, ctx_done.get("rexp"))
                t_x = sig.done(pool.tensor_copy(rexp[:, :, :, :], rinv[:, :, :].rearrange("p j t -> p t j")
                                                .unsqueeze(3).broadcast_to([P, TT, GROUP0, 32])), "pool_rexp")
                m = banks.take(pe)
                sig.wait(pe, t_x)
                for q in range(TT):
                    mm = pe.matmul(psum[:, m, q * P:(q + 1) * P], rexp[:, q].rearrange("p j i -> p (j i)"),
                                   self.ident[:, :], start=True, stop=True)
                t = sig.done(mm, "pe_rb")
                ctx_done["rexp"] = t
                sig.wait(act, t, ctx_done.get("ctx32"))
                t = sig.done(act.activation(rb[:, :], psum[:, m, :], ACT.Copy), "act_rb")
                banks.give(m, t)
                sig.wait(dve, t, t_pv, *ctx_done.get("split", ()))
                t = sig.done(dve.tensor_tensor(ctx32[:, :], psum[:, n, :], rb[:, :], ALU.mult), "dve_ctx")
                ctx_done["ctx32"] = t
                pv_banks.give(n, t)
                two = self.split(ctx[:, 0, g, :], ctx[:, 1, g, :], ctx32[:, :], [t], "ctx",
                                 ctx_done.get("out", ()))
                ctx_done["split"] = two
                ctx_ready[g] = two

            ctx_done, ctx_ready = {}, {}

            def output(b):
                nonlocal oT_free
                ready = []
                for m in range(KT):
                    n = banks.take(pe)
                    sig.wait(pe, *t_wo)
                    for g in range(GROUP0):
                        sig.wait(pe, *ctx_ready[g])
                        c = slice(g * D + m * P, g * D + (m + 1) * P)
                        mm = self.mm3(psum[:, n, :], (wo_hi[:, c], wo_lo[:, c]), (ctx[:, 0, g, :], ctx[:, 1, g, :]),
                                      g == 0, g == GROUP0 - 1)
                    t_mm = t = sig.done(mm, "pe_o")
                    sig.wait(dve, t, t_small, oT_free)
                    t = sig.done(dve.tensor_scalar(oT[:, m, :], psum[:, n, :], bo[:, m:m + 1],
                                                   self.gate[0][:, 0, m, b:b + 1], ALU.add, ALU.mult), "dve_o")
                    banks.give(n, t)
                    ready.append(t)
                ctx_done["out"] = (t_mm,)
                oT_free = self.residual(b, oT, ready, banks)

            def free_h(b, *names):
                self.h_ring.give(h_of[b][0], *[(n, sig.count[n]) for n in names])

            U = H0 * TT
            events = {}
            for b in range(B):
                at = lambda k, f, *a: events.setdefault(k, []).append((f, a))
                base = U * b
                if b:
                    at(base - 56, lambda b=b: h_of.__setitem__(b, self.norm(b, 0, 0, banks)))
                    start = [base - 30, base - 26, base - 5, base - 3, base - 40]
                else:
                    start = [-9, -8, -6, -5, -7]
                at(start[0], project_qk, b, 0, 0)
                at(start[1], project_qk, b, 1, 0)
                at(start[4], project_v, b)
                at(start[2], project_qk, b, 0, 1)
                at(start[3], project_qk, b, 1, 1)
                at(start[3], free_h, b, "pe_qk", "pe_v")
                for pair in range(H0 // 2):
                    at(base + 8 * pair - (4 if b == 0 or pair else 2), stack_pair, b, pair)
                for g in range(GROUP0):
                    at(base + 16 * (g + 1) + 3, context, b, g)
                at(base + U + 9, output, b)
            for i in range(-10, B * U + 12):
                for f, a in events.get(i, []):
                    f(*a)
                if 0 <= i < B * U:
                    scores(i)
                if 0 <= i - 2 < B * U:
                    turn(i - 2)

    def attention1(self):
        sig, ins, pe, dve, act, pool = self.sig, self.ins, self.pe, self.dve, self.act, self.pool
        psum = self.psum
        with ExitStack() as st:
            sb = lambda name, shape, dt=F32: self.sb(st, "a1_" + name, shape, dt)
            self.norm_buffers(st, "a1", 2)
            NQ, NKV = H1 * HD1, 2 * G1 * HD1
            wkv = [sb(f"wkv_{x}", [P, KT * NKV], F32R) for x in ("hi", "lo")]
            wq = [sb(f"wq_{x}", [P, KT * NQ], F32R) for x in ("hi", "lo")]
            wd = [sb(f"wd_{x}", [P, H1 * D], F32R) for x in ("hi", "lo")]
            stage, stage_ring = sb("stage", [P, 2, 512]), Ring(sig, 2)
            mask = sb("mask", [P, S])
            kT = sb("kT", [P, G1, 2, S], F32R)
            v = sb("v", [P, 2, TT, G1 * HD1])
            q = sb("q", [P, 2, 2, S], F32R)
            q_ring = Ring(sig, 2)
            e, e_ring = sb("e", [P, 3, S]), Ring(sig, 3)
            et, et_ring = sb("et", [P, 2, TT, S]), Ring(sig, 2)
            nmax, rsum, rinv = sb("nmax", [P, 4, 1]), sb("rsum", [P, 4, 1]), sb("rinv", [P, 4, 1])
            ctx, ctx_ring = sb("ctx", [P, 2, 2, S], F32R), Ring(sig, 2)
            oT = sb("oT", [P, KT, S])
            oT_free = None

            s_banks, t_banks = Ring(sig, 2), Ring(sig, 2, 2)
            banks, o_banks = Ring(sig, 2, 4), Ring(sig, 2, 6)

            h_of = {0: self.norm(0, 1, 0, banks)}
            t_mask = self.load(mask[:, :], ins["mask"])
            t_kv = self.split_weights(stage, stage_ring, "a1", ins["w1_kv"], *wkv, 512)
            t_q = self.split_weights(stage, stage_ring, "a1", ins["w1_q"], *wq, 512)
            t_d = self.split_weights(stage, stage_ring, "a1", ins["w1_d"], *wd, 512)

            def pair(w_, a, e_):
                return w_[0][:, a:e_], w_[1][:, a:e_]

            kv_of, kv_free = {}, {"k": None, ("v", 0): None, ("v", 1): None}

            def project_kv(b):
                slot, h_ready, _ = h_of[b]
                k_ready = []
                for g in range(G1):
                    n = banks.take(pe)
                    sig.wait(pe, *t_kv, *h_ready)
                    for k in range(KT):
                        mm = self.mm3(psum[:, n, :], pair(wkv, k * NKV + g * P, k * NKV + (g + 1) * P),
                                      self.h(slot, k), k == 0, k == KT - 1)
                    t = sig.done(mm, "pe_kv")
                    sig.wait(act, t, kv_free["k"])
                    t_hi = sig.done(act.activation(kT[:, g, 0, :], psum[:, n, :], ACT.Copy), "act_k_hi")
                    sig.wait(dve, t_hi, kv_free["k"])
                    t_lo = sig.done(dve.tensor_tensor(kT[:, g, 1, :], psum[:, n, :], kT[:, g, 0, :], ALU.subtract),
                                    "dve_k_lo")
                    banks.give(n, t_hi, t_lo)
                    k_ready.append((t_hi, t_lo))
                for t_ in range(TT):
                    n = banks.take(pe)
                    for k in range(KT):
                        c = k * NKV + G1 * HD1
                        mm = self.mm3(psum[:, n, :], self.h(slot, k, slice(t_ * P, (t_ + 1) * P)),
                                      pair(wkv, c, c + G1 * HD1), k == 0, k == KT - 1)
                    t = sig.done(mm, "pe_kv")
                    sig.wait(act, t, kv_free["v", b % 2])
                    t = sig.done(act.activation(v[:, b % 2, t_, :], psum[:, n, :], ACT.Copy), "act_v")
                    banks.give(n, t)
                kv_of[b] = k_ready, t

            q_of = {}

            def project_q(b, h):
                slot, h_ready, _ = h_of[b]
                n = banks.take(pe)
                sig.wait(pe, *t_q, *h_ready)
                for k in range(KT):
                    c = (h * KT + k) * P
                    mm = self.mm3(psum[:, n, :], pair(wq, c, c + P), self.h(slot, k), k == 0, k == KT - 1)
                t = sig.done(mm, "pe_q")
                if h == H1 - 1:
                    self.h_ring.give(slot, t)
                i = q_ring.turn % 2
                sig.wait(dve, *q_ring.freed[i])
                i = q_ring.take(act)
                sig.wait(act, t)
                t_hi = sig.done(act.activation(q[:, i, 0, :], psum[:, n, :], ACT.Copy, scale=-SCALE1), "act_q_hi")
                sig.wait(dve, t_hi)
                t_lo = sig.done(dve.scalar_tensor_tensor(q[:, i, 1, :], psum[:, n, :], -SCALE1, q[:, i, 0, :],
                                                         ALU.mult, ALU.subtract), "dve_q_lo")
                banks.give(n, t_hi, t_lo)
                q_of[b, h] = i, (t_hi, t_lo)

            e_of, et_of = {}, {}
            small_free = [None] * 4

            def scores(u):
                b, h, qt = u // (H1 * TT), u // TT % H1, u % TT
                g, W = h // HPG1, (qt + 1) * P
                i, ready = q_of[b, h]
                n = s_banks.take(pe)
                sig.wait(pe, *ready, *kv_of[b][0][g])
                mm = self.mm3(psum[:, n, 0:W], (q[:, i, 0, qt * P:W], q[:, i, 1, qt * P:W]),
                              (kT[:, g, 0, 0:W], kT[:, g, 1, 0:W]), True, True)
                t = sig.done(mm, "pe_s")
                if qt == TT - 1:
                    q_ring.give(i, t)
                    kv_free["k"] = t
                m = u % 4
                sig.wait(dve, t, t_mask, small_free[m])
                t = sig.done(dve.tensor_tensor_reduce(psum[:, n, 0:W], psum[:, n, 0:W], mask[:, S - W:S], 1.0, BIG,
                                                      ALU.add, ALU.min, nmax[:, m, :]), "dve_max")
                x = e_ring.take(act)
                sig.wait(act, t)
                t = sig.done(act.activation(e[:, x, 0:W], psum[:, n, 0:W], ACT.Exp, bias=nmax[:, m, :], scale=-1.0,
                                            accum_out=rsum[:, m, :]), "act_e")
                s_banks.give(n, t)
                e_of[u] = x, t

            def turn(u):
                b, h, qt = u // (H1 * TT), u // TT % H1, u % TT
                W, m = (qt + 1) * P, u % 4
                x, t_e = e_of[u]
                sig.wait(dve, t_e)
                t = sig.done(dve.reciprocal(rinv[:, m, :], rsum[:, m, :]), "dve_rinv")
                sig.wait(dve, t)
                t = sig.done(dve.tensor_scalar(e[:, x, 0:W], e[:, x, 0:W], rinv[:, m, 0:1], None, ALU.mult),
                             "dve_norm")
                small_free[m] = t
                n = t_banks.take(pe)
                sig.wait(pe, t)
                for k in range(qt + 1):
                    mm = pe.transpose(psum[:, n, k * P:(k + 1) * P], e[:, x, k * P:(k + 1) * P], self.ident[:, :])
                t = sig.done(mm, "pe_turn")
                e_ring.give(x, t)
                if qt == 0:
                    i = et_ring.turn % 2
                    sig.wait(act, *et_ring.freed[i])
                    et_of[b, h] = [et_ring.take(dve), []]
                i, ready = et_of[b, h]
                dst = et[:, i, 0:qt + 1, qt * P:W]
                src = psum[:, n, 0:W].rearrange("p (k q) -> p k q", q=P)
                sig.wait(act, t)
                t = sig.done(act.activation(dst, src, ACT.Copy), "act_et")
                t_banks.give(n, t)
                ready.append(t)

            o_of = {}

            def context(b, h):
                nonlocal oT_free
                g = h // HPG1
                i, ready = et_of[b, h]
                n = banks.take(pe)
                sig.wait(pe, *ready, kv_of[b][1])
                for k in range(TT):
                    mm = pe.matmul(psum[:, n, k * P:S], v[:, b % 2, k, g * HD1:(g + 1) * HD1], et[:, i, k, k * P:S],
                                   start=(k == 0), stop=(k == TT - 1), skip_group_check=True)
                t = sig.done(mm, "pe_pv")
                kv_free["v", b % 2] = t
                et_ring.give(i, t)
                j = ctx_ring.turn % 2
                sig.wait(dve, *ctx_ring.freed[j])
                j = ctx_ring.take(act)
                sig.wait(act, t)
                t_hi = sig.done(act.activation(ctx[:, j, 0, :], psum[:, n, :], ACT.Copy), "act_ctx_hi")
                sig.wait(dve, t_hi)
                t_lo = sig.done(dve.tensor_tensor(ctx[:, j, 1, :], psum[:, n, :], ctx[:, j, 0, :], ALU.subtract),
                                "dve_ctx_lo")
                banks.give(n, t_hi, t_lo)
                o_of[b, h] = j, (t_hi, t_lo)

            def output(b, h):
                nonlocal oT_free
                j, ready = o_of[b, h]
                if h == 0:
                    o_of[b] = [o_banks.take(pe) for _ in range(KT)]
                sig.wait(pe, *ready, *t_d)
                for m in range(KT):
                    c = h * D + m * P
                    mm = self.mm3(psum[:, o_of[b][m], :], pair(wd, c, c + P), (ctx[:, j, 0, :], ctx[:, j, 1, :]),
                                  h == 0, h == H1 - 1)
                t = sig.done(mm, "pe_o")
                ctx_ring.give(j, t)
                if h == H1 - 1:
                    ready = []
                    for m in range(KT):
                        sig.wait(dve, t, oT_free)
                        t_o = sig.done(dve.tensor_scalar(oT[:, m, :], psum[:, o_of[b][m], :],
                                                         self.gate[1][:, 0, m, b:b + 1], None, ALU.mult), "dve_o")
                        o_banks.give(o_of[b][m], t_o)
                        ready.append(t_o)
                    oT_free = self.residual(b, oT, ready, banks)

            U = H1 * TT
            events = {}
            at = lambda k, f, *a: events.setdefault(k, []).append((f, a))
            for b in range(B):
                base = U * b
                if b:
                    at(base - 40, lambda b=b: h_of.__setitem__(b, self.norm(b, 1, 0, banks)))
                at(base, project_kv, b)
                for h in range(H1):
                    at(base + TT * h - (0 if h == 0 else 2), project_q, b, h)
                    at(base + TT * (h + 1) + 3, context, b, h)
                    at(base + TT * (h + 1) + 5, output, b, h)
            for i in range(-2, B * U + 8):
                for f, a in events.get(i, []):
                    f(*a)
                if 0 <= i < B * U:
                    scores(i)
                if 0 <= i - 2 < B * U:
                    turn(i - 2)

    def experts(self, l, n_exp, picked, n_tiles, n_routed, last):
        sig, ins, pe, dve, act, pool = self.sig, self.ins, self.pe, self.dve, self.act, self.pool
        psum = self.psum
        with ExitStack() as st:
            sb = lambda name, shape, dt=F32: self.sb(st, f"m{l}_" + name, shape, dt)
            self.norm_buffers(st, f"m{l}", B)
            NS = 3
            WC = 2 * KT * P + D
            w32, w_ring = sb("w32", [P, NS, WC]), Ring(sig, NS)
            wh, wl, wh_ring = sb("wh", [P, NS, WC], F32R), sb("wl", [P, NS, WC], F32R), Ring(sig, NS)
            gate_w = sb("gate_w", [P, KT, n_exp])
            sel32 = sb("sel32", [2 * LO_ROW, n_routed * P])
            sel = sb("sel", [2 * LO_ROW, n_routed * P], F32R)
            combT = sb("combT", [2 * LO_ROW, B * S], F32R)
            silu, silu_ring = sb("silu", [P, 2, S]), Ring(sig, 2)
            up, up_ring = sb("up", [P, 2, S]), Ring(sig, 2)
            hid32, hid32_ring = sb("hid32", [P, 3, S]), Ring(sig, 3)
            hid, hid_ring = sb("hid", [P, 3, 2, S], F32R), Ring(sig, 3)
            yT = sb("yT", [P, KT, S])
            rt = sb("router", [P, 5, TT, n_exp])
            small = sb("router_small", [P, 3, TT])
            top = sb("top8", [P, TT, 8])

            banks, y_bank = Ring(sig, 4), 4
            t_gw = self.load(gate_w[:, :, :], ins[f"router{l}"])
            t_s = self.load(sel32[:, :], ins[f"sel{l}"])
            sig.wait(act, t_s)
            t_sel = sig.done(act.activation(sel[:, :], sel32[:, :], ACT.Copy), "act_sel")
            t_z = sig.done(pool.memset(combT[:, :].bitcast(F32), 0.0), "pool_combz")

            router_done = None

            def router(b, slot, t_h):
                nonlocal router_done
                n = banks.take(pe)
                sig.wait(pe, t_gw, t_h)
                for t_ in range(TT):
                    for k in range(KT):
                        mm = pe.matmul(psum[:, n, t_ * n_exp:(t_ + 1) * n_exp], self.h32[:, k, t_ * P:(t_ + 1) * P],
                                       gate_w[:, k, :], start=(k == 0), stop=(k == KT - 1))
                t_l = sig.done(mm, "pe_logits")
                self.h32_free = (*self.h32_free, t_l)
                logits = psum[:, n, 0:TT * n_exp].rearrange("p (t e) -> p t e", e=n_exp)
                ex, scores, rest, comb = (rt[:, i] for i in range(4))
                nmax, total, inv = (small[:, i, :] for i in range(3))
                sig.wait(dve, t_l, router_done)
                t = sig.done(dve.tensor_reduce(nmax, logits, AX.X, ALU.max, negate=True), "dve_router")
                sig.wait(act, t, router_done)
                for t_ in range(TT):
                    t = sig.done(act.activation(ex[:, t_, :], logits[:, t_, :], ACT.Exp, bias=nmax[:, t_:t_ + 1],
                                                accum_out=total[:, t_:t_ + 1]), "act_router")
                sig.wait(dve, t)
                banks.give(n, t)
                t = sig.done(dve.reciprocal(inv, total), "dve_router")
                sig.wait(dve, t)
                for t_ in range(TT):
                    t = sig.done(dve.tensor_scalar(scores[:, t_, :], ex[:, t_, :], inv[:, t_:t_ + 1], None, ALU.mult),
                                 "dve_router")
                sig.wait(dve, t)
                for t_ in range(TT):
                    t = sig.done(dve.max(top[:, t_, :], scores[:, t_, :]), "dve_router")
                sig.wait(dve, t)
                t = sig.done(dve.memset(top[:, :, picked:8], -1.0), "dve_router")
                sig.wait(dve, t)
                for t_ in range(TT):
                    t = sig.done(dve.match_replace(out=rest[:, t_, :], in_to_replace=top[:, t_, :],
                                                   in_values=scores[:, t_, :], imm_value=0.0), "dve_router")
                sig.wait(dve, t)
                t = sig.done(dve.tensor_tensor(comb, scores, rest, ALU.subtract), "dve_router")
                n = banks.take(pe)
                sig.wait(pe, t)
                for t_ in range(TT):
                    mm = pe.transpose(psum[0:n_exp, n, t_ * P:(t_ + 1) * P], comb[:, t_, :], self.ident[:, :])
                t = sig.done(mm, "pe_combT")
                router_done = t
                c = slice(b * S, (b + 1) * S)
                sig.wait(dve, t, t_z)
                t = sig.done(dve.tensor_copy(combT[0:n_exp, c], psum[0:n_exp, n, :]), "dve_combT")
                sig.wait(dve, t)
                t = sig.done(dve.tensor_tensor(combT[LO_ROW:LO_ROW + n_exp, c], psum[0:n_exp, n, :],
                                               combT[0:n_exp, c], ALU.subtract), "dve_combT")
                banks.give(n, t)
                comb_ready[b] = t

            comb_ready, h_of, w_of = {}, {}, {}

            def prepare(b):
                h_of[b] = self.norm(b, l, 1, banks)
                router(b, h_of[b][0], h_of[b][2])

            def weights(n):
                s = w_ring.take(self.sp)
                t = self.load(w32[:, s, :], ins[f"experts{l}"][n % n_tiles], name=f"load_m{l}_w{s}")
                i = wh_ring.take(act)
                two = self.split(wh[:, i, :], wl[:, i, :], w32[:, s, :], [t], "w", wh_ring.freed[i])
                w_ring.give(s, *two)
                w_of[n] = i, two

            def wpart(i, c, width=P):
                return wh[:, i, c:c + width], wl[:, i, c:c + width]

            hid_of = {}

            def unit(u):
                return u // (2 * n_tiles), u // 2 % n_tiles, u % 2

            def hidden(u):
                half, tile, c = unit(u)
                b = 2 * half + c
                slot, h_ready, _ = h_of[b]
                i, t_w = w_of[u // 2]
                out = []
                for part in range(2):
                    n = banks.take(pe)
                    sig.wait(pe, *t_w, *h_ready)
                    for k in range(KT):
                        mm = self.mm3(psum[:, n, :], wpart(i, (part * KT + k) * P), self.h(slot, k),
                                      k == 0, k == KT - 1)
                    out.append((n, sig.done(mm, "pe_gu")))
                x = silu_ring.take(act)
                sig.wait(act, out[0][1])
                t_s = sig.done(act.activation(silu[:, x, :], psum[:, out[0][0], :], ACT.Silu), "act_silu")
                banks.give(out[0][0], t_s)
                y = hid32_ring.take(dve)
                sig.wait(dve, t_s, out[1][1])
                if tile < n_routed:
                    n = banks.take(pe)
                    sig.wait(pe, comb_ready[b], t_sel)
                    mm = pe.matmul(psum[:, n, :], sel[:, tile * P:(tile + 1) * P], combT[:, b * S:(b + 1) * S],
                                   start=True, stop=True)
                    t_c = sig.done(mm, "pe_comb")
                    z = up_ring.take(dve)
                    t = sig.done(dve.tensor_tensor(up[:, z, :], psum[:, out[1][0], :], silu[:, x, :], ALU.mult),
                                 "dve_up")
                    banks.give(out[1][0], t)
                    silu_ring.give(x, t)
                    sig.wait(dve, t, t_c)
                    t = sig.done(dve.tensor_tensor(hid32[:, y, :], psum[:, n, :], up[:, z, :], ALU.mult), "dve_hid")
                    banks.give(n, t)
                    up_ring.give(z, t)
                else:
                    t = sig.done(dve.tensor_tensor(hid32[:, y, :], psum[:, out[1][0], :], silu[:, x, :], ALU.mult),
                                 "dve_hid")
                    banks.give(out[1][0], t)
                    silu_ring.give(x, t)
                f = hid_ring.turn % 3
                free = hid_ring.freed[f]
                hid_ring.turn += 1
                two = self.split(hid[:, f, 0, :], hid[:, f, 1, :], hid32[:, y, :], [t], "hid", free)
                hid32_ring.give(y, *two)
                hid_of[u] = f, two

            y_free = [None] * 2
            yT_free = None

            def down(u):
                nonlocal yT_free
                half, tile, c = unit(u)
                b = 2 * half + c
                i, _ = w_of[u // 2]
                f, ready = hid_of[u]
                sig.wait(pe, *ready)
                if tile == 0:
                    sig.wait(pe, y_free[c])
                for m in range(KT):
                    mm = self.mm3(psum[:, y_bank + 2 * c + m, :], wpart(i, 2 * KT * P + m * P),
                                  (hid[:, f, 0, :], hid[:, f, 1, :]), tile == 0, tile == n_tiles - 1)
                t = sig.done(mm, "pe_down")
                hid_ring.give(f, t)
                if c == 1:
                    wh_ring.give(i, t)
                if tile == n_tiles - 1:
                    ready = []
                    sig.wait(dve, t, yT_free)
                    for m in range(KT):
                        t = sig.done(dve.tensor_scalar(yT[:, m, :], psum[:, y_bank + 2 * c + m, :],
                                                       self.gate[l][:, 1, m, b:b + 1], None, ALU.mult), "dve_y")
                        ready.append(t)
                    y_free[c] = t
                    yT_free = self.residual(b, yT, ready, banks, store=last)

            total = 2 * n_tiles
            prepare(0)
            prepare(1)
            weights(0)
            weights(1)
            for u in range(2 * total + 1):
                if u % 2 == 0 and u // 2 + 2 < total and u < 2 * total:
                    pass
                if u in (6, 14):
                    prepare(2 + (u == 14))
                if u < 2 * total:
                    hidden(u)
                if u >= 1:
                    down(u - 1)
                if u % 2 == 0 and u and u // 2 + 1 < total:
                    weights(u // 2 + 1)


def adaln_program(nc, ins, out):
    with ExitStack() as stack:
        p = Program(nc, ins, out, stack)
        p.setup(stack)
        p.modulation(0)
        p.phase_barrier()
        p.modulation(1)
        p.phase_barrier()
        p.attention0()
        p.phase_barrier()
        p.experts(0, E0, K0, TILES0, TILES0_R, last=False)
        p.phase_barrier()
        p.attention1()
        p.phase_barrier()
        p.experts(1, E1, K1, TILES1, TILES1_R, last=True)
        p.sig.everything(p.sp)


def rope_table():
    theta = np.float32(10000.0) ** (-np.arange(0, HD0, 2, dtype=np.float32) / np.float32(HD0))
    freqs = np.arange(S, dtype=np.float32)[None, :] * theta.astype(np.float32)[:, None]
    table = np.zeros((P // HD0, HD0, 2, S), np.float32)
    table[:, :HD0 // 2, 0] = np.cos(freqs)
    table[:, :HD0 // 2, 1] = -np.sin(freqs)
    table[:, HD0 // 2:, 0] = 1.0
    return table.reshape(P, 2, S)


def stack_selectors():
    sel = np.zeros((P, 4, 4, P), np.float32)
    places = ((0, 1), (2, 3), (0, 2), (1, 3))
    for kind, where in enumerate(places):
        value = HD0 ** -0.5 if kind < 2 else 1.0
        for pair in range(4):
            for hh in range(2):
                for i in range(HD0):
                    for w in where:
                        sel[(2 * pair + hh) * HD0 + i, kind, pair, hh * STACK + w * HD0 + i] = value
    return sel.reshape(P, -1)


def expert_selector(n_exp, hidden, n_tiles):
    sel = np.zeros((2 * LO_ROW, n_tiles * P), np.float32)
    unit = np.arange(n_tiles * P)
    sel[unit // hidden, unit] = 1.0
    sel[LO_ROW + unit // hidden, unit] = 1.0
    return sel


def causal_mask():
    mask = np.zeros((P, S), np.float32)
    mask[:, S - P:] = np.where(np.arange(P)[:, None] >= np.arange(P)[None, :], 0.0, BIG)
    return mask


def k_tiles(w):
    k, n = w.shape
    return w.reshape(k // P, P, n).transpose(1, 0, 2).reshape(P, -1)


def pack_tiles(gate, up, down):
    n = -(-gate.shape[1] // P)
    pad = n * P - gate.shape[1]
    gate, up = (np.pad(a, ((0, 0), (0, pad))).reshape(KT, P, n, P).transpose(2, 1, 0, 3) for a in (gate, up))
    down = np.pad(down, ((0, pad), (0, 0))).reshape(n, P, D)
    return np.concatenate([gate.reshape(n, P, -1), up.reshape(n, P, -1), down], axis=2)


def lay_out(a):
    heads = np.arange(D).reshape(H0, HD0)
    even, odd = heads[:, ::2], heads[:, 1::2]
    value = np.concatenate([even, odd], axis=1).reshape(-1)
    partner = np.concatenate([odd, even], axis=1).reshape(-1)
    wq, wk, wv, wo = (a[f"L0_attn_w{x}"] for x in "qkvo")
    w0 = np.concatenate([w.T[:, o] for w in (wq, wk) for o in (value, partner)] + [wv.T], axis=1)
    b0 = np.concatenate([a[f"L0_attn_b{x}"][o].reshape(2, P) for x in "qk" for o in (value, partner)]).T
    wo_rows = np.zeros((H0, 32, D), np.float32)
    wo_rows[:, :HD0] = wo.T.reshape(H0, HD0, D)
    wq1 = a["L1_attn_w_q"].reshape(KT, P, H1, HD1).transpose(1, 2, 0, 3).reshape(P, -1)
    flat = lambda w: w.transpose(1, 0, 2).reshape(w.shape[1], -1)
    w1, w2, w3 = (a[f"L1_ffn_w{i}"] for i in (1, 2, 3))
    ffn0 = pack_tiles(
        np.concatenate([flat(a["L0_ffn_w_gate"]), a["L0_ffn_sw_gate"]], axis=1),
        np.concatenate([flat(a["L0_ffn_w_up"]), a["L0_ffn_sw_up"]], axis=1),
        np.concatenate([a["L0_ffn_w_down"].reshape(-1, D), a["L0_ffn_sw_down"]], axis=0))
    ffn1 = pack_tiles(
        np.concatenate([w1.reshape(-1, D), a["L1_ffn_sw1"]], axis=0).T,
        np.concatenate([w3.reshape(-1, D), a["L1_ffn_sw3"]], axis=0).T,
        np.concatenate([w2.transpose(0, 2, 1).reshape(-1, D), a["L1_ffn_sw2"].T], axis=0))
    return {
        "x": a["L0_attn_x"],
        "ident": np.eye(P, dtype=np.float32),
        "c0": a["L0_c"].T.reshape(KT, P, B).transpose(1, 0, 2),
        "c1": a["L1_c"].T.reshape(KT, P, B).transpose(1, 0, 2),
        "wmod0": a["L0_wmod"], "wmod1": a["L1_wmod"],
        "w0_qkv": k_tiles(w0), "b0_qk": b0, "b0_v": a["L0_attn_bv"],
        "w0_o": k_tiles(wo_rows.reshape(-1, D)), "b0_o": a["L0_attn_bo"].reshape(KT, P).T,
        "rope": rope_table(), "stack_sel": stack_selectors(), "mask": causal_mask(),
        "w1_q": wq1, "w1_kv": k_tiles(a["L1_attn_w_kv"]), "w1_d": k_tiles(a["L1_attn_w_dense"]),
        "router0": a["L0_ffn_gate_w"].reshape(KT, P, E0).transpose(1, 0, 2),
        "router1": a["L1_ffn_gate_w"].T.reshape(KT, P, E1).transpose(1, 0, 2),
        "sel0": expert_selector(E0, HID0, TILES0_R), "sel1": expert_selector(E1, HID1, TILES1_R),
        "experts0": ffn0, "experts1": ffn1,
    }


def kernel(**inputs):
    import concourse.bacc as bacc
    from concourse.bass_utils import run_bass_kernel_spmd

    nc = bacc.Bacc("TRN2", target_bir_lowering=False, num_devices=1)
    laid = lay_out({k: np.asarray(v) for k, v in inputs.items()})
    arrays, aps = {}, {}
    for name, a in laid.items():
        arrays[f"in_{name}"] = a = np.ascontiguousarray(a)
        aps[name] = nc.dram_tensor(f"in_{name}", a.shape, mybir.dt.from_np(a.dtype), kind="ExternalInput").ap()
    out = nc.dram_tensor("out_0_dram", (B, S, D), F32, kind="ExternalOutput").ap()
    adaln_program(nc, aps, out)
    r = run_bass_kernel_spmd(nc, [arrays], core_ids=[0])
    return r.results[0]["out_0_dram"]
```

```python
from contextlib import ExitStack

import numpy as np

import concourse.bass as bass
from concourse import mybir

ALU = mybir.AluOpType
ACT = mybir.ActivationFunctionType
AX = mybir.AxisListType
F32 = mybir.dt.float32
F32R = mybir.dt.float32r

P = 128
B, S, D = 4, 512, 256
KT = D // P
TT = S // P
NT = B * TT
LN_EPS = 1e-5
BIG = 3.0e38

H0, HD0 = 16, 16
GROUP0 = 4
STACK = 64
H1, G1, HD1 = 16, 4, 128
HPG1 = H1 // G1
SCALE1 = HD1 ** -0.5
E0, K0, HID0, SH0 = 8, 2, 176, 352
E1, K1, HID1, SH1 = 32, 4, 128, 256
TILES0_R = E0 * HID0 // P
TILES0 = -(-(E0 * HID0 + SH0) // P)
TILES1_R = E1
TILES1 = E1 + SH1 // P
DOWN_LAG = 2
LO_ROW = 32


class Signals:

    def __init__(self, nc, stack):
        self.nc, self.stack = nc, stack
        self.sems, self.count, self.passed = {}, {}, {}

    def done(self, instruction, name, by=1):
        if name not in self.sems:
            self.sems[name] = self.stack.enter_context(self.nc.semaphore(name))
            self.count[name] = 0
        instruction.then_inc(self.sems[name], by)
        self.count[name] += by
        return name, self.count[name]

    def wait(self, engine, *values):
        for value in values:
            if value is None:
                continue
            name, count = value
            key = (str(engine.engine), name)
            if self.passed.get(key, 0) < count:
                engine.wait_ge(self.sems[name], count)
                self.passed[key] = count

    def everything(self, engine):
        self.wait(engine, *self.count.items())


class Ring:

    def __init__(self, signals, n, first=0):
        self.signals, self.n, self.first, self.turn = signals, n, first, 0
        self.freed = [()] * n

    def open(self, k=1):
        return all(self.freed[(self.turn + j) % self.n] is not None for j in range(k))

    def take(self, *engines):
        assert self.open(), "a buffer is taken before it was given back"
        i = self.turn % self.n
        self.turn += 1
        for engine in engines:
            self.signals.wait(engine, *self.freed[i])
        self.freed[i] = None
        return i + self.first

    def give(self, i, *values):
        self.freed[i - self.first] = values


class Steps:

    def __init__(self):
        self.due, self.n = {}, 0

    def at(self, step, task):
        self.n += 1
        self.due.setdefault(step, []).append((step, self.n, task))

    def run(self):
        while self.due:
            step = min(self.due)
            for start, n, task in sorted(self.due.pop(step), key=lambda x: x[:2]):
                pause = next(task, None)
                if pause is not None:
                    self.due.setdefault(step + pause, []).append((start, n, task))


class Program:
    def __init__(self, nc, ins, out, stack):
        self.nc, self.ins, self.out = nc, ins, out
        self.pe, self.dve, self.act, self.pool, self.sp = nc.tensor, nc.vector, nc.scalar, nc.gpsimd, nc.sync
        self.sig = Signals(nc, stack)
        self.stack = stack
        self.psum = stack.enter_context(nc.psum_tensor("psum", [P, 8, 512], F32))
        self.n_loads = 0

    def sb(self, stack, name, shape, dtype=F32):
        return stack.enter_context(self.nc.sbuf_tensor(name, shape, dtype))

    def load(self, dst, src, *waits, name=None, queue=None):
        queue = queue or self.sp
        self.sig.wait(queue, *waits)
        self.n_loads += 1
        return self.sig.done(queue.dma_start(dst, src), name or f"load{self.n_loads}", 16)

    def mm3(self, out, lhs, rhs, start, stop):
        (lh, ll), (rh, rl) = lhs, rhs
        self.pe.matmul(out, lh, rh, start=start, stop=False, skip_group_check=True)
        self.pe.matmul(out, lh, rl, start=False, stop=False, skip_group_check=True)
        return self.pe.matmul(out, ll, rh, start=False, stop=stop, skip_group_check=True)

    def split(self, hi, lo, src, ready, name):
        sig = self.sig
        sig.wait(self.act, *ready)
        t_hi = sig.done(self.act.activation(hi, src, ACT.Copy), f"act_{name}_hi")
        sig.wait(self.pool, *ready, t_hi)
        t_lo = sig.done(self.pool.tensor_tensor(lo, src, hi, ALU.subtract), f"pool_{name}_lo")
        return t_hi, t_lo

    def phase_barrier(self):
        for engine in (self.pe, self.dve, self.act, self.pool, self.sp):
            self.sig.everything(engine)

    def setup(self, stack):
        sig, ins = self.sig, self.ins
        self.x = self.sb(stack, "x_nat", [P, NT, D])
        self.ident = self.sb(stack, "ident", [P, P])
        self.mod = [self.sb(stack, f"mod{l}", [P, 12, B]) for l in range(2)]
        self.gate = [self.sb(stack, f"gate{l}", [P, 2, KT, B]) for l in range(2)]
        self.stats = self.sb(stack, "ln_stats", [P, TT, 6])
        self.mv = self.sb(stack, "ln_mean_var", [P, TT, 2])
        self.lnw = self.sb(stack, "ln_work", [P, 5, TT])
        self.eps = self.sb(stack, "eps", [P, 1])
        self.t_ident = self.load(self.ident[:, :], ins["ident"])
        x_dram = ins["x"].rearrange("b (t p) d -> p (b t) d", p=P)
        self.x_ready = {}
        for b in range(B):
            t = self.load(self.x[:, b * TT:(b + 1) * TT, :], x_dram[:, b * TT:(b + 1) * TT, :])
            self.x_ready.update({b * TT + i: t for i in range(TT)})
        self.t_eps = sig.done(self.pool.memset(self.eps[:, :], LN_EPS), "pool_eps")
        self.ln_done = None

    def modulation(self, l):
        sig, ins = self.sig, self.ins
        with ExitStack() as st:
            c = self.sb(st, f"c{l}", [P, KT, B])
            sc = self.sb(st, f"silu_c{l}", [P, KT, B])
            w = self.sb(st, f"wmod{l}", [P, KT, 6 * D])
            work = self.sb(st, f"gate_work{l}", [P, 3, 2, KT, B])
            t_c = self.load(c[:, :, :], ins[f"c{l}"])
            t_w = self.load(w[:, :, :], ins[f"wmod{l}"].rearrange("(k p) n -> p k n", p=P))
            sig.wait(self.act, t_c)
            t_sc = sig.done(self.act.activation(sc[:, :, :], c[:, :, :], ACT.Silu), "act_silu_c")
            sig.wait(self.pe, t_sc, t_w)
            ps = self.psum[:, l, 0:12 * B].rearrange("p (m b) -> p m b", b=B)
            for m in range(12):
                for k in range(KT):
                    mm = self.pe.matmul(ps[:, m, :], w[:, k, m * P:(m + 1) * P], sc[:, k, :],
                                        start=(k == 0), stop=(k == KT - 1))
            t_mm = sig.done(mm, "pe_mod")
            mod = self.mod[l]
            sig.wait(self.dve, t_mm)
            t = sig.done(self.dve.tensor_copy(mod[:, :, :], ps), "dve_mod")
            sig.wait(self.dve, t)
            for j in (1, 4):
                v = mod[:, 2 * j:2 * j + 2, :]
                t = sig.done(self.dve.tensor_scalar(v, v, 1.0, None, ALU.add), "dve_mod")
            for n, j in enumerate((2, 5)):
                g = mod[:, 2 * j:2 * j + 2, :]
                neg, sign, mag = (work[:, i, n] for i in range(3))
                t1 = sig.done(self.dve.tensor_scalar(neg, g, -1.0, None, ALU.mult), "dve_mod")
                t2 = sig.done(self.dve.tensor_scalar(sign, g, 0.0, 2.0, ALU.is_ge, ALU.mult), "dve_mod")
                sig.wait(self.dve, t1)
                t3 = sig.done(self.dve.tensor_tensor(mag, g, neg, ALU.max), "dve_mod")
                sig.wait(self.dve, t3)
                t4 = sig.done(self.dve.tensor_scalar(neg, mag, 0.25, None, ALU.max), "dve_mod")
                sig.wait(self.dve, t4)
                t = sig.done(self.dve.scalar_tensor_tensor(self.gate[l][:, n], sign, -1.0, neg, ALU.add, ALU.mult),
                             "dve_mod")
            self.t_mod = t

    def norm_buffers(self, stack, tag, n_h):
        self.xn = self.sb(stack, f"xn_{tag}", [P, 2, D])
        self.xn_ring = Ring(self.sig, 2)
        self.h32, self.h32_ring = self.sb(stack, f"h32_{tag}", [P, 1, KT, S]), Ring(self.sig, 1)
        self.h_of = {}
        self.hh = self.sb(stack, f"h_hi_{tag}", [P, n_h, KT, S], F32R)
        self.hl = self.sb(stack, f"h_lo_{tag}", [P, n_h, KT, S], F32R)
        self.h_ring = Ring(self.sig, n_h)

    def norm(self, b, l, which, banks, spread=True):
        sig, dve, act, pe = self.sig, self.dve, self.act, self.pe
        stats, mv, w = self.stats, self.mv, self.lnw
        while any((b * TT + t) not in self.x_ready for t in range(TT)):
            yield 1
        sig.wait(dve, self.ln_done, self.t_mod)
        for t in range(TT):
            tile = b * TT + t
            sig.wait(dve, self.x_ready[tile])
            d = sig.done(dve.bn_stats(stats[:, t, :], self.x[:, tile, :]), "dve_stats")
        sig.wait(dve, d)
        for t in range(TT):
            d = sig.done(dve.bn_aggr(mv[:, t, :], stats[:, t, :]), "dve_stats")
        var, mean = mv[:, :, 1], mv[:, :, 0]
        sd, r, a, c, rstd = (w[:, i, :] for i in range(5))
        yield 1
        sig.wait(act, d, self.t_eps)
        d = sig.done(act.activation(sd, var, ACT.Sqrt, bias=self.eps[:, 0:1]), "act_sd")
        yield 1
        sig.wait(dve, d)
        d = sig.done(dve.reciprocal(r, sd), "dve_rstd")
        sig.wait(dve, d)
        d = sig.done(dve.scalar_tensor_tensor(a, var, LN_EPS, r, ALU.add, ALU.mult), "dve_rstd")
        sig.wait(dve, d)
        d = sig.done(dve.tensor_tensor(c, a, r, ALU.mult), "dve_rstd")
        sig.wait(dve, d)
        d = sig.done(dve.tensor_scalar(a, c, -0.5, 1.5, ALU.mult, ALU.add), "dve_rstd")
        sig.wait(dve, d)
        d = sig.done(dve.tensor_tensor(rstd, a, r, ALU.mult), "dve_rstd")
        sig.wait(dve, d)
        while not (banks.open(KT) and self.h_ring.open() and self.h32_ring.open()):
            yield 1
        bank = [banks.take(pe) for _ in range(KT)]
        sig.wait(pe, self.t_ident)
        for t in range(TT):
            n = self.xn_ring.take(dve)
            d = sig.done(dve.tensor_scalar(self.xn[:, n, :], self.x[:, b * TT + t, :], mean[:, t:t + 1],
                                           rstd[:, t:t + 1], ALU.subtract, ALU.mult), "dve_xn")
            sig.wait(pe, d)
            for k in range(KT):
                mm = pe.transpose(self.psum[:, bank[k], t * P:(t + 1) * P], self.xn[:, n, k * P:(k + 1) * P],
                                  self.ident[:, :])
            t_xT = sig.done(mm, "pe_xT")
            self.xn_ring.give(n, t_xT)
            if t < TT - 1 and spread:
                yield 1
        self.ln_done = d
        if spread:
            yield 1
        slot = self.h_ring.take(act, self.pool)
        s32 = self.h32_ring.take(dve)
        sig.wait(dve, t_xT)
        j = 3 * which
        mod = self.mod[l]
        ready = []
        for k in range(KT):
            t_h = sig.done(dve.tensor_scalar(self.h32[:, s32, k, :], self.psum[:, bank[k], :],
                                             mod[:, 2 * (j + 1) + k, b:b + 1], mod[:, 2 * j + k, b:b + 1],
                                             ALU.mult, ALU.add), "dve_h")
            banks.give(bank[k], t_h)
            ready += self.split(self.hh[:, slot, k, :], self.hl[:, slot, k, :], self.h32[:, s32, k, :], [t_h], "h")
        if which == 0:
            self.h32_ring.give(s32, *ready)
        self.h_of[b] = slot, ready, t_h, s32

    def h(self, slot, k, cols=slice(0, S)):
        return self.hh[:, slot, k, cols], self.hl[:, slot, k, cols]

    def residual(self, b, yT, ring, slot, y_ready, banks, store=False):
        sig, pe, dve = self.sig, self.pe, self.dve
        tiles = [b * TT + t for t in range(TT)]
        before = [self.x_ready.pop(t) for t in tiles]
        for half in range(2):
            while not banks.open():
                yield 1
            n = banks.take(pe)
            sig.wait(pe, *y_ready)
            for t in range(TT // 2):
                tile = half * (TT // 2) + t
                for k in range(KT):
                    mm = pe.transpose(self.psum[:, n, t * D + k * P:t * D + (k + 1) * P],
                                      yT[:, k, tile * P:(tile + 1) * P], self.ident[:, :])
            t_T = sig.done(mm, "pe_yT")
            if half:
                ring.give(slot, t_T)
            yield 1
            lo = b * TT + half * (TT // 2)
            xs = self.x[:, lo:lo + TT // 2, :].rearrange("p t d -> p (t d)")
            sig.wait(dve, t_T, *before)
            t_x = sig.done(dve.tensor_tensor(xs, xs, self.psum[:, n, :], ALU.add), "dve_x")
            banks.give(n, t_x)
            for t in range(TT // 2):
                self.x_ready[lo + t] = t_x
            if store:
                o = self.out.rearrange("b (t p) d -> p (b t) d", p=P)
                self.load(o[:, lo:lo + TT // 2, :], self.x[:, lo:lo + TT // 2, :], t_x)

    def split_weights(self, stage, ring, name, src, hi, lo, width):
        ready = []
        n = src.shape[1]
        for a in range(0, n, width):
            e = min(n, a + width)
            s = ring.take(self.sp)
            t = self.load(stage[:, s, 0:e - a], src[:, a:e], name=f"stage_{name}{s}")
            two = self.split(hi[:, a:e], lo[:, a:e], stage[:, s, 0:e - a], [t], "w")
            ring.give(s, *two)
            ready += two
        return ready

    def attention0(self):
        sig, ins, pe, dve, act, pool = self.sig, self.ins, self.pe, self.dve, self.act, self.pool
        psum = self.psum
        with ExitStack() as st:
            sb = lambda name, shape, dt=F32: self.sb(st, "a0_" + name, shape, dt)
            self.norm_buffers(st, "a0", 2)
            NW = 5 * D
            w_hi, w_lo = sb("w_hi", [P, KT * NW], F32R), sb("w_lo", [P, KT * NW], F32R)
            wo_hi, wo_lo = sb("wo_hi", [P, GROUP0 * D], F32R), sb("wo_lo", [P, GROUP0 * D], F32R)
            sel = sb("stack_sel", [P, 4, 4, P], F32R)
            rope = sb("rope", [P, 2, S])
            bias, bv, bo = sb("bias", [P, 8]), sb("bv", [P, D]), sb("bo", [P, KT])
            stage, stage_ring = sb("stage", [P, 2, 512]), Ring(sig, 2)
            rp = sb("rope_tmp", [P, 3, S])
            rp_ring = Ring(sig, 1)
            qk = sb("qk", [P, 2, 2, 2, S], F32R)
            qk_ready, qk_ring = {}, {(i, m): Ring(sig, 1) for i in range(2) for m in range(2)}
            stk = sb("stk", [P, 2, 3, S], F32R)
            stk_ring = Ring(sig, 3)
            v, v_ring = sb("v", [P, 2, TT, H0, 32]), Ring(sig, 2)
            e, e_ring = sb("e", [P, 3, S]), Ring(sig, 3)
            NET = 5
            et, et_ring = sb("et", [P, NET, TT, S]), Ring(sig, NET)
            nmax, rsum = sb("nmax", [P, H0, TT]), sb("rsum", [P, H0, TT])
            rinv, rexp = sb("rinv", [P, GROUP0, TT]), sb("rexp", [P, TT, GROUP0, 32])
            rb, ctx32 = sb("rb", [P, S]), sb("ctx32", [P, S])
            rexp_ring, ctx32_ring, oT_ring = Ring(sig, 1), Ring(sig, 1), Ring(sig, 1)
            ctx_rings = [Ring(sig, 1) for _ in range(GROUP0)]
            ctx = sb("ctx", [P, 2, GROUP0, S], F32R)
            oT = sb("oT", [P, KT, S])

            s_banks, t_banks = Ring(sig, 3), Ring(sig, 2, 3)
            pv_banks, banks = Ring(sig, 1, 5), Ring(sig, 2, 6)

            steps = Steps()
            h_of = self.h_of
            steps.at(-30, self.norm(0, 0, 0, banks))
            t_w = self.split_weights(stage, stage_ring, "a0", ins["w0_qkv"], w_hi, w_lo, 512)
            self.load(rope[:, :, :], ins["rope"], name="a0_small")
            self.load(bias[:, :], ins["b0_qk"], name="a0_small")
            self.load(bo[:, :], ins["b0_o"], name="a0_small")
            t_small = self.load(bv[:, :], ins["b0_v"].partition_broadcast(P), name="a0_small")
            sel_f = sel[:, :, :, :].rearrange("p a b c -> p (a b c)")
            t_sel = []
            for a in range(0, 2048, 512):
                s = stage_ring.take(self.sp)
                t = self.load(stage[:, s, :], ins["stack_sel"][:, a:a + 512], name=f"stage_a0{s}")
                sig.wait(act, t)
                t = sig.done(act.activation(sel_f[:, a:a + 512], stage[:, s, :], ACT.Copy), "act_sel")
                stage_ring.give(s, t)
                t_sel.append(t)
            t_wo = self.split_weights(stage, stage_ring, "a0", ins["w0_o"], wo_hi, wo_lo, 512)
            t_vz = sig.done(pool.memset(v[:, :, :, :, :].rearrange("p a b c d -> p (a b c d)"), 0.0), "pool_vzero")

            def w(k, a, e_):
                return w_hi[:, k * NW + a:k * NW + e_], w_lo[:, k * NW + a:k * NW + e_]

            def project(b):
                while b not in h_of:
                    yield 1
                slot, h_ready = h_of[b][:2]
                for m in range(2):
                    for i in range(2):
                        while not banks.open(2):
                            yield 1
                        two, pair = [], [banks.take(pe) for _ in range(2)]
                        for part, n in enumerate(pair):
                            sig.wait(pe, *t_w, *h_ready)
                            col = (2 * i + part) * D + m * P
                            for k in range(KT):
                                mm = self.mm3(psum[:, n, :], w(k, col, col + P), self.h(slot, k), k == 0,
                                              k == KT - 1)
                                if k == 0:
                                    yield 1
                            two.append((n, sig.done(mm, "pe_qk")))
                            yield 1
                        while not rp_ring.open():
                            yield 1
                        r = rp_ring.take(dve)
                        sig.wait(dve, t_small)
                        t_part = []
                        for part, (n, t) in enumerate(two):
                            sig.wait(dve, t)
                            c = 4 * i + 2 * part + m
                            t = sig.done(dve.scalar_tensor_tensor(rp[:, part, :], psum[:, n, :], bias[:, c:c + 1],
                                                                  rope[:, part, :], ALU.add, ALU.mult), "dve_rope")
                            banks.give(n, t)
                            t_part.append(t)
                        sig.wait(dve, *t_part)
                        t = sig.done(dve.tensor_tensor(rp[:, 2, :], rp[:, 0, :], rp[:, 1, :], ALU.add), "dve_rope")
                        yield 1
                        while not qk_ring[i, m].open():
                            yield 1
                        qk_ring[i, m].take(act, pool)
                        two = self.split(qk[:, i, m, 0, :], qk[:, i, m, 1, :], rp[:, 2, :], [t], "qk")
                        rp_ring.give(r, *two)
                        qk_ready[b, i, m] = two
                    if m == 0:
                        yield from project_v(b, slot, h_ready)
                self.h_ring.give(slot, ("pe_qk", sig.count["pe_qk"]), ("pe_v", sig.count["pe_v"]))

            def project_v(b, slot, h_ready):
                y = v_ring.take(dve)
                ready = []
                for t_ in range(TT):
                    while not banks.open():
                        yield 1
                    n = banks.take(pe)
                    sig.wait(pe, *t_w, *h_ready)
                    for k in range(KT):
                        mm = self.mm3(psum[:, n, 0:D], self.h(slot, k, slice(t_ * P, (t_ + 1) * P)),
                                      w(k, 4 * D, 5 * D), k == 0, k == KT - 1)
                    t = sig.done(mm, "pe_v")
                    yield 1
                    sig.wait(dve, t, t_small, t_vz)
                    t = sig.done(dve.tensor_tensor(v[:, y, t_, :, 0:HD0],
                                                   psum[:, n, 0:D].rearrange("p (h c) -> p h c", c=HD0),
                                                   bv[:, :].rearrange("p (h c) -> p h c", c=HD0), ALU.add), "dve_v")
                    banks.give(n, t)
                v_of[b] = y, t

            stk_of, v_of = {}, {}

            def stack_pair(b, pair):
                m, p = divmod(pair, 4)
                while (b, 1, m) not in qk_ready or not stk_ring.open() or not banks.open(2):
                    yield 1
                s = stk_ring.take(act)
                two = []
                for i in range(2):
                    n = banks.take(pe)
                    sig.wait(pe, *t_sel, *qk_ready[b, i, m])
                    for x in range(2):
                        mm = pe.matmul(psum[:, n, :], sel[:, 2 * i + x, p, :], qk[:, i, m, x, :],
                                       start=(x == 0), stop=(x == 1))
                    two.append((n, sig.done(mm, "pe_stack")))
                    if p == 3:
                        qk_ring[i, m].give(0, two[-1][1])
                yield 1
                ready = []
                for i, (n, t) in enumerate(two):
                    sig.wait(act, t)
                    t = sig.done(act.activation(stk[:, i, s, :], psum[:, n, :], ACT.Copy), "act_stack")
                    banks.give(n, t)
                    ready.append(t)
                stk_of[b, pair] = s, ready

            et_of, group_sums = {}, {}

            def unit(u):
                b, h, qt = u // (H0 * TT), u // TT % H0, u % TT
                g = h // GROUP0
                while (b, h // 2) not in stk_of or not s_banks.open():
                    yield 1
                s, ready = stk_of[b, h // 2]
                r0 = STACK * (h % 2)
                n = s_banks.take(pe)
                sig.wait(pe, *ready)
                mm = pe.matmul(psum[:, n, :], stk[r0:r0 + STACK, 0, s, qt * P:(qt + 1) * P],
                               stk[r0:r0 + STACK, 1, s, :], start=True, stop=True)
                t = sig.done(mm, "pe_s")
                if h % 2 and qt == TT - 1:
                    stk_ring.give(s, t)
                yield 1
                before = group_sums[b - 1, g] if b else None
                sig.wait(dve, t, before)
                t = sig.done(dve.tensor_reduce(nmax[:, h, qt:qt + 1], psum[:, n, :], AX.X, ALU.max, negate=True),
                             "dve_max")
                while not e_ring.open():
                    yield 1
                x = e_ring.take(act)
                sig.wait(act, t, before)
                t = sig.done(act.activation(e[:, x, :], psum[:, n, :], ACT.Exp, bias=nmax[:, h, qt:qt + 1],
                                            accum_out=rsum[:, h, qt:qt + 1]), "act_e")
                s_banks.give(n, t)
                yield 2
                while not t_banks.open():
                    yield 1
                n = t_banks.take(pe)
                sig.wait(pe, t, self.t_ident)
                for k in range(TT):
                    mm = pe.transpose(psum[:, n, k * P:(k + 1) * P], e[:, x, k * P:(k + 1) * P], self.ident[:, :])
                t_e, t = t, sig.done(mm, "pe_turn")
                e_ring.give(x, t)
                yield 1
                if qt == 0:
                    while not et_ring.open():
                        yield 1
                    et_of[b, h] = [et_ring.take(act, dve), []]
                while (b, h) not in et_of:
                    yield 1
                i, ready = et_of[b, h]
                dst = et[:, i, :, qt * P:(qt + 1) * P]
                src = psum[:, n, :].rearrange("p (k q) -> p k q", k=TT)
                if u % 5 in (1, 3):
                    sig.wait(act, t)
                    t = sig.done(act.activation(dst, src, ACT.Copy), "act_et")
                else:
                    sig.wait(dve, t)
                    t = sig.done(dve.tensor_copy(dst, src), "dve_et")
                t_banks.give(n, t)
                ready += [t, t_e]

            def context(b, g):
                heads = [(b, GROUP0 * g + j) for j in range(GROUP0)]
                while any(h not in et_of or len(et_of[h][1]) < 2 * TT for h in heads):
                    yield 1
                while not pv_banks.open():
                    yield 1
                n = pv_banks.take(pe)
                y, t_v = v_of[b]
                sig.wait(pe, t_v)
                for h in heads:
                    sig.wait(pe, *et_of[h][1])
                    sig.wait(dve, *et_of[h][1][1::2])
                t_r = sig.done(dve.reciprocal(rinv[:, :, :], rsum[:, GROUP0 * g:GROUP0 * (g + 1), :]), "dve_rinv")
                group_sums[b, g] = t_r
                for k in range(TT):
                    for j in range(GROUP0):
                        mm = pe.matmul(psum[32 * j:32 * j + 32, n, :], v[:, y, k, GROUP0 * g + j, :],
                                       et[:, et_of[heads[j]][0], k, :], start=(k == 0), stop=(k == TT - 1),
                                       tile_position=(0, 32 * j), skip_group_check=True)
                    if k < TT - 1:
                        yield 1
                t_pv = sig.done(mm, "pe_pv")
                if g == H0 // GROUP0 - 1:
                    v_ring.give(y, t_pv)
                for h in heads:
                    et_ring.give(et_of[h][0], t_pv)
                r = rexp_ring.take(pool)
                sig.wait(pool, t_r)
                t_x = sig.done(pool.tensor_copy(rexp[:, :, :, :], rinv[:, :, :].rearrange("p j t -> p t j")
                                                .unsqueeze(3).broadcast_to([P, TT, GROUP0, 32])), "pool_rexp")
                yield 2
                while not banks.open():
                    yield 1
                m = banks.take(pe)
                sig.wait(pe, t_x)
                for q in range(TT):
                    mm = pe.matmul(psum[:, m, q * P:(q + 1) * P], rexp[:, q].rearrange("p j i -> p (j i)"),
                                   self.ident[:, :], start=True, stop=True)
                t = sig.done(mm, "pe_rb")
                rexp_ring.give(r, t)
                yield 1
                c = ctx32_ring.take(act, dve)
                sig.wait(act, t)
                t = sig.done(act.activation(rb[:, :], psum[:, m, :], ACT.Copy), "act_rb")
                banks.give(m, t)
                yield 1
                sig.wait(dve, t, t_pv)
                t = sig.done(dve.tensor_tensor(ctx32[:, :], psum[:, n, :], rb[:, :], ALU.mult), "dve_ctx")
                pv_banks.give(n, t)
                yield 1
                while not ctx_rings[g].open():
                    yield 1
                ctx_rings[g].take(act, pool)
                two = self.split(ctx[:, 0, g, :], ctx[:, 1, g, :], ctx32[:, :], [t], "ctx")
                ctx32_ring.give(c, *two)
                ctx_ready[b, g] = two

            ctx_ready = {}

            def output(b):
                while (b, GROUP0 - 1) not in ctx_ready or not oT_ring.open():
                    yield 1
                y = oT_ring.take(dve)
                ready = []
                for m in range(KT):
                    while not banks.open():
                        yield 1
                    n = banks.take(pe)
                    sig.wait(pe, *t_wo)
                    for g in range(GROUP0):
                        sig.wait(pe, *ctx_ready[b, g])
                        c = slice(g * D + m * P, g * D + (m + 1) * P)
                        mm = self.mm3(psum[:, n, :], (wo_hi[:, c], wo_lo[:, c]), (ctx[:, 0, g, :], ctx[:, 1, g, :]),
                                      g == 0, g == GROUP0 - 1)
                        if g < GROUP0 - 1:
                            yield 1
                    t_mm = t = sig.done(mm, "pe_o")
                    yield 1
                    sig.wait(dve, t, t_small)
                    t = sig.done(dve.tensor_scalar(oT[:, m, :], psum[:, n, :], bo[:, m:m + 1],
                                                   self.gate[0][:, 0, m, b:b + 1], ALU.add, ALU.mult), "dve_o")
                    banks.give(n, t)
                    ready.append(t)
                for ring in ctx_rings:
                    ring.give(0, t_mm)
                yield from self.residual(b, oT, oT_ring, y, ready, banks)

            U = H0 * TT
            for b in range(B):
                base = U * b
                if b:
                    steps.at(base - 60, self.norm(b, 0, 0, banks))
                steps.at(base - (48 if b else 15), project(b))
                for pair in range(H0 // 2):
                    steps.at(base + 8 * pair - 6, stack_pair(b, pair))
                for g in range(GROUP0):
                    steps.at(base + 16 * (g + 1) + 4, context(b, g))
                steps.at(base + U + 12, output(b))
            for u in range(B * U):
                steps.at(u, unit(u))
            steps.run()

    def attention1(self):
        sig, ins, pe, dve, act, pool = self.sig, self.ins, self.pe, self.dve, self.act, self.pool
        psum = self.psum
        with ExitStack() as st:
            sb = lambda name, shape, dt=F32: self.sb(st, "a1_" + name, shape, dt)
            self.norm_buffers(st, "a1", 2)
            NQ, NKV = H1 * HD1, 2 * G1 * HD1
            wkv = [sb(f"wkv_{x}", [P, KT * NKV], F32R) for x in ("hi", "lo")]
            wq = [sb(f"wq_{x}", [P, KT * NQ], F32R) for x in ("hi", "lo")]
            wd = [sb(f"wd_{x}", [P, H1 * D], F32R) for x in ("hi", "lo")]
            stage, stage_ring = sb("stage", [P, 2, 512]), Ring(sig, 2)
            mask = sb("mask", [P, S])
            kT, k_rings = sb("kT", [P, G1, 2, S], F32R), [Ring(sig, 1) for _ in range(G1)]
            v, v_ring = sb("v", [P, 2, TT, G1 * HD1]), Ring(sig, 2)
            q = sb("q", [P, 2, 2, S], F32R)
            q_ring = Ring(sig, 2)
            e, e_ring = sb("e", [P, 3, S]), Ring(sig, 3)
            et, et_ring = sb("et", [P, 2, TT, S]), Ring(sig, 2)
            nmax, rsum, rinv = sb("nmax", [P, 4, 1]), sb("rsum", [P, 4, 1]), sb("rinv", [P, 4, 1])
            small_ring = Ring(sig, 4)
            ctx, ctx_ring = sb("ctx", [P, 2, 2, S], F32R), Ring(sig, 2)
            oT, oT_ring = sb("oT", [P, KT, S]), Ring(sig, 1)

            s_banks, t_banks = Ring(sig, 2), Ring(sig, 2, 2)
            banks, o_banks = Ring(sig, 2, 4), Ring(sig, 2, 6)

            steps = Steps()
            h_of = self.h_of
            steps.at(-30, self.norm(0, 1, 0, banks))
            t_mask = self.load(mask[:, :], ins["mask"])
            t_kv = self.split_weights(stage, stage_ring, "a1", ins["w1_kv"], *wkv, 512)
            t_q = self.split_weights(stage, stage_ring, "a1", ins["w1_q"], *wq, 512)
            t_d = self.split_weights(stage, stage_ring, "a1", ins["w1_d"], *wd, 512)

            def pair(w_, a, e_):
                return w_[0][:, a:e_], w_[1][:, a:e_]

            k_of, v_of, q_of, o_of, et_of = {}, {}, {}, {}, {}

            def project_kv(b):
                while b not in h_of:
                    yield 1
                slot, h_ready = h_of[b][:2]
                for g in range(G1):
                    while not (banks.open() and k_rings[g].open()):
                        yield 1
                    n = banks.take(pe)
                    sig.wait(pe, *t_kv, *h_ready)
                    for k in range(KT):
                        mm = self.mm3(psum[:, n, :], pair(wkv, k * NKV + g * P, k * NKV + (g + 1) * P),
                                      self.h(slot, k), k == 0, k == KT - 1)
                        if k == 0:
                            yield 1
                    t = sig.done(mm, "pe_kv")
                    yield 1
                    k_rings[g].take(act, dve)
                    sig.wait(act, t)
                    t_hi = sig.done(act.activation(kT[:, g, 0, :], psum[:, n, :], ACT.Copy), "act_k_hi")
                    sig.wait(dve, t_hi)
                    t_lo = sig.done(dve.tensor_tensor(kT[:, g, 1, :], psum[:, n, :], kT[:, g, 0, :], ALU.subtract),
                                    "dve_k_lo")
                    banks.give(n, t_hi, t_lo)
                    k_of[b, g] = t_hi, t_lo
                while not v_ring.open():
                    yield 1
                y = v_ring.take(act)
                for t_ in range(TT):
                    while not banks.open():
                        yield 1
                    n = banks.take(pe)
                    for k in range(KT):
                        c = k * NKV + G1 * HD1
                        mm = self.mm3(psum[:, n, :], self.h(slot, k, slice(t_ * P, (t_ + 1) * P)),
                                      pair(wkv, c, c + G1 * HD1), k == 0, k == KT - 1)
                        if k == 0:
                            yield 1
                    t = sig.done(mm, "pe_kv")
                    yield 1
                    sig.wait(act, t)
                    t = sig.done(act.activation(v[:, y, t_, :], psum[:, n, :], ACT.Copy), "act_v")
                    banks.give(n, t)
                v_of[b] = y, t

            def project_q(b, h):
                while not (b in h_of and banks.open() and q_ring.open()):
                    yield 1
                slot, h_ready = h_of[b][:2]
                n = banks.take(pe)
                sig.wait(pe, *t_q[h // 2 * 2:h // 2 * 2 + 2], *h_ready)
                for k in range(KT):
                    c = (h * KT + k) * P
                    mm = self.mm3(psum[:, n, :], pair(wq, c, c + P), self.h(slot, k), k == 0, k == KT - 1)
                    if k == 0:
                        yield 1
                t = sig.done(mm, "pe_q")
                if h == H1 - 1:
                    self.h_ring.give(slot, t, ("pe_kv", sig.count["pe_kv"]))
                yield 1
                i = q_ring.take(act, dve)
                sig.wait(act, t)
                t_hi = sig.done(act.activation(q[:, i, 0, :], psum[:, n, :], ACT.Copy, scale=-SCALE1), "act_q_hi")
                sig.wait(dve, t_hi)
                t_lo = sig.done(dve.scalar_tensor_tensor(q[:, i, 1, :], psum[:, n, :], -SCALE1, q[:, i, 0, :],
                                                         ALU.mult, ALU.subtract), "dve_q_lo")
                banks.give(n, t_hi, t_lo)
                q_of[b, h] = i, (t_hi, t_lo)

            def unit(u):
                b, h, qt = u // (H1 * TT), u // TT % H1, u % TT
                g, W = h // HPG1, (qt + 1) * P
                while not ((b, h) in q_of and (b, g) in k_of and s_banks.open()):
                    yield 1
                i, ready = q_of[b, h]
                n = s_banks.take(pe)
                sig.wait(pe, *ready, *k_of[b, g])
                mm = self.mm3(psum[:, n, 0:W], (q[:, i, 0, qt * P:W], q[:, i, 1, qt * P:W]),
                              (kT[:, g, 0, 0:W], kT[:, g, 1, 0:W]), True, True)
                t = sig.done(mm, "pe_s")
                if qt == TT - 1:
                    q_ring.give(i, t)
                    if h % HPG1 == HPG1 - 1:
                        k_rings[g].give(0, t)
                yield 1
                while not small_ring.open():
                    yield 1
                m = small_ring.take(dve, act)
                sig.wait(dve, t, t_mask)
                t = sig.done(dve.tensor_tensor_reduce(psum[:, n, 0:W], psum[:, n, 0:W], mask[:, S - W:S], 1.0, BIG,
                                                      ALU.add, ALU.min, nmax[:, m, :]), "dve_max")
                while not e_ring.open():
                    yield 1
                x = e_ring.take(act)
                sig.wait(act, t)
                t = sig.done(act.activation(e[:, x, 0:W], psum[:, n, 0:W], ACT.Exp, bias=nmax[:, m, :], scale=-1.0,
                                            accum_out=rsum[:, m, :]), "act_e")
                s_banks.give(n, t)
                yield 1
                sig.wait(dve, t)
                t = sig.done(dve.reciprocal(rinv[:, m, :], rsum[:, m, :]), "dve_rinv")
                sig.wait(dve, t)
                t = sig.done(dve.tensor_scalar(e[:, x, 0:W], e[:, x, 0:W], rinv[:, m, 0:1], None, ALU.mult),
                             "dve_norm")
                small_ring.give(m, t)
                yield 1
                while not t_banks.open():
                    yield 1
                n = t_banks.take(pe)
                sig.wait(pe, t)
                for k in range(qt + 1):
                    mm = pe.transpose(psum[:, n, k * P:(k + 1) * P], e[:, x, k * P:(k + 1) * P], self.ident[:, :])
                t = sig.done(mm, "pe_turn")
                e_ring.give(x, t)
                yield 1
                if qt == 0:
                    while not et_ring.open():
                        yield 1
                    et_of[b, h] = [et_ring.take(act), []]
                while (b, h) not in et_of:
                    yield 1
                i, ready = et_of[b, h]
                sig.wait(act, t)
                t = sig.done(act.activation(et[:, i, 0:qt + 1, qt * P:W],
                                            psum[:, n, 0:W].rearrange("p (k q) -> p k q", q=P), ACT.Copy), "act_et")
                t_banks.give(n, t)
                ready.append(t)

            def context(b, h):
                g = h // HPG1
                while not ((b, h) in et_of and len(et_of[b, h][1]) == TT and b in v_of and banks.open()):
                    yield 1
                i, ready = et_of[b, h]
                y, t_v = v_of[b]
                n = banks.take(pe)
                sig.wait(pe, *ready, t_v)
                for k in range(TT):
                    mm = pe.matmul(psum[:, n, k * P:S], v[:, y, k, g * HD1:(g + 1) * HD1], et[:, i, k, k * P:S],
                                   start=(k == 0), stop=(k == TT - 1), skip_group_check=True)
                    if k < TT - 2:
                        yield 1
                t = sig.done(mm, "pe_pv")
                if h == H1 - 1:
                    v_ring.give(y, t)
                et_ring.give(i, t)
                yield 1
                while not ctx_ring.open():
                    yield 1
                j = ctx_ring.take(act, dve)
                sig.wait(act, t)
                t_hi = sig.done(act.activation(ctx[:, j, 0, :], psum[:, n, :], ACT.Copy), "act_ctx_hi")
                sig.wait(dve, t_hi)
                t_lo = sig.done(dve.tensor_tensor(ctx[:, j, 1, :], psum[:, n, :], ctx[:, j, 0, :], ALU.subtract),
                                "dve_ctx_lo")
                banks.give(n, t_hi, t_lo)
                yield 1
                if h == 0:
                    while not o_banks.open(KT):
                        yield 1
                    o_of[b] = [o_banks.take(pe) for _ in range(KT)]
                sig.wait(pe, t_hi, t_lo, *t_d)
                for m in range(KT):
                    c = h * D + m * P
                    mm = self.mm3(psum[:, o_of[b][m], :], pair(wd, c, c + P), (ctx[:, j, 0, :], ctx[:, j, 1, :]),
                                  h == 0, h == H1 - 1)
                    if m < KT - 1:
                        yield 1
                t = sig.done(mm, "pe_o")
                ctx_ring.give(j, t)
                if h == H1 - 1:
                    while not oT_ring.open():
                        yield 1
                    y = oT_ring.take(dve)
                    ready = []
                    for m in range(KT):
                        sig.wait(dve, t)
                        t_o = sig.done(dve.tensor_scalar(oT[:, m, :], psum[:, o_of[b][m], :],
                                                         self.gate[1][:, 0, m, b:b + 1], None, ALU.mult), "dve_o")
                        o_banks.give(o_of[b][m], t_o)
                        ready.append(t_o)
                    yield 1
                    yield from self.residual(b, oT, oT_ring, y, ready, banks)

            U = H1 * TT
            for b in range(B):
                base = U * b
                if b:
                    steps.at(base - 45, self.norm(b, 1, 0, banks))
                steps.at(base - 18, project_kv(b))
                for h in range(H1):
                    steps.at(base + TT * h - 6, project_q(b, h))
                    steps.at(base + TT * (h + 1) + 3, context(b, h))
            for u in range(B * U):
                steps.at(u, unit(u))
            steps.run()

    def experts(self, l, n_exp, picked, n_tiles, n_routed, last):
        sig, ins, pe, dve, act, pool = self.sig, self.ins, self.pe, self.dve, self.act, self.pool
        psum = self.psum
        with ExitStack() as st:
            sb = lambda name, shape, dt=F32: self.sb(st, f"m{l}_" + name, shape, dt)
            self.norm_buffers(st, f"m{l}", B)
            NS = 3
            WC = 2 * KT * P + D
            w32, w_ring = sb("w32", [P, NS, WC]), Ring(sig, NS)
            wh, wl, wh_ring = sb("wh", [P, NS, WC], F32R), sb("wl", [P, NS, WC], F32R), Ring(sig, NS)
            gate_w = sb("gate_w", [P, KT, n_exp])
            sel32 = sb("sel32", [2 * LO_ROW, n_routed * P])
            sel = sb("sel", [2 * LO_ROW, n_routed * P], F32R)
            combT = sb("combT", [2 * LO_ROW, B * S], F32R)
            silu, silu_ring = sb("silu", [P, 2, S]), Ring(sig, 2)
            up, up_ring = sb("up", [P, 2, S]), Ring(sig, 2)
            hid32, hid32_ring = sb("hid32", [P, 3, S]), Ring(sig, 3)
            hid, hid_ring = sb("hid", [P, 3, 2, S], F32R), Ring(sig, 3)
            yT, yT_ring = sb("yT", [P, KT, S]), Ring(sig, 1)
            y_rings = [Ring(sig, 1) for _ in range(2)]
            rt = sb("router", [P, 5, TT, n_exp])
            small = sb("router_small", [P, 3, TT])
            top = sb("top8", [P, TT, 8])
            rt_ring = Ring(sig, 1)

            banks, y_bank = Ring(sig, 4), 4
            t_gw = self.load(gate_w[:, :, :], ins[f"router{l}"])
            t_s = self.load(sel32[:, :], ins[f"sel{l}"])
            sig.wait(act, t_s)
            t_sel = sig.done(act.activation(sel[:, :], sel32[:, :], ACT.Copy), "act_sel")
            t_z = sig.done(pool.memset(combT[:, :].bitcast(F32), 0.0), "pool_combz")

            comb_ready, h_of, w_of, hid_of, y_ready = {}, self.h_of, {}, {}, {}

            def router(b):
                while b not in h_of or not banks.open() or not rt_ring.open():
                    yield 1
                _, _, t_h, s32 = h_of[b]
                n = banks.take(pe)
                sig.wait(pe, t_gw, t_h)
                for t_ in range(TT):
                    for k in range(KT):
                        mm = pe.matmul(psum[:, n, t_ * n_exp:(t_ + 1) * n_exp],
                                       self.h32[:, s32, k, t_ * P:(t_ + 1) * P],
                                       gate_w[:, k, :], start=(k == 0), stop=(k == KT - 1))
                t_l = sig.done(mm, "pe_logits")
                self.h32_ring.give(s32, t_l, *h_of[b][1])
                logits = psum[:, n, 0:TT * n_exp].rearrange("p (t e) -> p t e", e=n_exp)
                ex, scores, rest, comb = (rt[:, i] for i in range(4))
                nmax, total, inv = (small[:, i, :] for i in range(3))
                rt_ring.take(dve, act)
                sig.wait(dve, t_l)
                t = sig.done(dve.tensor_reduce(nmax, logits, AX.X, ALU.max, negate=True), "dve_router")
                sig.wait(act, t)
                for t_ in range(TT):
                    t = sig.done(act.activation(ex[:, t_, :], logits[:, t_, :], ACT.Exp, bias=nmax[:, t_:t_ + 1],
                                                accum_out=total[:, t_:t_ + 1]), "act_router")
                banks.give(n, t)
                yield 1
                sig.wait(dve, t)
                t = sig.done(dve.reciprocal(inv, total), "dve_router")
                sig.wait(dve, t)
                for t_ in range(TT):
                    t = sig.done(dve.tensor_scalar(scores[:, t_, :], ex[:, t_, :], inv[:, t_:t_ + 1], None, ALU.mult),
                                 "dve_router")
                sig.wait(dve, t)
                for t_ in range(TT):
                    t = sig.done(dve.max(top[:, t_, :], scores[:, t_, :]), "dve_router")
                sig.wait(dve, t)
                t = sig.done(dve.memset(top[:, :, picked:8], -1.0), "dve_router")
                sig.wait(dve, t)
                for t_ in range(TT):
                    t = sig.done(dve.match_replace(out=rest[:, t_, :], in_to_replace=top[:, t_, :],
                                                   in_values=scores[:, t_, :], imm_value=0.0), "dve_router")
                sig.wait(dve, t)
                t = sig.done(dve.tensor_tensor(comb, scores, rest, ALU.subtract), "dve_router")
                yield 1
                while not banks.open():
                    yield 1
                n = banks.take(pe)
                sig.wait(pe, t)
                for t_ in range(TT):
                    mm = pe.transpose(psum[0:n_exp, n, t_ * P:(t_ + 1) * P], comb[:, t_, :], self.ident[:, :])
                t = sig.done(mm, "pe_combT")
                rt_ring.give(0, t)
                c = slice(b * S, (b + 1) * S)
                sig.wait(dve, t, t_z)
                t = sig.done(dve.tensor_copy(combT[0:n_exp, c], psum[0:n_exp, n, :]), "dve_combT")
                sig.wait(dve, t)
                t = sig.done(dve.tensor_tensor(combT[LO_ROW:LO_ROW + n_exp, c], psum[0:n_exp, n, :],
                                               combT[0:n_exp, c], ALU.subtract), "dve_combT")
                banks.give(n, t)
                comb_ready[b] = t

            def weights(n):
                while not w_ring.open():
                    yield 1
                s = w_ring.take(self.sp)
                t = self.load(w32[:, s, :], ins[f"experts{l}"][n % n_tiles], name=f"load_m{l}_w{s}")
                yield 1
                while not wh_ring.open():
                    yield 1
                i = wh_ring.take(act, pool)
                two = self.split(wh[:, i, :], wl[:, i, :], w32[:, s, :], [t], "w")
                w_ring.give(s, *two)
                w_of[n] = i, two

            def wpart(i, c, width=P):
                return wh[:, i, c:c + width], wl[:, i, c:c + width]

            def place(u):
                return u // (2 * n_tiles), u // 2 % n_tiles, u % 2

            def hidden(u):
                half, tile, c = place(u)
                b = 2 * half + c
                while not (b in comb_ready and u // 2 in w_of and banks.open(3)):
                    yield 1
                slot, h_ready = h_of[b][:2]
                i, t_w = w_of[u // 2]
                out = []
                for part in range(2):
                    n = banks.take(pe)
                    sig.wait(pe, *t_w, *h_ready)
                    for k in range(KT):
                        mm = self.mm3(psum[:, n, :], wpart(i, (part * KT + k) * P), self.h(slot, k),
                                      k == 0, k == KT - 1)
                    out.append((n, sig.done(mm, "pe_gu")))
                x = silu_ring.take(act)
                sig.wait(act, out[0][1])
                t_s = sig.done(act.activation(silu[:, x, :], psum[:, out[0][0], :], ACT.Silu), "act_silu")
                banks.give(out[0][0], t_s)
                y = hid32_ring.take(dve)
                sig.wait(dve, t_s, out[1][1])
                if tile < n_routed:
                    z = up_ring.take(dve)
                    t = sig.done(dve.tensor_tensor(up[:, z, :], psum[:, out[1][0], :], silu[:, x, :], ALU.mult),
                                 "dve_up")
                    banks.give(out[1][0], t)
                    silu_ring.give(x, t)
                    n = banks.take(pe)
                    sig.wait(pe, comb_ready[b], t_sel)
                    mm = pe.matmul(psum[:, n, :], sel[:, tile * P:(tile + 1) * P], combT[:, b * S:(b + 1) * S],
                                   start=True, stop=True)
                    t_c = sig.done(mm, "pe_comb")
                    sig.wait(dve, t, t_c)
                    t = sig.done(dve.tensor_tensor(hid32[:, y, :], psum[:, n, :], up[:, z, :], ALU.mult), "dve_hid")
                    banks.give(n, t)
                    up_ring.give(z, t)
                else:
                    t = sig.done(dve.tensor_tensor(hid32[:, y, :], psum[:, out[1][0], :], silu[:, x, :], ALU.mult),
                                 "dve_hid")
                    banks.give(out[1][0], t)
                    silu_ring.give(x, t)
                f = hid_ring.take(act, pool)
                ready = self.split(hid[:, f, 0, :], hid[:, f, 1, :], hid32[:, y, :], [t], "hid")
                hid32_ring.give(y, *ready)
                yield DOWN_LAG
                sig.wait(pe, *ready)
                if tile == 0:
                    while not y_rings[c].open():
                        yield 1
                    y_rings[c].take(pe)
                for m in range(KT):
                    mm = self.mm3(psum[:, y_bank + 2 * c + m, :], wpart(i, 2 * KT * P + m * P),
                                  (hid[:, f, 0, :], hid[:, f, 1, :]), tile == 0, tile == n_tiles - 1)
                t = sig.done(mm, "pe_down")
                hid_ring.give(f, t)
                if c == 1:
                    wh_ring.give(i, t)
                if tile == n_tiles - 1:
                    yield 1
                    while not yT_ring.open():
                        yield 1
                    y = yT_ring.take(dve)
                    ready = []
                    sig.wait(dve, t)
                    for m in range(KT):
                        t = sig.done(dve.tensor_scalar(yT[:, m, :], psum[:, y_bank + 2 * c + m, :],
                                                       self.gate[l][:, 1, m, b:b + 1], None, ALU.mult), "dve_y")
                        ready.append(t)
                    y_rings[c].give(0, t)
                    yield from self.residual(b, yT, yT_ring, y, ready, banks, store=last)

            steps = Steps()
            for b, at in enumerate((-40, -30, 4, 12)):
                steps.at(at, self.norm(b, l, 1, banks, spread=False))
                steps.at(at + 8, router(b))
            for n in range(2 * n_tiles):
                steps.at(2 * n - 4, weights(n))
                for c in range(2):
                    steps.at(2 * n + c, hidden(2 * n + c))
            steps.run()


def adaln_program(nc, ins, out):
    with ExitStack() as stack:
        p = Program(nc, ins, out, stack)
        p.setup(stack)
        p.modulation(0)
        p.phase_barrier()
        p.modulation(1)
        p.phase_barrier()
        p.attention0()
        p.phase_barrier()
        p.experts(0, E0, K0, TILES0, TILES0_R, last=False)
        p.phase_barrier()
        p.attention1()
        p.phase_barrier()
        p.experts(1, E1, K1, TILES1, TILES1_R, last=True)
        p.sig.everything(p.sp)


def rope_table():
    theta = np.float32(10000.0) ** (-np.arange(0, HD0, 2, dtype=np.float32) / np.float32(HD0))
    freqs = np.arange(S, dtype=np.float32)[None, :] * theta.astype(np.float32)[:, None]
    table = np.zeros((P // HD0, HD0, 2, S), np.float32)
    table[:, :HD0 // 2, 0] = np.cos(freqs)
    table[:, :HD0 // 2, 1] = -np.sin(freqs)
    table[:, HD0 // 2:, 0] = 1.0
    return table.reshape(P, 2, S)


def stack_selectors():
    sel = np.zeros((P, 4, 4, P), np.float32)
    places = ((0, 1), (2, 3), (0, 2), (1, 3))
    for kind, where in enumerate(places):
        value = HD0 ** -0.5 if kind < 2 else 1.0
        for pair in range(4):
            for hh in range(2):
                for i in range(HD0):
                    for w in where:
                        sel[(2 * pair + hh) * HD0 + i, kind, pair, hh * STACK + w * HD0 + i] = value
    return sel.reshape(P, -1)


def expert_selector(n_exp, hidden, n_tiles):
    sel = np.zeros((2 * LO_ROW, n_tiles * P), np.float32)
    unit = np.arange(n_tiles * P)
    sel[unit // hidden, unit] = 1.0
    sel[LO_ROW + unit // hidden, unit] = 1.0
    return sel


def causal_mask():
    mask = np.zeros((P, S), np.float32)
    mask[:, S - P:] = np.where(np.arange(P)[:, None] >= np.arange(P)[None, :], 0.0, BIG)
    return mask


def k_tiles(w):
    k, n = w.shape
    return w.reshape(k // P, P, n).transpose(1, 0, 2).reshape(P, -1)


def pack_tiles(gate, up, down):
    n = -(-gate.shape[1] // P)
    pad = n * P - gate.shape[1]
    gate, up = (np.pad(a, ((0, 0), (0, pad))).reshape(KT, P, n, P).transpose(2, 1, 0, 3) for a in (gate, up))
    down = np.pad(down, ((0, pad), (0, 0))).reshape(n, P, D)
    return np.concatenate([gate.reshape(n, P, -1), up.reshape(n, P, -1), down], axis=2)


def lay_out(a):
    heads = np.arange(D).reshape(H0, HD0)
    even, odd = heads[:, ::2], heads[:, 1::2]
    value = np.concatenate([even, odd], axis=1).reshape(-1)
    partner = np.concatenate([odd, even], axis=1).reshape(-1)
    wq, wk, wv, wo = (a[f"L0_attn_w{x}"] for x in "qkvo")
    w0 = np.concatenate([w.T[:, o] for w in (wq, wk) for o in (value, partner)] + [wv.T], axis=1)
    b0 = np.concatenate([a[f"L0_attn_b{x}"][o].reshape(2, P) for x in "qk" for o in (value, partner)]).T
    wo_rows = np.zeros((H0, 32, D), np.float32)
    wo_rows[:, :HD0] = wo.T.reshape(H0, HD0, D)
    wq1 = a["L1_attn_w_q"].reshape(KT, P, H1, HD1).transpose(1, 2, 0, 3).reshape(P, -1)
    flat = lambda w: w.transpose(1, 0, 2).reshape(w.shape[1], -1)
    w1, w2, w3 = (a[f"L1_ffn_w{i}"] for i in (1, 2, 3))
    ffn0 = pack_tiles(
        np.concatenate([flat(a["L0_ffn_w_gate"]), a["L0_ffn_sw_gate"]], axis=1),
        np.concatenate([flat(a["L0_ffn_w_up"]), a["L0_ffn_sw_up"]], axis=1),
        np.concatenate([a["L0_ffn_w_down"].reshape(-1, D), a["L0_ffn_sw_down"]], axis=0))
    ffn1 = pack_tiles(
        np.concatenate([w1.reshape(-1, D), a["L1_ffn_sw1"]], axis=0).T,
        np.concatenate([w3.reshape(-1, D), a["L1_ffn_sw3"]], axis=0).T,
        np.concatenate([w2.transpose(0, 2, 1).reshape(-1, D), a["L1_ffn_sw2"].T], axis=0))
    return {
        "x": a["L0_attn_x"],
        "ident": np.eye(P, dtype=np.float32),
        "c0": a["L0_c"].T.reshape(KT, P, B).transpose(1, 0, 2),
        "c1": a["L1_c"].T.reshape(KT, P, B).transpose(1, 0, 2),
        "wmod0": a["L0_wmod"], "wmod1": a["L1_wmod"],
        "w0_qkv": k_tiles(w0), "b0_qk": b0, "b0_v": a["L0_attn_bv"],
        "w0_o": k_tiles(wo_rows.reshape(-1, D)), "b0_o": a["L0_attn_bo"].reshape(KT, P).T,
        "rope": rope_table(), "stack_sel": stack_selectors(), "mask": causal_mask(),
        "w1_q": wq1, "w1_kv": k_tiles(a["L1_attn_w_kv"]), "w1_d": k_tiles(a["L1_attn_w_dense"]),
        "router0": a["L0_ffn_gate_w"].reshape(KT, P, E0).transpose(1, 0, 2),
        "router1": a["L1_ffn_gate_w"].T.reshape(KT, P, E1).transpose(1, 0, 2),
        "sel0": expert_selector(E0, HID0, TILES0_R), "sel1": expert_selector(E1, HID1, TILES1_R),
        "experts0": ffn0, "experts1": ffn1,
    }


def kernel(**inputs):
    import concourse.bacc as bacc
    from concourse.bass_utils import run_bass_kernel_spmd

    nc = bacc.Bacc("TRN2", target_bir_lowering=False, num_devices=1)
    laid = lay_out({k: np.asarray(v) for k, v in inputs.items()})
    arrays, aps = {}, {}
    for name, a in laid.items():
        arrays[f"in_{name}"] = a = np.ascontiguousarray(a)
        aps[name] = nc.dram_tensor(f"in_{name}", a.shape, mybir.dt.from_np(a.dtype), kind="ExternalInput").ap()
    out = nc.dram_tensor("out_0_dram", (B, S, D), F32, kind="ExternalOutput").ap()
    adaln_program(nc, aps, out)
    r = run_bass_kernel_spmd(nc, [arrays], core_ids=[0])
    return r.results[0]["out_0_dram"]
```

```python
from contextlib import ExitStack

import numpy as np

import concourse.bass as bass
from concourse import mybir

ALU = mybir.AluOpType
ACT = mybir.ActivationFunctionType
AX = mybir.AxisListType
F32 = mybir.dt.float32
F32R = mybir.dt.float32r
I32 = mybir.dt.int32
U32 = mybir.dt.uint32

P = 128
B, S, D = 4, 512, 256
KT = D // P
TT = S // P
NT = B * TT
LN_EPS = 1e-5
BIG = 3.0e38

H0, HD0 = 16, 16
GROUP0 = 4
STACK = 64
H1, G1, HD1 = 16, 4, 128
HPG1 = H1 // G1
SCALE1 = HD1 ** -0.5
E0, K0, HID0 = 8, 2, 176
E1, K1, HID1 = 32, 4, 128
SHARED = 2
ROW = D + 2


def slot_tiles(n_exp, picked):
    return NT * picked + n_exp - 1


class Signals:

    def __init__(self, nc, stack):
        self.nc, self.stack = nc, stack
        self.sems, self.count, self.passed = {}, {}, {}

    def done(self, instruction, name, by=1):
        if name not in self.sems:
            self.sems[name] = self.stack.enter_context(self.nc.semaphore(name))
            self.count[name] = 0
        instruction.then_inc(self.sems[name], by)
        self.count[name] += by
        return name, self.count[name]

    def wait(self, engine, *values):
        for value in values:
            if value is None:
                continue
            name, count = value
            key = (str(engine.engine), name)
            if self.passed.get(key, 0) < count:
                engine.wait_ge(self.sems[name], count)
                self.passed[key] = count

    def everything(self, engine):
        self.wait(engine, *self.count.items())


class Ring:

    def __init__(self, signals, n, first=0):
        self.signals, self.n, self.first, self.turn = signals, n, first, 0
        self.freed = [()] * n

    def open(self, k=1):
        return all(self.freed[(self.turn + j) % self.n] is not None for j in range(k))

    def take(self, *engines):
        assert self.open(), "a buffer is taken before it was given back"
        i = self.turn % self.n
        self.turn += 1
        for engine in engines:
            self.signals.wait(engine, *self.freed[i])
        self.freed[i] = None
        return i + self.first

    def give(self, i, *values):
        self.freed[i - self.first] = values


class Steps:

    def __init__(self):
        self.due, self.n = {}, 0

    def at(self, step, task):
        self.n += 1
        self.due.setdefault(step, []).append((step, self.n, task))

    def run(self):
        while self.due:
            step = min(self.due)
            for start, n, task in sorted(self.due.pop(step), key=lambda x: x[:2]):
                pause = next(task, None)
                if pause is not None:
                    self.due.setdefault(step + pause, []).append((start, n, task))


class Program:
    def __init__(self, nc, ins, out, stack):
        self.nc, self.ins, self.out = nc, ins, out
        self.pe, self.dve, self.act, self.pool, self.sp = nc.tensor, nc.vector, nc.scalar, nc.gpsimd, nc.sync
        self.sig = Signals(nc, stack)
        self.stack = stack
        self.psum = stack.enter_context(nc.psum_tensor("psum", [P, 8, 512], F32))
        self.n_loads = 0

    def sb(self, stack, name, shape, dtype=F32):
        return stack.enter_context(self.nc.sbuf_tensor(name, shape, dtype))

    def load(self, dst, src, *waits, name=None, queue=None):
        queue = queue or self.sp
        self.sig.wait(queue, *waits)
        self.n_loads += 1
        return self.sig.done(queue.dma_start(dst, src), name or f"load{self.n_loads}", 16)

    def mm3(self, out, lhs, rhs, start, stop):
        (lh, ll), (rh, rl) = lhs, rhs
        self.pe.matmul(out, lh, rh, start=start, stop=False, skip_group_check=True)
        self.pe.matmul(out, lh, rl, start=False, stop=False, skip_group_check=True)
        return self.pe.matmul(out, ll, rh, start=False, stop=stop, skip_group_check=True)

    def split(self, hi, lo, src, ready, name):
        sig = self.sig
        sig.wait(self.act, *ready)
        t_hi = sig.done(self.act.activation(hi, src, ACT.Copy), f"act_{name}_hi")
        sig.wait(self.pool, *ready, t_hi)
        t_lo = sig.done(self.pool.tensor_tensor(lo, src, hi, ALU.subtract), f"pool_{name}_lo")
        return t_hi, t_lo

    def phase_barrier(self):
        for engine in (self.pe, self.dve, self.act, self.pool, self.sp):
            self.sig.everything(engine)

    def setup(self, stack):
        sig, ins = self.sig, self.ins
        self.x = self.sb(stack, "x_nat", [P, NT, D])
        self.ident = self.sb(stack, "ident", [P, P])
        self.mod = [self.sb(stack, f"mod{l}", [P, 12, B]) for l in range(2)]
        self.gate = [self.sb(stack, f"gate{l}", [P, 2, KT, B]) for l in range(2)]
        self.stats = self.sb(stack, "ln_stats", [P, NT, 6])
        self.mv = self.sb(stack, "ln_mean_var", [P, NT, 2])
        self.lnw = self.sb(stack, "ln_work", [P, 5, NT])
        self.eps = self.sb(stack, "eps", [P, 1])
        self.c = self.sb(stack, "c", [P, 2, KT, B])
        self.silu_c = self.sb(stack, "silu_c", [P, 2, KT, B])
        self.gate_work = self.sb(stack, "gate_work", [P, 2, 3, 2, KT, B])
        self.t_mod = {}
        self.x_ready = {}
        self.load_x(0, self.act)
        self.t_ident = self.load(self.ident[:, :], ins["ident"], queue=self.act)
        self.t_eps = sig.done(self.pool.memset(self.eps[:, :], LN_EPS), "pool_eps")
        self.ln_ring = Ring(sig, 1)

    def load_x(self, b, queue):
        tiles = slice(b * TT, (b + 1) * TT)
        t = self.load(self.x[:, tiles, :], self.ins["x"].rearrange("b (t p) d -> p (b t) d", p=P)[:, tiles, :],
                      queue=queue)
        self.x_ready.update({b * TT + i: t for i in range(TT)})

    def modulation(self, l, w, banks):
        sig, ins, c, sc, work = self.sig, self.ins, self.c, self.silu_c, self.gate_work
        t_c = self.load(c[:, l], ins[f"c{l}"])
        t_w = self.load(w, ins[f"wmod{l}"].rearrange("(k p) n -> p k n", p=P))
        sig.wait(self.act, t_c)
        t_sc = sig.done(self.act.activation(sc[:, l], c[:, l], ACT.Silu), "act_silu_c")
        bank = banks.take(self.pe)
        sig.wait(self.pe, t_sc, t_w)
        ps = self.psum[:, bank, 0:12 * B].rearrange("p (m b) -> p m b", b=B)
        for m in range(12):
            for k in range(KT):
                mm = self.pe.matmul(ps[:, m, :], w[:, k, m * P:(m + 1) * P], sc[:, l, k, :],
                                    start=(k == 0), stop=(k == KT - 1))
        t_mm = sig.done(mm, "pe_mod")
        mod = self.mod[l]
        sig.wait(self.dve, t_mm)
        t = sig.done(self.dve.tensor_copy(mod[:, :, :], ps), "dve_mod")
        banks.give(bank, t)
        sig.wait(self.dve, t)
        for j in (1, 4):
            v = mod[:, 2 * j:2 * j + 2, :]
            t = sig.done(self.dve.tensor_scalar(v, v, 1.0, None, ALU.add), "dve_mod")
        for n, j in enumerate((2, 5)):
            g = mod[:, 2 * j:2 * j + 2, :]
            neg, sign, mag = (work[:, l, i, n] for i in range(3))
            t1 = sig.done(self.dve.tensor_scalar(neg, g, -1.0, None, ALU.mult), "dve_mod")
            t2 = sig.done(self.dve.tensor_scalar(sign, g, 0.0, 2.0, ALU.is_ge, ALU.mult), "dve_mod")
            sig.wait(self.dve, t1)
            t3 = sig.done(self.dve.tensor_tensor(mag, g, neg, ALU.max), "dve_mod")
            sig.wait(self.dve, t3)
            t4 = sig.done(self.dve.tensor_scalar(neg, mag, 0.25, None, ALU.max), "dve_mod")
            sig.wait(self.dve, t2, t4)
            t = sig.done(self.dve.scalar_tensor_tensor(self.gate[l][:, n], sign, -1.0, neg, ALU.add, ALU.mult),
                         "dve_mod")
        self.t_mod[l] = t
        return t_mm

    def norm_buffers(self, stack, tag, n_h, n_32=1):
        self.xn = self.sb(stack, f"xn_{tag}", [P, 2, D])
        self.xn_ring = Ring(self.sig, 2)
        self.h32, self.h32_ring = self.sb(stack, f"h32_{tag}", [P, n_32, KT, S]), Ring(self.sig, n_32)
        self.h_of = {}
        if not n_h:
            return
        self.hh = self.sb(stack, f"h_hi_{tag}", [P, n_h, KT, S], F32R)
        self.hl = self.sb(stack, f"h_lo_{tag}", [P, n_h, KT, S], F32R)
        self.h_ring = Ring(self.sig, n_h)

    def statistics(self, tiles):
        sig, dve, act, n = self.sig, self.dve, self.act, len(tiles)
        while not (all(tile in self.x_ready for tile in tiles) and self.ln_ring.open()):
            yield 1
        self.ln_ring.take(dve, act)
        for i, tile in enumerate(tiles):
            sig.wait(dve, self.x_ready[tile])
            d = sig.done(dve.bn_stats(self.stats[:, i, :], self.x[:, tile, :]), "dve_stats")
        sig.wait(dve, d)
        for i in range(n):
            d = sig.done(dve.bn_aggr(self.mv[:, i, :], self.stats[:, i, :]), "dve_stats")
        var, mean = self.mv[:, 0:n, 1], self.mv[:, 0:n, 0]
        sd, r, a, c, rstd = (self.lnw[:, i, 0:n] for i in range(5))
        yield 1
        sig.wait(act, d, self.t_eps)
        d = sig.done(act.activation(sd, var, ACT.Sqrt, bias=self.eps[:, 0:1]), "act_sd")
        yield 1
        sig.wait(dve, d)
        d = sig.done(dve.reciprocal(r, sd), "dve_rstd")
        sig.wait(dve, d)
        d = sig.done(dve.scalar_tensor_tensor(a, var, LN_EPS, r, ALU.add, ALU.mult), "dve_rstd")
        sig.wait(dve, d)
        d = sig.done(dve.tensor_tensor(c, a, r, ALU.mult), "dve_rstd")
        sig.wait(dve, d)
        d = sig.done(dve.tensor_scalar(a, c, -0.5, 1.5, ALU.mult, ALU.add), "dve_rstd")
        sig.wait(dve, d)
        d = sig.done(dve.tensor_tensor(rstd, a, r, ALU.mult), "dve_rstd")
        self.moments = mean, rstd, d

    def norm(self, b, l, which, banks, together=False):
        sig, dve, act, pe = self.sig, self.dve, self.act, self.pe
        if together:
            while self.moments is None:
                yield 1
        else:
            yield from self.statistics(range(b * TT, (b + 1) * TT))
        mean, rstd, d = self.moments
        first = b * TT if together else 0
        sig.wait(dve, d, self.t_mod[l])
        while not (banks.open(KT) and self.h32_ring.open() and (which or self.h_ring.open())):
            yield 1
        bank = [banks.take(pe) for _ in range(KT)]
        sig.wait(pe, self.t_ident)
        for t in range(TT):
            n = self.xn_ring.take(dve)
            d = sig.done(dve.tensor_scalar(self.xn[:, n, :], self.x[:, b * TT + t, :],
                                           mean[:, first + t:first + t + 1], rstd[:, first + t:first + t + 1],
                                           ALU.subtract, ALU.mult), "dve_xn")
            sig.wait(pe, d)
            for k in range(KT):
                mm = pe.transpose(self.psum[:, bank[k], t * P:(t + 1) * P], self.xn[:, n, k * P:(k + 1) * P],
                                  self.ident[:, :])
            t_xT = sig.done(mm, "pe_xT")
            self.xn_ring.give(n, t_xT)
            if t < TT - 1 and not together:
                yield 1
        if b == B - 1 or not together:
            self.ln_ring.give(0, d)
        if not together:
            yield 1
        slot = None if which else self.h_ring.take(act, self.pool)
        s32 = self.h32_ring.take(dve)
        sig.wait(dve, t_xT)
        j = 3 * which
        mod = self.mod[l]
        ready = []
        for k in range(KT):
            t_h = sig.done(dve.tensor_scalar(self.h32[:, s32, k, :], self.psum[:, bank[k], :],
                                             mod[:, 2 * (j + 1) + k, b:b + 1], mod[:, 2 * j + k, b:b + 1],
                                             ALU.mult, ALU.add), "dve_h")
            banks.give(bank[k], t_h)
            if not which:
                ready += self.split(self.hh[:, slot, k, :], self.hl[:, slot, k, :], self.h32[:, s32, k, :], [t_h],
                                    "h")
        if not which:
            self.h32_ring.give(s32, *ready)
        self.h_of[b] = slot, ready, t_h, s32

    def h(self, slot, k, cols=slice(0, S)):
        return self.hh[:, slot, k, cols], self.hl[:, slot, k, cols]

    def residual(self, b, yT, ring, slot, y_ready, banks):
        sig, pe, dve = self.sig, self.pe, self.dve
        tiles = [b * TT + t for t in range(TT)]
        before = [self.x_ready.pop(t) for t in tiles]
        for half in range(2):
            while not banks.open():
                yield 1
            n = banks.take(pe)
            sig.wait(pe, *y_ready)
            for t in range(TT // 2):
                tile = half * (TT // 2) + t
                for k in range(KT):
                    mm = pe.transpose(self.psum[:, n, t * D + k * P:t * D + (k + 1) * P],
                                      yT[:, k, tile * P:(tile + 1) * P], self.ident[:, :])
            t_T = sig.done(mm, "pe_yT")
            if half:
                ring.give(slot, t_T)
            yield 1
            lo = b * TT + half * (TT // 2)
            xs = self.x[:, lo:lo + TT // 2, :].rearrange("p t d -> p (t d)")
            sig.wait(dve, t_T, *before)
            t_x = sig.done(dve.tensor_tensor(xs, xs, self.psum[:, n, :], ALU.add), "dve_x")
            banks.give(n, t_x)
            for t in range(TT // 2):
                self.x_ready[lo + t] = t_x

    def split_weights(self, stage, ring, name, width, jobs, late=0):
        for number, (src, hi, lo, ready) in enumerate(jobs):
            for a in range(0, src.shape[1], width):
                c = slice(a, a + width)
                while not ring.open():
                    yield 1
                s = ring.take(self.sp)
                t = self.load(stage[:, s, :], src[:, c], name=f"stage_{name}{s}")
                if lo is None:
                    self.sig.wait(self.act, t)
                    done = [self.sig.done(self.act.activation(hi[:, c], stage[:, s, :], ACT.Copy), "act_w_hi")]
                else:
                    done = self.split(hi[:, c], lo[:, c], stage[:, s, :], [t], "w")
                ring.give(s, *done)
                ready += done
                yield 1 + (number >= late)

    def attention0(self):
        sig, ins, pe, dve, act, pool = self.sig, self.ins, self.pe, self.dve, self.act, self.pool
        psum = self.psum
        with ExitStack() as st:
            sb = lambda name, shape, dt=F32: self.sb(st, "a0_" + name, shape, dt)
            self.norm_buffers(st, "a0", 2)
            NW = 5 * D
            w_hi, w_lo = sb("w_hi", [P, KT * NW], F32R), sb("w_lo", [P, KT * NW], F32R)
            wo_hi, wo_lo = sb("wo_hi", [P, GROUP0 * D], F32R), sb("wo_lo", [P, GROUP0 * D], F32R)
            sel = sb("stack_sel", [P, 4, 4, P], F32R)
            rope = sb("rope", [P, 2, S])
            bias, bv, bo = sb("bias", [P, 8]), sb("bv", [P, D]), sb("bo", [P, KT])
            rp = sb("rope_tmp", [P, 3, S])
            rp_ring = Ring(sig, 1)
            qk = sb("qk", [P, 2, 2, 2, S], F32R)
            qk_ready, qk_ring = {}, {(i, m): Ring(sig, 1) for i in range(2) for m in range(2)}
            stk = sb("stk", [P, 2, 3, S], F32R)
            stk_ring = Ring(sig, 3)
            v, v_ring = sb("v", [P, 2, TT, H0, 32]), Ring(sig, 2)
            e, e_ring = sb("e", [P, 3, S]), Ring(sig, 3)
            NET = 5
            et, et_ring = sb("et", [P, NET, TT, S]), Ring(sig, NET)
            nmax, rsum = sb("nmax", [P, H0, TT]), sb("rsum", [P, H0, TT])
            rinv, rexp = sb("rinv", [P, GROUP0, TT]), sb("rexp", [P, TT, GROUP0, 32])
            rb, ctx32 = sb("rb", [P, S]), sb("ctx32", [P, S])
            rexp_ring, ctx32_ring, oT_ring = Ring(sig, 1), Ring(sig, 1), Ring(sig, 1)
            ctx_rings = [Ring(sig, 1) for _ in range(GROUP0)]
            ctx = sb("ctx", [P, 2, GROUP0, S], F32R)
            oT = sb("oT", [P, KT, S])

            s_banks, t_banks = Ring(sig, 3), Ring(sig, 2, 3)
            pv_banks, banks = Ring(sig, 1, 5), Ring(sig, 2, 6)

            steps = Steps()
            h_of = self.h_of
            steps.at(-32, self.norm(0, 0, 0, banks))
            wmod = et[:, 0:2].rearrange("p a t s -> p (a t s)")[:, 0:KT * 6 * D].rearrange("p (k n) -> p k n", k=KT)
            stage = et[:, 2:NET].rearrange("p a t s -> p (a t) s")
            stage_ring = Ring(sig, (NET - 2) * TT)
            for i in range(NET):
                et_ring.freed[i] = None

            def prepare():
                t_free = self.modulation(0, wmod, banks)
                et_ring.give(0, t_free)
                et_ring.give(1, t_free)
                yield from self.split_weights(stage, stage_ring, "a0", S, (
                    (ins["w0_qkv"], w_hi, w_lo, t_w),
                    (ins["stack_sel"], sel[:, :, :, :].rearrange("p a b c -> p (a b c)"), None, t_sel),
                    (ins["w0_o"], wo_hi, wo_lo, t_wo)), late=3)
                for i in range(2, NET):
                    et_ring.give(i, *t_w[-2:], t_sel[-1], *t_wo[-2:])
                for b in range(1, B):
                    self.load_x(b, self.sp)

            steps.at(8, self.fill_slots())
            t_w, t_sel, t_wo = [], [], []
            steps.at(-31, prepare())
            n_w, n_sel, n_wo = 2 * KT * NW // S, 16 * P // S, 2 * GROUP0 * D // S
            self.load(rope[:, :, :], ins["rope"], name="a0_small")
            self.load(bias[:, :], ins["b0_qk"], name="a0_small")
            self.load(bo[:, :], ins["b0_o"], name="a0_small")
            t_small = self.load(bv[:, :], ins["b0_v"].partition_broadcast(P), name="a0_small")
            t_vz = sig.done(pool.memset(v[:, :, :, :, :].rearrange("p a b c d -> p (a b c d)"), 0.0), "pool_vzero")

            def w(k, a, e_):
                return w_hi[:, k * NW + a:k * NW + e_], w_lo[:, k * NW + a:k * NW + e_]

            def project(b):
                while b not in h_of or len(t_w) < n_w:
                    yield 1
                slot, h_ready = h_of[b][:2]
                for m in range(2):
                    for i in range(2):
                        while not banks.open(2):
                            yield 1
                        two, pair = [], [banks.take(pe) for _ in range(2)]
                        for part, n in enumerate(pair):
                            sig.wait(pe, *t_w, *h_ready)
                            col = (2 * i + part) * D + m * P
                            for k in range(KT):
                                mm = self.mm3(psum[:, n, :], w(k, col, col + P), self.h(slot, k), k == 0,
                                              k == KT - 1)
                                if k == 0:
                                    yield 1
                            two.append((n, sig.done(mm, "pe_qk")))
                            yield 1
                        while not rp_ring.open():
                            yield 1
                        r = rp_ring.take(dve)
                        sig.wait(dve, t_small)
                        t_part = []
                        for part, (n, t) in enumerate(two):
                            sig.wait(dve, t)
                            c = 4 * i + 2 * part + m
                            t = sig.done(dve.scalar_tensor_tensor(rp[:, part, :], psum[:, n, :], bias[:, c:c + 1],
                                                                  rope[:, part, :], ALU.add, ALU.mult), "dve_rope")
                            banks.give(n, t)
                            t_part.append(t)
                        sig.wait(dve, *t_part)
                        t = sig.done(dve.tensor_tensor(rp[:, 2, :], rp[:, 0, :], rp[:, 1, :], ALU.add), "dve_rope")
                        yield 1
                        while not qk_ring[i, m].open():
                            yield 1
                        qk_ring[i, m].take(act, pool)
                        two = self.split(qk[:, i, m, 0, :], qk[:, i, m, 1, :], rp[:, 2, :], [t], "qk")
                        rp_ring.give(r, *two)
                        qk_ready[b, i, m] = two
                    if m == 0:
                        yield from project_v(b, slot, h_ready)
                self.h_ring.give(slot, ("pe_qk", sig.count["pe_qk"]), ("pe_v", sig.count["pe_v"]))

            def project_v(b, slot, h_ready):
                y = v_ring.take(dve)
                ready = []
                for t_ in range(TT):
                    while not banks.open():
                        yield 1
                    n = banks.take(pe)
                    sig.wait(pe, *t_w, *h_ready)
                    for k in range(KT):
                        mm = self.mm3(psum[:, n, 0:D], self.h(slot, k, slice(t_ * P, (t_ + 1) * P)),
                                      w(k, 4 * D, 5 * D), k == 0, k == KT - 1)
                    t = sig.done(mm, "pe_v")
                    yield 1
                    sig.wait(dve, t, t_small, t_vz)
                    t = sig.done(dve.tensor_tensor(v[:, y, t_, :, 0:HD0],
                                                   psum[:, n, 0:D].rearrange("p (h c) -> p h c", c=HD0),
                                                   bv[:, :].rearrange("p (h c) -> p h c", c=HD0), ALU.add), "dve_v")
                    banks.give(n, t)
                v_of[b] = y, t

            stk_of, v_of = {}, {}

            def stack_pair(b, pair):
                m, p = divmod(pair, 4)
                while not ((b, 1, m) in qk_ready and len(t_sel) == n_sel and stk_ring.open() and
                           banks.open(2)):
                    yield 1
                s = stk_ring.take(act)
                two = []
                for i in range(2):
                    n = banks.take(pe)
                    sig.wait(pe, *t_sel, *qk_ready[b, i, m])
                    for x in range(2):
                        mm = pe.matmul(psum[:, n, :], sel[:, 2 * i + x, p, :], qk[:, i, m, x, :],
                                       start=(x == 0), stop=(x == 1))
                    two.append((n, sig.done(mm, "pe_stack")))
                    if p == 3:
                        qk_ring[i, m].give(0, two[-1][1])
                yield 1
                ready = []
                for i, (n, t) in enumerate(two):
                    sig.wait(act, t)
                    t = sig.done(act.activation(stk[:, i, s, :], psum[:, n, :], ACT.Copy), "act_stack")
                    banks.give(n, t)
                    ready.append(t)
                stk_of[b, pair] = s, ready

            et_of, group_sums = {}, {}

            def unit(u):
                b, h, qt = u // (H0 * TT), u // TT % H0, u % TT
                g = h // GROUP0
                while (b, h // 2) not in stk_of or not s_banks.open():
                    yield 1
                s, ready = stk_of[b, h // 2]
                r0 = STACK * (h % 2)
                n = s_banks.take(pe)
                sig.wait(pe, *ready)
                mm = pe.matmul(psum[:, n, :], stk[r0:r0 + STACK, 0, s, qt * P:(qt + 1) * P],
                               stk[r0:r0 + STACK, 1, s, :], start=True, stop=True)
                t = sig.done(mm, "pe_s")
                if h % 2 and qt == TT - 1:
                    stk_ring.give(s, t)
                yield 1
                before = group_sums[b - 1, g] if b else None
                sig.wait(dve, t, before)
                t = sig.done(dve.tensor_reduce(nmax[:, h, qt:qt + 1], psum[:, n, :], AX.X, ALU.max, negate=True),
                             "dve_max")
                while not e_ring.open():
                    yield 1
                x = e_ring.take(act)
                sig.wait(act, t, before)
                t = sig.done(act.activation(e[:, x, :], psum[:, n, :], ACT.Exp, bias=nmax[:, h, qt:qt + 1],
                                            accum_out=rsum[:, h, qt:qt + 1]), "act_e")
                s_banks.give(n, t)
                yield 2
                while not t_banks.open():
                    yield 1
                n = t_banks.take(pe)
                sig.wait(pe, t, self.t_ident)
                for k in range(TT):
                    mm = pe.transpose(psum[:, n, k * P:(k + 1) * P], e[:, x, k * P:(k + 1) * P], self.ident[:, :])
                t_e, t = t, sig.done(mm, "pe_turn")
                e_ring.give(x, t)
                yield 1
                if qt == 0:
                    while not et_ring.open():
                        yield 1
                    et_of[b, h] = [et_ring.take(act, dve), []]
                while (b, h) not in et_of:
                    yield 1
                i, ready = et_of[b, h]
                dst = et[:, i, :, qt * P:(qt + 1) * P]
                src = psum[:, n, :].rearrange("p (k q) -> p k q", k=TT)
                if u % 5 in (1, 3):
                    sig.wait(act, t)
                    t = sig.done(act.activation(dst, src, ACT.Copy), "act_et")
                else:
                    sig.wait(dve, t)
                    t = sig.done(dve.tensor_copy(dst, src), "dve_et")
                t_banks.give(n, t)
                ready += [t, t_e]

            def context(b, g):
                heads = [(b, GROUP0 * g + j) for j in range(GROUP0)]
                while any(h not in et_of or len(et_of[h][1]) < 2 * TT for h in heads):
                    yield 1
                while not pv_banks.open():
                    yield 1
                n = pv_banks.take(pe)
                y, t_v = v_of[b]
                sig.wait(pe, t_v)
                for h in heads:
                    sig.wait(pe, *et_of[h][1])
                    sig.wait(dve, *et_of[h][1][1::2])
                t_r = sig.done(dve.reciprocal(rinv[:, :, :], rsum[:, GROUP0 * g:GROUP0 * (g + 1), :]), "dve_rinv")
                group_sums[b, g] = t_r
                for k in range(TT):
                    for j in range(GROUP0):
                        mm = pe.matmul(psum[32 * j:32 * j + 32, n, :], v[:, y, k, GROUP0 * g + j, :],
                                       et[:, et_of[heads[j]][0], k, :], start=(k == 0), stop=(k == TT - 1),
                                       tile_position=(0, 32 * j), skip_group_check=True)
                    if k < TT - 1:
                        yield 1
                t_pv = sig.done(mm, "pe_pv")
                if g == H0 // GROUP0 - 1:
                    v_ring.give(y, t_pv)
                for h in heads:
                    et_ring.give(et_of[h][0], t_pv)
                r = rexp_ring.take(pool)
                sig.wait(pool, t_r)
                t_x = sig.done(pool.tensor_copy(rexp[:, :, :, :], rinv[:, :, :].rearrange("p j t -> p t j")
                                                .unsqueeze(3).broadcast_to([P, TT, GROUP0, 32])), "pool_rexp")
                yield 2
                while not banks.open():
                    yield 1
                m = banks.take(pe)
                sig.wait(pe, t_x)
                for q in range(TT):
                    mm = pe.matmul(psum[:, m, q * P:(q + 1) * P], rexp[:, q].rearrange("p j i -> p (j i)"),
                                   self.ident[:, :], start=True, stop=True)
                t = sig.done(mm, "pe_rb")
                rexp_ring.give(r, t)
                yield 1
                c = ctx32_ring.take(act, dve)
                sig.wait(act, t)
                t = sig.done(act.activation(rb[:, :], psum[:, m, :], ACT.Copy), "act_rb")
                banks.give(m, t)
                yield 1
                sig.wait(dve, t, t_pv)
                t = sig.done(dve.tensor_tensor(ctx32[:, :], psum[:, n, :], rb[:, :], ALU.mult), "dve_ctx")
                pv_banks.give(n, t)
                yield 1
                while not ctx_rings[g].open():
                    yield 1
                ctx_rings[g].take(act, pool)
                two = self.split(ctx[:, 0, g, :], ctx[:, 1, g, :], ctx32[:, :], [t], "ctx")
                ctx32_ring.give(c, *two)
                ctx_ready[b, g] = two

            ctx_ready = {}

            def output(b):
                while (b, GROUP0 - 1) not in ctx_ready or len(t_wo) < n_wo or not oT_ring.open():
                    yield 1
                y = oT_ring.take(dve)
                ready = []
                for m in range(KT):
                    while not banks.open():
                        yield 1
                    n = banks.take(pe)
                    sig.wait(pe, *t_wo)
                    for g in range(GROUP0):
                        sig.wait(pe, *ctx_ready[b, g])
                        c = slice(g * D + m * P, g * D + (m + 1) * P)
                        mm = self.mm3(psum[:, n, :], (wo_hi[:, c], wo_lo[:, c]), (ctx[:, 0, g, :], ctx[:, 1, g, :]),
                                      g == 0, g == GROUP0 - 1)
                        if g < GROUP0 - 1:
                            yield 1
                    t_mm = t = sig.done(mm, "pe_o")
                    yield 1
                    sig.wait(dve, t, t_small)
                    t = sig.done(dve.tensor_scalar(oT[:, m, :], psum[:, n, :], bo[:, m:m + 1],
                                                   self.gate[0][:, 0, m, b:b + 1], ALU.add, ALU.mult), "dve_o")
                    banks.give(n, t)
                    ready.append(t)
                for ring in ctx_rings:
                    ring.give(0, t_mm)
                yield from self.residual(b, oT, oT_ring, y, ready, banks)

            U = H0 * TT
            for b in range(B):
                base = U * b
                if b:
                    steps.at(base - 60, self.norm(b, 0, 0, banks))
                steps.at(base - (48 if b else 18), project(b))
                for pair in range(H0 // 2):
                    steps.at(base + 8 * pair - 8, stack_pair(b, pair))
                for g in range(GROUP0):
                    steps.at(base + 16 * (g + 1) + 4, context(b, g))
                steps.at(base + U + 12, output(b))
            for u in range(B * U):
                steps.at(u, unit(u))
            steps.run()

    def early_weights(self, stack):
        sb = lambda name, shape, dt=F32: self.sb(stack, "a1_" + name, shape, dt)
        self.w1_kv = [sb(f"wkv_{x}", [P, KT * 2 * G1 * HD1], F32R) for x in ("hi", "lo")]
        self.w1_q = [sb(f"wq_{x}", [P, KT * H1 * HD1], F32R) for x in ("hi", "lo")]
        self.t_w1 = []
        self.stage1, self.stage1_ring = sb("stage", [P, 2, 512]), Ring(self.sig, 2)
        return self.split_weights(self.stage1, self.stage1_ring, "a1", 512, (
            (self.ins["w1_kv"], *self.w1_kv, self.t_w1), (self.ins["w1_q"], *self.w1_q, self.t_w1)))

    def attention1(self):
        sig, ins, pe, dve, act, pool = self.sig, self.ins, self.pe, self.dve, self.act, self.pool
        psum = self.psum
        with ExitStack() as st:
            sb = lambda name, shape, dt=F32: self.sb(st, "a1_" + name, shape, dt)
            self.norm_buffers(st, "a1", 2)
            NKV = 2 * G1 * HD1
            wkv, wq = self.w1_kv, self.w1_q
            wd = [sb(f"wd_{x}", [P, H1 * D], F32R) for x in ("hi", "lo")]
            mask = sb("mask", [P, S])
            kT, k_rings = sb("kT", [P, G1, 2, S], F32R), [Ring(sig, 1) for _ in range(G1)]
            v, v_ring = sb("v", [P, 2, TT, G1 * HD1]), Ring(sig, 2)
            q = sb("q", [P, 2, 2, S], F32R)
            q_ring = Ring(sig, 2)
            e, e_ring = sb("e", [P, 4, S]), Ring(sig, 4)
            et, et_ring = sb("et", [P, 2, TT, S]), Ring(sig, 2)
            nmax, rsum, rinv = sb("nmax", [P, 4, 1]), sb("rsum", [P, 4, 1]), sb("rinv", [P, 4, 1])
            small_ring = Ring(sig, 4)
            ctx, ctx_ring = sb("ctx", [P, 2, 2, S], F32R), Ring(sig, 2)
            oT, oT_ring = sb("oT", [P, KT, S]), Ring(sig, 1)

            s_banks, t_banks = Ring(sig, 2), Ring(sig, 2, 2)
            banks, o_banks = Ring(sig, 2, 4), Ring(sig, 2, 6)

            steps = Steps()
            h_of = self.h_of
            steps.at(-30, self.norm(0, 1, 0, banks))
            t_mask = self.load(mask[:, :], ins["mask"])
            t_d, n_d = [], 2 * H1 * D // 512
            steps.at(-31, self.split_weights(self.stage1, self.stage1_ring, "a1", 512, ((ins["w1_d"], *wd, t_d),)))

            def pair(w_, a, e_):
                return w_[0][:, a:e_], w_[1][:, a:e_]

            k_of, v_of, q_of, o_of, et_of = {}, {}, {}, {}, {}

            def project_kv(b):
                while b not in h_of:
                    yield 1
                slot, h_ready = h_of[b][:2]
                for g in range(G1):
                    while not (banks.open() and k_rings[g].open()):
                        yield 1
                    n = banks.take(pe)
                    sig.wait(pe, *self.t_w1, *h_ready)
                    for k in range(KT):
                        mm = self.mm3(psum[:, n, :], pair(wkv, k * NKV + g * P, k * NKV + (g + 1) * P),
                                      self.h(slot, k), k == 0, k == KT - 1)
                        if k == 0:
                            yield 1
                    t = sig.done(mm, "pe_kv")
                    yield 1
                    k_rings[g].take(act, dve)
                    sig.wait(act, t)
                    t_hi = sig.done(act.activation(kT[:, g, 0, :], psum[:, n, :], ACT.Copy), "act_k_hi")
                    sig.wait(dve, t_hi)
                    t_lo = sig.done(dve.tensor_tensor(kT[:, g, 1, :], psum[:, n, :], kT[:, g, 0, :], ALU.subtract),
                                    "dve_k_lo")
                    banks.give(n, t_hi, t_lo)
                    k_of[b, g] = t_hi, t_lo
                while not v_ring.open():
                    yield 1
                y = v_ring.take(act)
                for t_ in range(TT):
                    while not banks.open():
                        yield 1
                    n = banks.take(pe)
                    for k in range(KT):
                        c = k * NKV + G1 * HD1
                        mm = self.mm3(psum[:, n, :], self.h(slot, k, slice(t_ * P, (t_ + 1) * P)),
                                      pair(wkv, c, c + G1 * HD1), k == 0, k == KT - 1)
                        if k == 0:
                            yield 1
                    t = sig.done(mm, "pe_kv")
                    yield 1
                    sig.wait(act, t)
                    t = sig.done(act.activation(v[:, y, t_, :], psum[:, n, :], ACT.Copy), "act_v")
                    banks.give(n, t)
                v_of[b] = y, t

            def project_q(b, h):
                while not (b in h_of and banks.open() and q_ring.open()):
                    yield 1
                slot, h_ready = h_of[b][:2]
                n = banks.take(pe)
                sig.wait(pe, *self.t_w1, *h_ready)
                for k in range(KT):
                    c = (h * KT + k) * P
                    mm = self.mm3(psum[:, n, :], pair(wq, c, c + P), self.h(slot, k), k == 0, k == KT - 1)
                    if k == 0:
                        yield 1
                t = sig.done(mm, "pe_q")
                if h == H1 - 1:
                    self.h_ring.give(slot, t, ("pe_kv", sig.count["pe_kv"]))
                yield 1
                while not q_ring.open():
                    yield 1
                i = q_ring.take(act, dve)
                sig.wait(act, t)
                t_hi = sig.done(act.activation(q[:, i, 0, :], psum[:, n, :], ACT.Copy, scale=-SCALE1), "act_q_hi")
                sig.wait(dve, t_hi)
                t_lo = sig.done(dve.scalar_tensor_tensor(q[:, i, 1, :], psum[:, n, :], -SCALE1, q[:, i, 0, :],
                                                         ALU.mult, ALU.subtract), "dve_q_lo")
                banks.give(n, t_hi, t_lo)
                q_of[b, h] = i, (t_hi, t_lo)

            def unit(u):
                b, h, qt = u // (H1 * TT), u // TT % H1, u % TT
                g, W = h // HPG1, (qt + 1) * P
                while not ((b, h) in q_of and (b, g) in k_of and s_banks.open()):
                    yield 1
                i, ready = q_of[b, h]
                n = s_banks.take(pe)
                sig.wait(pe, *ready, *k_of[b, g])
                mm = self.mm3(psum[:, n, 0:W], (q[:, i, 0, qt * P:W], q[:, i, 1, qt * P:W]),
                              (kT[:, g, 0, 0:W], kT[:, g, 1, 0:W]), True, True)
                t = sig.done(mm, "pe_s")
                if qt == TT - 1:
                    q_ring.give(i, t)
                    if h % HPG1 == HPG1 - 1:
                        k_rings[g].give(0, t)
                yield 1
                while not small_ring.open():
                    yield 1
                m = small_ring.take(dve, act)
                sig.wait(dve, t, t_mask)
                t = sig.done(dve.tensor_tensor_reduce(psum[:, n, 0:W], psum[:, n, 0:W], mask[:, S - W:S], 1.0, BIG,
                                                      ALU.add, ALU.min, nmax[:, m, :]), "dve_max")
                while not e_ring.open():
                    yield 1
                x = e_ring.take(act)
                sig.wait(act, t)
                t = sig.done(act.activation(e[:, x, 0:W], psum[:, n, 0:W], ACT.Exp, bias=nmax[:, m, :], scale=-1.0,
                                            accum_out=rsum[:, m, :]), "act_e")
                s_banks.give(n, t)
                yield 1
                sig.wait(dve, t)
                t = sig.done(dve.reciprocal(rinv[:, m, :], rsum[:, m, :]), "dve_rinv")
                sig.wait(dve, t)
                t = sig.done(dve.tensor_scalar(e[:, x, 0:W], e[:, x, 0:W], rinv[:, m, 0:1], None, ALU.mult),
                             "dve_norm")
                small_ring.give(m, t)
                yield 1
                while not t_banks.open():
                    yield 1
                n = t_banks.take(pe)
                sig.wait(pe, t)
                for k in range(qt + 1):
                    mm = pe.transpose(psum[:, n, k * P:(k + 1) * P], e[:, x, k * P:(k + 1) * P], self.ident[:, :])
                t = sig.done(mm, "pe_turn")
                e_ring.give(x, t)
                yield 1
                if qt == 0:
                    while not et_ring.open():
                        yield 1
                    et_of[b, h] = [et_ring.take(act), []]
                while (b, h) not in et_of:
                    yield 1
                i, ready = et_of[b, h]
                sig.wait(act, t)
                t = sig.done(act.activation(et[:, i, 0:qt + 1, qt * P:W],
                                            psum[:, n, 0:W].rearrange("p (k q) -> p k q", q=P), ACT.Copy), "act_et")
                t_banks.give(n, t)
                ready.append(t)

            def context(b, h):
                g = h // HPG1
                while not ((b, h) in et_of and len(et_of[b, h][1]) == TT and b in v_of and banks.open()):
                    yield 1
                i, ready = et_of[b, h]
                y, t_v = v_of[b]
                n = banks.take(pe)
                sig.wait(pe, *ready, t_v)
                for k in range(TT):
                    mm = pe.matmul(psum[:, n, k * P:S], v[:, y, k, g * HD1:(g + 1) * HD1], et[:, i, k, k * P:S],
                                   start=(k == 0), stop=(k == TT - 1), skip_group_check=True)
                    if k < TT - 2:
                        yield 1
                t = sig.done(mm, "pe_pv")
                if h == H1 - 1:
                    v_ring.give(y, t)
                et_ring.give(i, t)
                yield 1
                while not ctx_ring.open():
                    yield 1
                j = ctx_ring.take(act, dve)
                sig.wait(act, t)
                t_hi = sig.done(act.activation(ctx[:, j, 0, :], psum[:, n, :], ACT.Copy), "act_ctx_hi")
                sig.wait(dve, t_hi)
                t_lo = sig.done(dve.tensor_tensor(ctx[:, j, 1, :], psum[:, n, :], ctx[:, j, 0, :], ALU.subtract),
                                "dve_ctx_lo")
                banks.give(n, t_hi, t_lo)
                yield 1
                if h == 0:
                    while not o_banks.open(KT):
                        yield 1
                    o_of[b] = [o_banks.take(pe) for _ in range(KT)]
                while len(t_d) < n_d:
                    yield 1
                sig.wait(pe, t_hi, t_lo, *t_d)
                for m in range(KT):
                    c = h * D + m * P
                    mm = self.mm3(psum[:, o_of[b][m], :], pair(wd, c, c + P), (ctx[:, j, 0, :], ctx[:, j, 1, :]),
                                  h == 0, h == H1 - 1)
                    if m < KT - 1:
                        yield 1
                t = sig.done(mm, "pe_o")
                ctx_ring.give(j, t)
                if h == H1 - 1:
                    while not oT_ring.open():
                        yield 1
                    y = oT_ring.take(dve)
                    ready = []
                    for m in range(KT):
                        sig.wait(dve, t)
                        t_o = sig.done(dve.tensor_scalar(oT[:, m, :], psum[:, o_of[b][m], :],
                                                         self.gate[1][:, 0, m, b:b + 1], None, ALU.mult), "dve_o")
                        o_banks.give(o_of[b][m], t_o)
                        ready.append(t_o)
                    yield 1
                    yield from self.residual(b, oT, oT_ring, y, ready, banks)

            U = H1 * TT
            for b in range(B):
                base = U * b
                if b:
                    steps.at(base - 45, self.norm(b, 1, 0, banks))
                steps.at(base - 28, project_kv(b))
                for h in range(H1):
                    steps.at(base + TT * h - 6, project_q(b, h))
                    steps.at(base + TT * (h + 1) + 4, context(b, h))
            for u in range(B * U):
                steps.at(u, unit(u))
            steps.run()

    def empty_slots(self, stack):
        sig, pool = self.sig, self.pool
        self.slots, self.results, self.t_slots = [], [], []
        for l, (n_exp, picked) in enumerate(((E0, K0), (E1, K1))):
            self.slots.append(self.nc.dram_tensor(f"slots{l}", (slot_tiles(n_exp, picked) * P, ROW), F32).ap())
            self.results.append(self.nc.dram_tensor(f"results{l}", (NT * P * picked, D), F32).ap())
        self.empty = self.sb(stack, "empty", [P, ROW])
        t = sig.done(pool.memset(self.empty[:, :], 0.0), "pool_empty")
        sig.wait(pool, t)
        self.t_empty = sig.done(pool.iota(self.empty[:, D:D + 1].bitcast(I32), pattern=[[0, 1]],
                                          base=NT * P * max(K0, K1), channel_multiplier=1), "pool_empty")

    def fill_slots(self):
        for slots in self.slots:
            n = slots.shape[0] // P
            self.t_slots.append(self.load(slots.rearrange("(n p) c -> p n c", p=P),
                                          self.empty[:, :].unsqueeze(1).broadcast_to([P, n, ROW]), self.t_empty))
            yield 1

    def mixture(self, l, n_exp, picked, hid, last, background=None):
        sig, ins, pe, dve, act, pool = self.sig, self.ins, self.pe, self.dve, self.act, self.pool
        psum = self.psum
        n_tiles, n_all = slot_tiles(n_exp, picked), n_exp + SHARED
        chunks = [(a, min(P, hid - a)) for a in range(0, hid, P)]
        GU, WE = 2 * hid, KT * 2 * hid + len(chunks) * D
        slots, results = self.slots[l], self.results[l]
        with ExitStack() as st:
            sb = lambda name, shape, dt=F32: self.sb(st, f"m{l}_" + name, shape, dt)
            self.norm_buffers(st, f"m{l}", 0, B)
            w = sb("w", [P, n_all * WE])
            gate_w = sb("gate_w", [P, KT, n_exp])
            gate_rows = sb("gate_rows", [P, B, D])
            xT, xT_ring = sb("xT", [P, 2, KT, P]), Ring(sig, 2)
            silu, silu_ring = sb("silu", [P, 2, hid]), Ring(sig, 2)
            hd, hd_ring = sb("hid", [P, 2, hid]), Ring(sig, 2)
            hdT, hdT_ring = sb("hidT", [P, 2, len(chunks), P]), Ring(sig, 2)
            w_at = sb("w_at", [1, P], I32)
            banks, gu_banks = Ring(sig, 2), Ring(sig, 2, 2)
            hT_banks, y_banks = Ring(sig, 2, 4), Ring(sig, 2, 6)
            t_gw = self.load(gate_w[:, :, :], ins[f"router{l}"])
            t_w = {}
            for a in range(0, n_all, SHARED):
                t = self.load(w[:, a * WE:(a + SHARED) * WE].rearrange("p (e c) -> p e c", c=WE),
                              ins[f"experts{l}"][a:a + SHARED].rearrange("e p c -> p e c"),
                              name=f"load_m{l}_{'experts' if a else 'shared'}")
                t_w[a > 0] = t

            def gate_up(x_of, at, ready):
                n = gu_banks.take(pe)
                sig.wait(pe, *ready)
                for k in range(KT):
                    mm = pe.matmul(psum[:, n, 0:GU], x_of(k), w[:, at(k * GU, GU)], start=(k == 0),
                                   stop=(k == KT - 1))
                return n, sig.done(mm, "pe_gu")

            def swiglu(n, t):
                x = silu_ring.take(act)
                sig.wait(act, t)
                t_s = sig.done(act.activation(silu[:, x, :], psum[:, n, 0:hid], ACT.Silu), "act_silu")
                y = hd_ring.take(dve)
                sig.wait(dve, t_s)
                t = sig.done(dve.tensor_tensor(hd[:, y, :], silu[:, x, :], psum[:, n, hid:GU], ALU.mult), "dve_hid")
                silu_ring.give(x, t)
                gu_banks.give(n, t)
                return y, t

            def turn_hidden(y, t):
                n = hT_banks.take(pe)
                sig.wait(pe, t)
                for c, (a, m) in enumerate(chunks):
                    mm = pe.transpose(psum[0:m, n, c * P:(c + 1) * P], hd[:, y, a:a + m], self.ident[:, :])
                t = sig.done(mm, "pe_hidT")
                hd_ring.give(y, t)
                return n, t

            def copy_hidden(n, t):
                z = hdT_ring.take(dve)
                sig.wait(dve, t)
                for c, (a, m) in enumerate(chunks):
                    t = sig.done(dve.tensor_copy(hdT[0:m, z, c, :], psum[0:m, n, c * P:(c + 1) * P]), "dve_hidT")
                hT_banks.give(n, t)
                return z, t

            def down(n, z, at, t, first=True, end=True):
                sig.wait(pe, t)
                for c, (a, m) in enumerate(chunks):
                    mm = pe.matmul(psum[:, n, 0:D], hdT[0:m, z, c, :], w[0:m, at(KT * GU + c * D, D)],
                                   start=(first and c == 0), stop=(end and c == len(chunks) - 1))
                t = sig.done(mm, "pe_down")
                hdT_ring.give(z, t)
                return t

            with ExitStack() as route:
                rb = lambda name, shape, dt=F32: self.sb(route, f"r{l}_" + name, shape, dt)
                hn, hn_ready = rb("h_nat", [P, NT, D]), {}
                work, work_ring = rb("work", [P, 2, 2, TT, n_exp]), Ring(sig, 2)
                small, tops = rb("small", [P, 2, 3, TT]), rb("top8", [P, 2, TT, 8])
                scores, mask = rb("scores", [P, NT, n_exp]), rb("mask", [P, NT, n_exp])
                count, base = rb("count", [P, NT, n_exp]), rb("base", [P, NT, n_exp])
                key, tmp = rb("key", [P, NT, n_exp]), rb("tmp", [P, NT, n_exp])
                per = rb("per_expert", [P, 5, n_exp])
                per_i = rb("per_expert_int", [P, n_exp], I32)
                key8, slot_of = rb("key8", [P, NT, 8]), rb("slot_of", [P, NT, picked], U32)
                weight = rb("weight", [P, picked, NT])
                result_of = rb("result_of", [P, NT, picked], I32)
                part = rb("partition", [P, 1], I32), rb("partition_f", [P, 1]), rb("tile_expert", [P, 1])
                before, ones = rb("before", [P, P]), rb("ones", [P, P])
                rows, rows_ring = rb("rows", [P, 3, picked, ROW]), Ring(sig, 3)
                spread_g = rb("gate_spread", [P, P])
                t_before = self.load(before[:, :], ins["before"])
                t_ones = sig.done(pool.memset(ones[:, :], 1.0), "pool_route")
                sig.done(pool.iota(result_of[:, :, :], pattern=[[P * picked, NT], [1, picked]], base=0,
                                   channel_multiplier=picked), "pool_route")
                t_iota = sig.done(pool.iota(part[0][:, :], pattern=[[0, 1]], base=0, channel_multiplier=1),
                                  "pool_route")

                gates = {}

                def gate_row():
                    t_done = None
                    for b in range(B):
                        for k in range(KT):
                            sig.wait(dve, self.t_mod[l], t_ones, t_done)
                            t = sig.done(dve.tensor_scalar(spread_g[:, :], ones[:, :], self.gate[l][:, 1, k, b:b + 1],
                                                           None, ALU.mult), "dve_gate")
                            while not banks.open():
                                yield 1
                            n = banks.take(pe)
                            sig.wait(pe, t)
                            mm = pe.matmul(psum[:, n, 0:P], spread_g[:, :], self.ident[:, :], start=True, stop=True)
                            t_done = t = sig.done(mm, "pe_gate")
                            yield 1
                            sig.wait(dve, t)
                            t = sig.done(dve.tensor_copy(gate_rows[:, b, k * P:(k + 1) * P], psum[:, n, 0:P]),
                                         "dve_gate")
                            banks.give(n, t)
                        gates[b] = t

                def router(b):
                    while b not in self.h_of or not banks.open():
                        yield 1
                    _, _, t_h, s32 = self.h_of[b]
                    n = banks.take(pe)
                    sig.wait(pe, t_gw, t_h)
                    for t_ in range(TT):
                        for k in range(KT):
                            mm = pe.matmul(psum[:, n, t_ * n_exp:(t_ + 1) * n_exp],
                                           self.h32[:, s32, k, t_ * P:(t_ + 1) * P], gate_w[:, k, :],
                                           start=(k == 0), stop=(k == KT - 1))
                    t_l = sig.done(mm, "pe_logits")
                    logits = psum[:, n, 0:TT * n_exp].rearrange("p (t e) -> p t e", e=n_exp)
                    yield 1
                    while not work_ring.open():
                        yield 1
                    y = work_ring.take(dve, act)
                    ex, rest, top = work[:, y, 0], work[:, y, 1], tops[:, y]
                    nmax, total, inv = (small[:, y, i, :] for i in range(3))
                    sig.wait(dve, t_l)
                    t = sig.done(dve.tensor_reduce(nmax, logits, AX.X, ALU.max, negate=True), "dve_router")
                    sig.wait(act, t)
                    for t_ in range(TT):
                        t = sig.done(act.activation(ex[:, t_, :], logits[:, t_, :], ACT.Exp, bias=nmax[:, t_:t_ + 1],
                                                    accum_out=total[:, t_:t_ + 1]), "act_router")
                    banks.give(n, t)
                    yield 1
                    sig.wait(dve, t)
                    t = sig.done(dve.reciprocal(inv, total), "dve_router")
                    sig.wait(dve, t)
                    sc = scores[:, b * TT:(b + 1) * TT, :]
                    for t_ in range(TT):
                        t = sig.done(dve.tensor_scalar(sc[:, t_, :], ex[:, t_, :], inv[:, t_:t_ + 1], None, ALU.mult),
                                     "dve_router")
                    sig.wait(dve, t)
                    for t_ in range(TT):
                        t = sig.done(dve.max(top[:, t_, :], sc[:, t_, :]), "dve_router")
                    sig.wait(dve, t)
                    t = sig.done(dve.memset(top[:, :, picked:8], -1.0), "dve_router")
                    sig.wait(dve, t)
                    for t_ in range(TT):
                        t = sig.done(dve.match_replace(out=rest[:, t_, :], in_to_replace=top[:, t_, :],
                                                       in_values=sc[:, t_, :], imm_value=-1.0), "dve_router")
                    sig.wait(dve, t)
                    t = sig.done(dve.tensor_scalar(mask[:, b * TT:(b + 1) * TT, :], rest, 0.0, None, ALU.is_lt),
                                 "dve_router")
                    work_ring.give(y, t)
                    mask_ready[b] = t
                    yield 1
                    for half in range(2):
                        while not hT_banks.open():
                            yield 1
                        n = hT_banks.take(pe)
                        for i in range(2):
                            t_ = 2 * half + i
                            for k in range(KT):
                                mm = pe.transpose(psum[:, n, i * D + k * P:i * D + (k + 1) * P],
                                                  self.h32[:, s32, k, t_ * P:(t_ + 1) * P], self.ident[:, :])
                        t = sig.done(mm, "pe_h_nat")
                        yield 1
                        lo = b * TT + 2 * half
                        sig.wait(act, t)
                        t = sig.done(act.activation(hn[:, lo:lo + 2, :].rearrange("p t d -> p (t d)"), psum[:, n, :],
                                                    ACT.Copy), "act_h_nat")
                        hT_banks.give(n, t)
                        hn_ready[lo] = hn_ready[lo + 1] = t

                mask_ready = {}

                def places():
                    while len(mask_ready) < B or not banks.open(2):
                        yield 1
                    link = lambda ins_: sig.wait(dve, sig.done(ins_, "dve_places"))
                    flat = lambda a: a.rearrange("p t e -> p (t e)")
                    N = NT * n_exp
                    n_pre, n_every = banks.take(pe), banks.take(pe)
                    sig.wait(pe, *mask_ready.values(), t_before, t_ones)
                    pe.matmul(psum[:, n_pre, 0:N], before[:, :], flat(mask[:, :, :]), start=True, stop=True)
                    t = sig.done(pe.matmul(psum[:, n_every, 0:N], ones[:, :], flat(mask[:, :, :]), start=True,
                                           stop=True), "pe_count")
                    yield 1
                    sig.wait(dve, t, t_iota)
                    t = sig.done(dve.tensor_copy(flat(count[:, :, :]), psum[:, n_every, 0:N]), "dve_places")
                    banks.give(n_every, t)
                    sig.wait(dve, t)
                    link(dve.memset(base[:, 0, :], 0.0))
                    for t_ in range(1, NT):
                        link(dve.tensor_tensor(base[:, t_, :], base[:, t_ - 1, :], count[:, t_ - 1, :], ALU.add))
                    n_picks, n_t, end, other, first = (per[:, i, :] for i in range(5))
                    link(dve.tensor_tensor(n_picks, base[:, NT - 1, :], count[:, NT - 1, :], ALU.add))
                    t = sig.done(dve.tensor_tensor(flat(tmp[:, :, :]), psum[:, n_pre, 0:N], flat(base[:, :, :]),
                                                   ALU.add), "dve_places")
                    banks.give(n_pre, t)
                    link(dve.tensor_scalar(per_i[:, :], n_picks, float(P - 1), None, ALU.add))
                    link(dve.tensor_scalar(per_i[:, :], per_i[:, :], P.bit_length() - 1, None,
                                           ALU.arith_shift_right))
                    link(dve.tensor_copy(n_t, per_i[:, :]))
                    link(dve.tensor_copy(end, n_t))
                    shift = 1
                    while shift < n_exp:
                        link(dve.tensor_copy(other, end))
                        link(dve.tensor_tensor(end[:, shift:], other[:, shift:], other[:, 0:n_exp - shift], ALU.add))
                        shift *= 2
                    link(dve.tensor_tensor(first, end, n_t, ALU.subtract))
                    link(dve.tensor_scalar(first, first, float(P), None, ALU.mult))
                    link(dve.tensor_tensor(key[:, :, :], tmp[:, :, :], first.unsqueeze(1).broadcast_to([P, NT, n_exp]),
                                           ALU.add))
                    link(dve.scalar_tensor_tensor(flat(key[:, :, :]), flat(key[:, :, :]), 1.0, flat(mask[:, :, :]),
                                                  ALU.add, ALU.mult))
                    for t_ in range(NT):
                        t = sig.done(dve.max(key8[:, t_, :], key[:, t_, :]), "dve_places")
                    sig.wait(dve, t)
                    t_slot = sig.done(dve.tensor_scalar(slot_of[:, :, :], key8[:, :, 0:picked], -1.0, None, ALU.add),
                                      "dve_places")
                    link(dve.tensor_copy(part[1][:, :], part[0][:, :]))
                    link(dve.tensor_scalar(other, end, part[1][:, 0:1], None, ALU.is_le))
                    link(dve.tensor_reduce(part[2][:, :], other, AX.X, ALU.add))
                    t = sig.done(dve.tensor_scalar(part[2][:, :], part[2][:, :], float(n_exp - 1), float(SHARED),
                                                   ALU.min, ALU.add), "dve_places")
                    while not banks.open():
                        yield 1
                    n = banks.take(pe)
                    sig.wait(pe, t)
                    t = sig.done(pe.transpose(psum[0:1, n, 0:P], part[2][:, :], self.ident[:, :]), "pe_count")
                    sig.wait(dve, t)
                    t = sig.done(dve.tensor_scalar(w_at[:, :], psum[0:1, n, 0:P], float(WE), None, ALU.mult),
                                 "dve_places")
                    banks.give(n, t)
                    self.t_w_at = t
                    for t_ in range(NT):
                        if t_ % TT == 0:
                            of = slice(t_, t_ + TT)
                            for j in range(picked):
                                link(dve.tensor_tensor(tmp[:, of, :], key[:, of, :],
                                                       key8[:, of, j:j + 1].broadcast_to([P, TT, n_exp]),
                                                       ALU.is_equal))
                                link(dve.tensor_tensor(tmp[:, of, :], tmp[:, of, :], scores[:, of, :], ALU.mult))
                                link(dve.tensor_reduce(weight[:, j, of], tmp[:, of, :], AX.X, ALU.add))
                            t_places = "dve_places", sig.count["dve_places"]
                        while not rows_ring.open():
                            yield 1
                        r = rows_ring.take(act, dve)
                        sig.wait(act, hn_ready[t_])
                        t_r = sig.done(act.activation(rows[:, r, :, 0:D],
                                                      hn[:, t_, :].unsqueeze(1).broadcast_to([P, picked, D]),
                                                      ACT.Copy), "act_rows")
                        sig.wait(dve, t_places)
                        sig.done(dve.tensor_copy(rows[:, r, :, D].bitcast(I32), result_of[:, t_, :]), "dve_rows")
                        t_x = sig.done(dve.tensor_copy(rows[:, r, :, D + 1], weight[:, :, t_]), "dve_rows")
                        sig.wait(pool, t_r, t_x, t_slot, self.t_slots[l])
                        for j in range(picked):
                            t = sig.done(pool.indirect_dma_start(
                                slots[:, :], bass.IndirectOffsetOnAxis(ap=slot_of[:, t_, j:j + 1], axis=0),
                                rows[:, r, j, :], None), f"send_m{l}_{r}", 16)
                        rows_ring.give(r, t)
                        sent[r] = t
                        yield picked // 2
                    slots_filled.extend(sent.values())

                sent, slots_filled = {}, []
                shared_past = []

                def shared(tile):
                    b, t_ = divmod(tile, TT)
                    while not (b in self.h_of and b in gates and gu_banks.open(SHARED)):
                        yield 1
                    s32 = self.h_of[b][3]
                    ats = [lambda c, n, e=e: slice(e * WE + c, e * WE + c + n) for e in range(SHARED)]
                    two = [gate_up(lambda k: self.h32[:, s32, k, t_ * P:(t_ + 1) * P], at,
                                   [self.h_of[b][2], t_w[False]]) for at in ats]
                    yield 1
                    while not (silu_ring.open(SHARED) and hd_ring.open(SHARED)):
                        yield 1
                    two = [swiglu(n, t) for n, t in two]
                    yield 1
                    while not hT_banks.open(SHARED):
                        yield 1
                    two = [turn_hidden(y, t) for y, t in two]
                    while not hdT_ring.open(SHARED):
                        yield 1
                    two = [copy_hidden(n, t) for n, t in two]
                    shared_past.append(tile)
                    yield 1
                    while not y_banks.open():
                        yield 1
                    m = y_banks.take(pe)
                    for e, (z, t) in enumerate(two):
                        t = down(m, z, ats[e], t, e == 0, e == SHARED - 1)
                    yield 1
                    while not fin_ring.open():
                        yield 1
                    f = fin_ring.take(dve)
                    sig.wait(dve, t)
                    t = sig.done(dve.tensor_tensor(fin[:, f, :], psum[:, m, 0:D], gate_rows[:, b, :], ALU.mult),
                                 "dve_shared")
                    y_banks.give(m, t)
                    sig.wait(dve, t, self.x_ready[tile])
                    t = sig.done(dve.tensor_tensor(self.x[:, tile, :], self.x[:, tile, :], fin[:, f, :], ALU.add),
                                 "dve_x")
                    fin_ring.give(f, t)
                    self.x_ready[tile] = t

                fin, fin_ring = rb("fin", [P, 2, D]), Ring(sig, 2)
                steps = Steps()
                if not last:
                    wmod = rb("wmod", [P, KT, 6 * D])

                    def next_modulation():
                        while not y_banks.open():
                            yield 1
                        self.modulation(l + 1, wmod[:, :, :], y_banks)
                    steps.at(6 * B + 8, next_modulation())
                self.moments = None
                steps.at(0, self.statistics(range(NT)))
                for b in range(B):
                    steps.at(2 + b, self.norm(b, l, 1, banks, together=True))
                    steps.at(6 + b, router(b))
                steps.at(4 + B, places())
                steps.at(12, gate_row())
                for tile in range(NT):
                    steps.at(13 + 2 * tile, shared(tile))

                NX, NY, NI = 5, 4, 16
                to, to_ring = rb("to", [P, NI, ROW - D]), Ring(sig, NI)
                xs, xs_ring = rb("xs", [P, NX, ROW]), Ring(sig, NX)
                ys, ys_ring = rb("ys", [P, NY, D]), Ring(sig, NY)

                def slot_tile(i):
                    while not (xs_ring.open() and slots_filled):
                        yield 1
                    x = xs_ring.take(self.sp)
                    t_x = self.load(xs[:, x, :], slots[i * P:(i + 1) * P, :], *slots_filled, name=f"load_l{l}_xs{x}")
                    yield 3
                    while not banks.open():
                        yield 1
                    n = banks.take(pe)
                    while not to_ring.open():
                        yield 1
                    q = to_ring.take(dve)
                    sig.wait(dve, t_x)
                    t_to = sig.done(dve.tensor_copy(to[:, q, :].bitcast(I32), xs[:, x, D:ROW].bitcast(I32)), "dve_to")
                    sig.wait(pe, self.t_w_at)
                    start = pe.value_load(w_at[0:1, i:i + 1], min_val=SHARED * WE, max_val=(n_all - 1) * WE)
                    at = lambda c, n_: bass.ds(start + c, n_)
                    sig.wait(pe, t_x)
                    for k in range(KT):
                        mm = pe.transpose(psum[:, n, k * P:(k + 1) * P], xs[:, x, k * P:(k + 1) * P],
                                          self.ident[:, :])
                    t = sig.done(mm, "pe_xsT")
                    xs_ring.give(x, t, t_to)
                    yield 1
                    while not xT_ring.open():
                        yield 1
                    v = xT_ring.take(act)
                    sig.wait(act, t)
                    t = sig.done(act.activation(xT[:, v].rearrange("p k t -> p (k t)"), psum[:, n, 0:D], ACT.Copy),
                                 "act_xsT")
                    banks.give(n, t)
                    yield 1
                    while not (gu_banks.open() and len(shared_past) == NT):
                        yield 1
                    if i == 0:
                        sig.wait(pe, *t_w.values())
                    sig.wait(pe, t)
                    n, t = gate_up(lambda k: xT[:, v, k, :], at, [t])
                    xT_ring.give(v, t)
                    yield 1
                    y, t = swiglu(n, t)
                    yield 1
                    n, t = turn_hidden(y, t)
                    yield 1
                    z, t = copy_hidden(n, t)
                    yield 1
                    while not y_banks.open():
                        yield 1
                    m = y_banks.take(pe)
                    sig.wait(pe, t)
                    t = down(m, z, at, t)
                    pe.free_register(start.val)
                    yield 1
                    while not ys_ring.open():
                        yield 1
                    o = ys_ring.take(act)
                    sig.wait(act, t, t_to)
                    t = sig.done(act.activation(ys[:, o, :], psum[:, m, 0:D], ACT.Copy, scale=to[:, q, 1:2]),
                                 "act_ys")
                    y_banks.give(m, t)
                    sig.wait(pool, t, t_to)
                    t = sig.done(pool.indirect_dma_start(
                        results[:, :], bass.IndirectOffsetOnAxis(ap=to[:, q, 0:1].bitcast(U32), axis=0),
                        ys[:, o, :], None, bounds_check=NT * P * picked - 1, oob_is_err=False),
                        f"send_l{l}_{o}", 16)
                    ys_ring.give(o, t)
                    to_ring.give(q, t)

                if background:
                    steps.at(4 + 2 * NT, background)
                for i in range(n_tiles):
                    steps.at(10 + 2 * NT + i, slot_tile(i))
                steps.run()
            self.phase_barrier()

            with ExitStack() as combine:
                NR = 6
                res, res_ring = self.sb(combine, f"l{l}_res", [P, NR, picked * D]), Ring(sig, NR)
                acc, acc_ring = self.sb(combine, f"l{l}_acc", [P, 4, 2 * D]), Ring(sig, 4)
                sent = [(name, n) for name, n in sig.count.items() if name.startswith(f"send_l{l}")]
                o_dram = self.out.rearrange("b (t p) d -> p (b t) d", p=P)

                def finish(tile, a, t):
                    sig.wait(dve, t)
                    t = sig.done(dve.tensor_tensor(self.x[:, tile, :], self.x[:, tile, :], acc[:, a, 0:D], ALU.add),
                                 "dve_x")
                    acc_ring.give(a, t)
                    self.x_ready[tile] = t
                    if last:
                        self.load(o_dram[:, tile:tile + 1, :], self.x[:, tile:tile + 1, :], t, name="store",
                                  queue=act)

                for tile in range(NT):
                    r = res_ring.take(self.sp)
                    t = self.load(res[:, r, :], results[tile * P * picked:(tile + 1) * P * picked, :]
                                  .rearrange("(p j) d -> p (j d)", j=picked), *sent, name=f"load_l{l}_res{r}")
                    engine, done = (pool, "pool_res") if tile % 4 == 1 else (dve, "dve_res")
                    a = acc_ring.take(engine)
                    width, src = picked * D, res[:, r, :]
                    while width > D:
                        width //= 2
                        sig.wait(engine, t)
                        t = sig.done(engine.tensor_tensor(acc[:, a, 0:width], src[:, 0:width],
                                                          src[:, width:2 * width], ALU.add), done)
                        if width == picked * D // 2:
                            res_ring.give(r, t)
                        src = acc[:, a, :]
                    sig.wait(engine, t)
                    t = sig.done(engine.tensor_tensor(acc[:, a, 0:D], acc[:, a, 0:D], gate_rows[:, tile // TT, :],
                                                      ALU.mult), done)
                    if engine is pool:
                        held = tile, a, t
                    else:
                        finish(tile, a, t)
                    if tile % 4 == 3:
                        finish(*held)


def adaln_program(nc, ins, out):
    with ExitStack() as stack:
        p = Program(nc, ins, out, stack)
        p.setup(stack)
        p.empty_slots(stack)
        p.attention0()
        p.phase_barrier()
        with ExitStack() as early:
            p.mixture(0, E0, K0, HID0, last=False, background=p.early_weights(early))
            p.phase_barrier()
            p.attention1()
        p.phase_barrier()
        p.mixture(1, E1, K1, HID1, last=True)
        p.sig.everything(p.sp)


def rope_table():
    theta = np.float32(10000.0) ** (-np.arange(0, HD0, 2, dtype=np.float32) / np.float32(HD0))
    freqs = np.arange(S, dtype=np.float32)[None, :] * theta.astype(np.float32)[:, None]
    table = np.zeros((P // HD0, HD0, 2, S), np.float32)
    table[:, :HD0 // 2, 0] = np.cos(freqs)
    table[:, :HD0 // 2, 1] = -np.sin(freqs)
    table[:, HD0 // 2:, 0] = 1.0
    return table.reshape(P, 2, S)


def stack_selectors():
    sel = np.zeros((P, 4, 4, P), np.float32)
    places = ((0, 1), (2, 3), (0, 2), (1, 3))
    for kind, where in enumerate(places):
        value = HD0 ** -0.5 if kind < 2 else 1.0
        for pair in range(4):
            for hh in range(2):
                for i in range(HD0):
                    for w in where:
                        sel[(2 * pair + hh) * HD0 + i, kind, pair, hh * STACK + w * HD0 + i] = value
    return sel.reshape(P, -1)


def causal_mask():
    mask = np.zeros((P, S), np.float32)
    mask[:, S - P:] = np.where(np.arange(P)[:, None] >= np.arange(P)[None, :], 0.0, BIG)
    return mask


def k_tiles(w):
    k, n = w.shape
    return w.reshape(k // P, P, n).transpose(1, 0, 2).reshape(P, -1)


def pack_experts(gate, up, down):
    e, _, h = gate.shape
    tiles = -(-h // P)
    gu = np.concatenate([a.reshape(e, KT, P, h) for a in (gate, up)], axis=3).transpose(0, 2, 1, 3)
    down = np.pad(down, ((0, 0), (0, tiles * P - h), (0, 0))).reshape(e, tiles, P, D).transpose(0, 2, 1, 3)
    return np.concatenate([gu.reshape(e, P, -1), down.reshape(e, P, -1)], axis=2)


def lay_out(a):
    heads = np.arange(D).reshape(H0, HD0)
    even, odd = heads[:, ::2], heads[:, 1::2]
    value = np.concatenate([even, odd], axis=1).reshape(-1)
    partner = np.concatenate([odd, even], axis=1).reshape(-1)
    wq, wk, wv, wo = (a[f"L0_attn_w{x}"] for x in "qkvo")
    w0 = np.concatenate([w.T[:, o] for w in (wq, wk) for o in (value, partner)] + [wv.T], axis=1)
    b0 = np.concatenate([a[f"L0_attn_b{x}"][o].reshape(2, P) for x in "qk" for o in (value, partner)]).T
    wo_rows = np.zeros((H0, 32, D), np.float32)
    wo_rows[:, :HD0] = wo.T.reshape(H0, HD0, D)
    wq1 = a["L1_attn_w_q"].reshape(KT, P, H1, HD1).transpose(1, 2, 0, 3).reshape(P, -1)
    cut = lambda w: w.reshape(D, SHARED, -1).transpose(1, 0, 2)
    ffn0 = pack_experts(np.concatenate([cut(a["L0_ffn_sw_gate"]), a["L0_ffn_w_gate"]]),
                        np.concatenate([cut(a["L0_ffn_sw_up"]), a["L0_ffn_w_up"]]),
                        np.concatenate([a["L0_ffn_sw_down"].reshape(SHARED, -1, D), a["L0_ffn_w_down"]]))
    turn = lambda w: w.transpose(0, 2, 1)
    ffn1 = pack_experts(np.concatenate([cut(a["L1_ffn_sw1"].T), turn(a["L1_ffn_w1"])]),
                        np.concatenate([cut(a["L1_ffn_sw3"].T), turn(a["L1_ffn_w3"])]),
                        np.concatenate([a["L1_ffn_sw2"].T.reshape(SHARED, -1, D), turn(a["L1_ffn_w2"])]))
    return {
        "x": a["L0_attn_x"],
        "ident": np.eye(P, dtype=np.float32),
        "c0": a["L0_c"].T.reshape(KT, P, B).transpose(1, 0, 2),
        "c1": a["L1_c"].T.reshape(KT, P, B).transpose(1, 0, 2),
        "wmod0": a["L0_wmod"], "wmod1": a["L1_wmod"],
        "w0_qkv": k_tiles(w0), "b0_qk": b0, "b0_v": a["L0_attn_bv"],
        "w0_o": k_tiles(wo_rows.reshape(-1, D)), "b0_o": a["L0_attn_bo"].reshape(KT, P).T,
        "rope": rope_table(), "stack_sel": stack_selectors(), "mask": causal_mask(),
        "w1_q": wq1, "w1_kv": k_tiles(a["L1_attn_w_kv"]), "w1_d": k_tiles(a["L1_attn_w_dense"]),
        "router0": a["L0_ffn_gate_w"].reshape(KT, P, E0).transpose(1, 0, 2),
        "router1": a["L1_ffn_gate_w"].T.reshape(KT, P, E1).transpose(1, 0, 2),
        "before": np.triu(np.ones((P, P), np.float32), 1),
        "experts0": ffn0, "experts1": ffn1,
    }


def kernel(**inputs):
    import concourse.bacc as bacc
    from concourse.bass_utils import run_bass_kernel_spmd

    nc = bacc.Bacc("TRN2", target_bir_lowering=False, num_devices=1)
    laid = lay_out({k: np.asarray(v) for k, v in inputs.items()})
    arrays, aps = {}, {}
    for name, a in laid.items():
        arrays[f"in_{name}"] = a = np.ascontiguousarray(a)
        aps[name] = nc.dram_tensor(f"in_{name}", a.shape, mybir.dt.from_np(a.dtype), kind="ExternalInput").ap()
    out = nc.dram_tensor("out_0_dram", (B, S, D), F32, kind="ExternalOutput").ap()
    adaln_program(nc, aps, out)
    r = run_bass_kernel_spmd(nc, [arrays], core_ids=[0])
    return r.results[0]["out_0_dram"]
```
